# Optimizing a Trainium2 kernel written in Bass

```python
import numpy as np
import jax
import jax.numpy as jnp

def _softmax(x, axis=-1):
    return jax.nn.softmax(x, axis=axis)

def _gelu(x):
    return jax.nn.gelu(x, approximate=True)

def _silu(x):
    return jax.nn.silu(x)

def _sigmoid(x):
    return jax.nn.sigmoid(x)

def _layernorm(x, axis=-1, eps=1e-05):
    m = jnp.mean(x, axis=axis, keepdims=True)
    v = jnp.var(x, axis=axis, keepdims=True)
    return (x - m) / jnp.sqrt(v + eps)

def _scatter_add(tgt, idx, src, axis=0):
    return tgt.at[idx].add(src)

def _segment_sum(src, seg, n):
    return jax.ops.segment_sum(src, seg, n)
kernel_name = 'mk_early_fusion_d2_tok_img256_r4_57a93a'

def setup_inputs(seed: int=0):
    np.random.seed(seed)
    _w = jnp.asarray

    def _rec_inputs():
        import jax
        import jax.numpy as jnp
        _rk = jax.random.key(seed)
        x = -0.000596345 + 1.00056 * jax.random.normal(jax.random.fold_in(_rk, 1), (32, 64, 64, 3), jnp.float32)
        txt = -0.093804 + 0.29155 * jax.random.normal(jax.random.fold_in(_rk, 2), (32, 32, 64), jnp.float32)
        return (x, txt)
    x, txt = _rec_inputs()

    def _L0_tok_setup():
        import jax, jax.numpy as jnp
        import numpy as np
        B, H, W = (16, 64, 64)
        WIDTH, LAYERS, M1, M2 = (32, 4, 12, 12)
        EPS = 1e-05

        def layer_norm(x, g, b):
            mu = jnp.mean(x, axis=-1, keepdims=True)
            var = jnp.mean((x - mu) ** 2, axis=-1, keepdims=True)
            return (x - mu) * jax.lax.rsqrt(var + EPS) * g + b

        def gelu(x):
            return jax.nn.gelu(x, approximate=False)

        def spectral_conv(x, w1, w2):
            b, c, h, w = x.shape
            x_ft = jnp.fft.rfft2(x)
            out_ft = jnp.zeros((b, w1.shape[1], h, w // 2 + 1), dtype=x_ft.dtype)
            out_ft = out_ft.at[:, :, :M1, :M2].set(jnp.einsum('bixy,ioxy->boxy', x_ft[:, :, :M1, :M2], w1))
            out_ft = out_ft.at[:, :, -M1:, :M2].set(jnp.einsum('bixy,ioxy->boxy', x_ft[:, :, -M1:, :M2], w2))
            return jnp.fft.irfft2(out_ft, s=(h, w))
        key = jax.random.key(seed)
        ks = jax.random.split(key, 16)
        scale = 1.0 / (WIDTH * WIDTH)
        d = {'x': jax.random.normal(ks[0], (B, H, W, 3), jnp.float32), 'fc0_w': jax.random.normal(ks[1], (3, WIDTH), jnp.float32) * 0.5, 'fc0_b': jnp.zeros((WIDTH,), jnp.float32), 'ln0_g': jnp.ones((WIDTH,), jnp.float32), 'ln0_b': jnp.zeros((WIDTH,), jnp.float32), 'w1r': jax.random.uniform(ks[2], (LAYERS, WIDTH, WIDTH, M1, M2), jnp.float32) * scale, 'w1i': jax.random.uniform(ks[3], (LAYERS, WIDTH, WIDTH, M1, M2), jnp.float32) * scale, 'w2r': jax.random.uniform(ks[4], (LAYERS, WIDTH, WIDTH, M1, M2), jnp.float32) * scale, 'w2i': jax.random.uniform(ks[5], (LAYERS, WIDTH, WIDTH, M1, M2), jnp.float32) * scale, 'conv_w': jax.random.normal(ks[6], (LAYERS, WIDTH, WIDTH), jnp.float32) * (1.0 / np.sqrt(WIDTH)), 'conv_b': jnp.zeros((LAYERS, WIDTH), jnp.float32), 'ln_g': jnp.ones((LAYERS, WIDTH), jnp.float32), 'ln_b': jnp.zeros((LAYERS, WIDTH), jnp.float32), 'fc1_w': jax.random.normal(ks[7], (WIDTH, 128), jnp.float32) * (1.0 / np.sqrt(WIDTH)), 'fc1_b': jnp.zeros((128,), jnp.float32), 'fc2_w': jax.random.normal(ks[8], (128, 64), jnp.float32) * (1.0 / np.sqrt(128)), 'fc2_b': jnp.zeros((64,), jnp.float32), 'fc3_w': jax.random.normal(ks[9], (64, 1), jnp.float32) * (1.0 / np.sqrt(64)), 'fc3_b': jnp.zeros((1,), jnp.float32)}
        return d
    _L0_tok_all = _L0_tok_setup()
    _L0_tok_in = {k: v for k, v in _L0_tok_all.items() if k in ('fc0_w', 'fc0_b', 'ln0_g', 'ln0_b', 'w1r', 'w1i', 'w2r', 'w2i', 'conv_w', 'conv_b', 'ln_g', 'ln_b', 'fc1_w', 'fc1_b', 'fc2_w', 'fc2_b', 'fc3_w', 'fc3_b')}
    del _L0_tok_all

    def _L0_attn_setup():
        import jax, jax.numpy as jnp
        import numpy as np
        key = jax.random.key(seed)
        k1, k2, k3 = jax.random.split(key, 3)
        b, n_t, n, n_h = (8, 256, 64, 8)
        s = jax.random.normal(k1, (b, n_t, n), dtype=jnp.float32)
        Q = jax.random.normal(k2, (n_h, n, n), dtype=jnp.float32) * 0.02
        E = jax.random.normal(k3, (n_h, n, n), dtype=jnp.float32) * 0.02
        return {'s': s, 'Q': Q, 'E': E}
    _L0_attn_all = _L0_attn_setup()
    _L0_attn_in = {k: v for k, v in _L0_attn_all.items() if k in ('Q', 'E')}
    del _L0_attn_all

    def _L0_ffn_setup():
        import jax, jax.numpy as jnp
        import numpy as np
        TOP_K = 2
        key = jax.random.key(seed)
        ks = jax.random.split(key, 4)
        B, L, D, H, E = (8, 1024, 64, 256, 8)
        s = 0.02
        return {'x': jax.random.normal(ks[0], (B, L, D), jnp.float32), 'Wg': jax.random.normal(ks[1], (D, E), jnp.float32) * s, 'bg': jnp.zeros((E,), jnp.float32), 'W1': jax.random.normal(ks[2], (E, D, H), jnp.float32) * s, 'b1': jnp.zeros((E, H), jnp.float32), 'W2': jax.random.normal(ks[3], (E, H, D), jnp.float32) * s, 'b2': jnp.zeros((E, D), jnp.float32)}
    _L0_ffn_all = _L0_ffn_setup()
    _L0_ffn_in = {k: v for k, v in _L0_ffn_all.items() if k in ('Wg', 'bg', 'W1', 'b1', 'W2', 'b2')}
    del _L0_ffn_all

    def _L1_attn_setup():
        import jax, jax.numpy as jnp
        import numpy as np
        B, T, F, H = (128, 256, 64, 128)

        def _lstm(xWb, U, reverse=False, return_sequences=False):
            Hn = U.shape[0]
            xs = jnp.swapaxes(xWb, 0, 1)
            h0 = jnp.zeros((xWb.shape[0], Hn), xWb.dtype)
            c0 = h0

            def step(carry, xw):
                h, c = carry
                z = xw + h @ U
                i, f, g, o = jnp.split(z, 4, axis=-1)
                i = jax.nn.sigmoid(i)
                f = jax.nn.sigmoid(f)
                g = jnp.tanh(g)
                o = jax.nn.sigmoid(o)
                c = f * c + i * g
                h = o * jnp.tanh(c)
                return ((h, c), h)
            (hT, _), hs = jax.lax.scan(step, (h0, c0), xs, reverse=reverse)
            if return_sequences:
                return jnp.swapaxes(hs, 0, 1)
            return hT
        key = jax.random.key(seed)
        ks = jax.random.split(key, 9)
        g = lambda k, shape: jax.random.normal(k, shape, jnp.float32) * 0.05
        return {'x': jax.random.uniform(ks[0], (B, T, F), jnp.float32), 'Wf': g(ks[1], (F, 4 * H)), 'Uf': g(ks[2], (H, 4 * H)), 'bf': jnp.zeros((4 * H,), jnp.float32), 'Wb': g(ks[3], (F, 4 * H)), 'Ub': g(ks[4], (H, 4 * H)), 'bb': jnp.zeros((4 * H,), jnp.float32), 'Wd': g(ks[5], (2 * H, 4 * H)), 'Ud': g(ks[6], (H, 4 * H)), 'bd': jnp.zeros((4 * H,), jnp.float32), 'Wo': g(ks[7], (H, F)), 'bo': jnp.zeros((F,), jnp.float32)}
    _L1_attn_all = _L1_attn_setup()
    _L1_attn_in = {k: v for k, v in _L1_attn_all.items() if k in ('Wf', 'Uf', 'bf', 'Wb', 'Ub', 'bb', 'Wd', 'Ud', 'bd', 'Wo', 'bo')}
    del _L1_attn_all

    def _L1_ffn_setup():
        import math
        import jax, jax.numpy as jnp
        import numpy as np
        CAPACITY_FACTOR = 1.25
        key = jax.random.key(seed)
        ks = jax.random.split(key, 5)
        B, L, D, F, E = (8, 2048, 64, 256, 8)
        h = jax.random.normal(ks[0], (B, L, D), dtype=jnp.float32)
        gate_w = jax.random.normal(ks[1], (D, E), dtype=jnp.float32) * 0.02
        gate_b = jnp.zeros((E,), dtype=jnp.float32)
        w1 = jax.random.normal(ks[2], (E, D, F), dtype=jnp.float32) * (1.0 / math.sqrt(D))
        b1 = jnp.zeros((E, F), dtype=jnp.float32)
        w2 = jax.random.normal(ks[3], (E, F, D), dtype=jnp.float32) * (1.0 / math.sqrt(F))
        b2 = jnp.zeros((E, D), dtype=jnp.float32)
        return {'h': h, 'gate_w': gate_w, 'gate_b': gate_b, 'w1': w1, 'b1': b1, 'w2': w2, 'b2': b2}
    _L1_ffn_all = _L1_ffn_setup()
    _L1_ffn_in = {k: v for k, v in _L1_ffn_all.items() if k in ('gate_w', 'gate_b', 'w1', 'b1', 'w2', 'b2')}
    del _L1_ffn_all
    return {'x': x, 'txt': txt, 'L0_tok_fc0_w': _L0_tok_in['fc0_w'], 'L0_tok_fc0_b': _L0_tok_in['fc0_b'], 'L0_tok_ln0_g': _L0_tok_in['ln0_g'], 'L0_tok_ln0_b': _L0_tok_in['ln0_b'], 'L0_tok_w1r': _L0_tok_in['w1r'], 'L0_tok_w1i': _L0_tok_in['w1i'], 'L0_tok_w2r': _L0_tok_in['w2r'], 'L0_tok_w2i': _L0_tok_in['w2i'], 'L0_tok_conv_w': _L0_tok_in['conv_w'], 'L0_tok_conv_b': _L0_tok_in['conv_b'], 'L0_tok_ln_g': _L0_tok_in['ln_g'], 'L0_tok_ln_b': _L0_tok_in['ln_b'], 'L0_tok_fc1_w': _L0_tok_in['fc1_w'], 'L0_tok_fc1_b': _L0_tok_in['fc1_b'], 'L0_tok_fc2_w': _L0_tok_in['fc2_w'], 'L0_tok_fc2_b': _L0_tok_in['fc2_b'], 'L0_tok_fc3_w': _L0_tok_in['fc3_w'], 'L0_tok_fc3_b': _L0_tok_in['fc3_b'], 'L0_attn_Q': _L0_attn_in['Q'], 'L0_attn_E': _L0_attn_in['E'], 'L0_ffn_Wg': _L0_ffn_in['Wg'], 'L0_ffn_bg': _L0_ffn_in['bg'], 'L0_ffn_W1': _L0_ffn_in['W1'], 'L0_ffn_b1': _L0_ffn_in['b1'], 'L0_ffn_W2': _L0_ffn_in['W2'], 'L0_ffn_b2': _L0_ffn_in['b2'], 'L1_attn_Wf': _L1_attn_in['Wf'], 'L1_attn_Uf': _L1_attn_in['Uf'], 'L1_attn_bf': _L1_attn_in['bf'], 'L1_attn_Wb': _L1_attn_in['Wb'], 'L1_attn_Ub': _L1_attn_in['Ub'], 'L1_attn_bb': _L1_attn_in['bb'], 'L1_attn_Wd': _L1_attn_in['Wd'], 'L1_attn_Ud': _L1_attn_in['Ud'], 'L1_attn_bd': _L1_attn_in['bd'], 'L1_attn_Wo': _L1_attn_in['Wo'], 'L1_attn_bo': _L1_attn_in['bo'], 'L1_ffn_gate_w': _L1_ffn_in['gate_w'], 'L1_ffn_gate_b': _L1_ffn_in['gate_b'], 'L1_ffn_w1': _L1_ffn_in['w1'], 'L1_ffn_b1': _L1_ffn_in['b1'], 'L1_ffn_w2': _L1_ffn_in['w2'], 'L1_ffn_b2': _L1_ffn_in['b2']}

def reference(x, txt, L0_tok_fc0_w, L0_tok_fc0_b, L0_tok_ln0_g, L0_tok_ln0_b, L0_tok_w1r, L0_tok_w1i, L0_tok_w2r, L0_tok_w2i, L0_tok_conv_w, L0_tok_conv_b, L0_tok_ln_g, L0_tok_ln_b, L0_tok_fc1_w, L0_tok_fc1_b, L0_tok_fc2_w, L0_tok_fc2_b, L0_tok_fc3_w, L0_tok_fc3_b, L0_attn_Q, L0_attn_E, L0_ffn_Wg, L0_ffn_bg, L0_ffn_W1, L0_ffn_b1, L0_ffn_W2, L0_ffn_b2, L1_attn_Wf, L1_attn_Uf, L1_attn_bf, L1_attn_Wb, L1_attn_Ub, L1_attn_bb, L1_attn_Wd, L1_attn_Ud, L1_attn_bd, L1_attn_Wo, L1_attn_bo, L1_ffn_gate_w, L1_ffn_gate_b, L1_ffn_w1, L1_ffn_b1, L1_ffn_w2, L1_ffn_b2):
    import jax
    import jax.numpy as jnp

    def _L0_tok_ref(x, fc0_w, fc0_b, ln0_g, ln0_b, w1r, w1i, w2r, w2i, conv_w, conv_b, ln_g, ln_b, fc1_w, fc1_b, fc2_w, fc2_b, fc3_w, fc3_b):
        import jax, jax.numpy as jnp
        import numpy as np
        B, H, W = (16, 64, 64)
        WIDTH, LAYERS, M1, M2 = (32, 4, 12, 12)
        EPS = 1e-05

        def layer_norm(x, g, b):
            mu = jnp.mean(x, axis=-1, keepdims=True)
            var = jnp.mean((x - mu) ** 2, axis=-1, keepdims=True)
            return (x - mu) * jax.lax.rsqrt(var + EPS) * g + b

        def gelu(x):
            return jax.nn.gelu(x, approximate=False)

        def spectral_conv(x, w1, w2):
            b, c, h, w = x.shape
            x_ft = jnp.fft.rfft2(x)
            out_ft = jnp.zeros((b, w1.shape[1], h, w // 2 + 1), dtype=x_ft.dtype)
            out_ft = out_ft.at[:, :, :M1, :M2].set(jnp.einsum('bixy,ioxy->boxy', x_ft[:, :, :M1, :M2], w1))
            out_ft = out_ft.at[:, :, -M1:, :M2].set(jnp.einsum('bixy,ioxy->boxy', x_ft[:, :, -M1:, :M2], w2))
            return jnp.fft.irfft2(out_ft, s=(h, w))
        h = layer_norm(x @ fc0_w + fc0_b, ln0_g, ln0_b)
        h = jnp.transpose(h, (0, 3, 1, 2))
        for i in range(LAYERS):
            w1 = w1r[i] + 1j * w1i[i]
            w2 = w2r[i] + 1j * w2i[i]
            x1 = spectral_conv(h, w1, w2)
            x2 = jnp.einsum('bchw,oc->bohw', h, conv_w[i]) + conv_b[i][None, :, None, None]
            h = x1 + x2
            h = jnp.transpose(h, (0, 2, 3, 1))
            h = layer_norm(h, ln_g[i], ln_b[i])
            if i < LAYERS - 1:
                h = gelu(h)
            h = jnp.transpose(h, (0, 3, 1, 2))
        h = jnp.transpose(h, (0, 2, 3, 1))
        h = gelu(h @ fc1_w + fc1_b)
        h = gelu(h @ fc2_w + fc2_b)
        h = h @ fc3_w + fc3_b
        return h[..., 0]

    def _L0_attn_ref(s, Q, E):
        import jax, jax.numpy as jnp
        import numpy as np
        n_t = s.shape[1]
        qs = jnp.einsum('bti,hij->bhtj', s, Q)
        Omega = jnp.einsum('bhtj,buj->bhtu', qs, s)
        mask = jnp.tril(jnp.ones((n_t, n_t), dtype=s.dtype))
        Omega = Omega * mask
        es = jnp.einsum('hij,buj->bhui', E, s)
        r = jnp.einsum('bhtu,bhui->bti', Omega, es)
        return r

    def _L0_ffn_ref(x, Wg, bg, W1, b1, W2, b2):
        import jax, jax.numpy as jnp
        import numpy as np
        TOP_K = 2
        B, L, D = x.shape
        E = W1.shape[0]
        xf = x.reshape(-1, D)
        gate_logits = xf @ Wg + bg
        top_w, top_i = jax.lax.top_k(gate_logits, TOP_K)
        top_w = jax.nn.softmax(top_w, axis=-1)
        w_dense = jnp.sum(jax.nn.one_hot(top_i, E, dtype=xf.dtype) * top_w[..., None], axis=1)
        out = jnp.zeros_like(xf)
        for e in range(E):
            h = jax.nn.gelu(xf @ W1[e] + b1[e], approximate=False)
            out = out + w_dense[:, e:e + 1] * (h @ W2[e] + b2[e])
        return out.reshape(B, L, D)

    def _L1_attn_ref(x, Wf, Uf, bf, Wb, Ub, bb, Wd, Ud, bd, Wo, bo):
        import jax, jax.numpy as jnp
        import numpy as np
        B, T, F, H = (128, 256, 64, 128)

        def _lstm(xWb, U, reverse=False, return_sequences=False):
            Hn = U.shape[0]
            xs = jnp.swapaxes(xWb, 0, 1)
            h0 = jnp.zeros((xWb.shape[0], Hn), xWb.dtype)
            c0 = h0

            def step(carry, xw):
                h, c = carry
                z = xw + h @ U
                i, f, g, o = jnp.split(z, 4, axis=-1)
                i = jax.nn.sigmoid(i)
                f = jax.nn.sigmoid(f)
                g = jnp.tanh(g)
                o = jax.nn.sigmoid(o)
                c = f * c + i * g
                h = o * jnp.tanh(c)
                return ((h, c), h)
            (hT, _), hs = jax.lax.scan(step, (h0, c0), xs, reverse=reverse)
            if return_sequences:
                return jnp.swapaxes(hs, 0, 1)
            return hT
        h_fwd = _lstm(x @ Wf + bf, Uf, reverse=False)
        h_bwd = _lstm(x @ Wb + bb, Ub, reverse=True)
        latent = jnp.concatenate([h_fwd, h_bwd], axis=-1)
        rep = jnp.broadcast_to(latent[:, None, :], (x.shape[0], x.shape[1], 2 * H))
        dec = _lstm(rep @ Wd + bd, Ud, return_sequences=True)
        return dec @ Wo + bo

    def _L1_ffn_ref(h, gate_w, gate_b, w1, b1, w2, b2):
        import math
        import jax, jax.numpy as jnp
        import numpy as np
        CAPACITY_FACTOR = 1.25
        B, L, D = h.shape
        E = gate_w.shape[1]
        T = B * L
        C = max(1, math.ceil(CAPACITY_FACTOR * T / E))
        x = h.reshape(T, D)
        logits = x @ gate_w + gate_b
        probs = jax.nn.softmax(logits, axis=-1)
        idx = jnp.argmax(probs, axis=-1)
        prb = jnp.take_along_axis(probs, idx[:, None], axis=1)[:, 0]
        one_hot = jax.nn.one_hot(idx, E, dtype=jnp.float32)
        pos = (jnp.cumsum(one_hot, axis=0) * one_hot).sum(-1).astype(jnp.int32) - 1
        kept = pos < C
        pos_safe = jnp.where(kept, pos, C)
        buf = jnp.zeros((E, C, D), dtype=h.dtype).at[idx, pos_safe].set(x, mode='drop')
        hmid = jax.nn.relu(jnp.einsum('ecd,edf->ecf', buf, w1) + b1[:, None, :])
        ybuf = jnp.einsum('ecf,efd->ecd', hmid, w2) + b2[:, None, :]
        pos_g = jnp.minimum(pos, C - 1)
        y_tok = ybuf[idx, pos_g] * (prb * kept)[:, None]
        y = y_tok.reshape(B, L, D)
        y = jnp.nan_to_num(y, nan=0.0, posinf=10000.0, neginf=-10000.0)
        return y
    h = _L0_tok_ref(x, L0_tok_fc0_w, L0_tok_fc0_b, L0_tok_ln0_g, L0_tok_ln0_b, L0_tok_w1r, L0_tok_w1i, L0_tok_w2r, L0_tok_w2i, L0_tok_conv_w, L0_tok_conv_b, L0_tok_ln_g, L0_tok_ln_b, L0_tok_fc1_w, L0_tok_fc1_b, L0_tok_fc2_w, L0_tok_fc2_b, L0_tok_fc3_w, L0_tok_fc3_b)
    h = jnp.concatenate([h, txt], axis=1)
    h = h + _L0_attn_ref(_layernorm(h, axis=-1), L0_attn_Q, L0_attn_E)
    h = h + _L0_ffn_ref(_layernorm(h, axis=-1), L0_ffn_Wg, L0_ffn_bg, L0_ffn_W1, L0_ffn_b1, L0_ffn_W2, L0_ffn_b2)
    h = h + _L1_attn_ref(_layernorm(h, axis=-1), L1_attn_Wf, L1_attn_Uf, L1_attn_bf, L1_attn_Wb, L1_attn_Ub, L1_attn_bb, L1_attn_Wd, L1_attn_Ud, L1_attn_bd, L1_attn_Wo, L1_attn_bo)
    h = h + _L1_ffn_ref(_layernorm(h, axis=-1), L1_ffn_gate_w, L1_ffn_gate_b, L1_ffn_w1, L1_ffn_b1, L1_ffn_w2, L1_ffn_b2)
    return h

_drawn_inputs = setup_inputs


def setup_inputs(seed=0):
    import zlib

    import numpy as np

    out = dict(_drawn_inputs(seed))
    spreads = {'L0_tok_fc0_b': (0.0, 0.1),
     'L0_tok_ln0_g': (1.0, 0.2),
     'L0_tok_ln0_b': (0.0, 0.1),
     'L0_tok_conv_b': (0.0, 0.1),
     'L0_tok_ln_g': (1.0, 0.2),
     'L0_tok_ln_b': (0.0, 0.1),
     'L0_tok_fc1_b': (0.0, 0.1),
     'L0_tok_fc2_b': (0.0, 0.1),
     'L0_ffn_bg': (0.0, 0.8),
     'L0_ffn_b1': (0.0, 0.8),
     'L0_ffn_b2': (0.0, 0.686),
     'L1_attn_bf': (0.0, 0.8),
     'L1_attn_bb': (0.0, 0.8),
     'L1_attn_bd': (0.0, 0.8),
     'L1_attn_bo': (0.0, 0.529),
     'L1_ffn_gate_b': (0.0, 0.573),
     'L1_ffn_b1': (0.0, 0.8),
     'L1_ffn_b2': (0.0, 0.8)}
    factors = {'L0_tok_w1r': 8.0,
     'L0_tok_w1i': 8.0,
     'L0_tok_w2r': 8.0,
     'L0_tok_w2i': 8.0,
     'L0_ffn_Wg': 5.296,
     'L0_ffn_W1': 8.0,
     'L0_ffn_W2': 8.0,
     'L1_attn_Wf': 8.0,
     'L1_attn_Uf': 8.0,
     'L1_attn_Wb': 8.0,
     'L1_attn_Ub': 8.0,
     'L1_attn_Wd': 8.0,
     'L1_attn_Ud': 8.0,
     'L1_attn_Wo': 7.149,
     'L1_ffn_gate_w': 3.478,
     'L1_ffn_w1': 3.821,
     'L1_ffn_w2': 3.169}
    for name, (base, spread) in spreads.items():
        noise = np.random.default_rng([zlib.crc32(name.encode()), seed]).standard_normal(out[name].shape)
        drawn = base * np.exp(spread * noise) if base else spread * noise
        out[name] = jnp.asarray(drawn.astype(out[name].dtype))
    for name, factor in factors.items():
        out[name] = (out[name] * factor).astype(out[name].dtype)
    return out
```

```python
from contextlib import ExitStack

import numpy as np
import concourse.bass as bass
from concourse import mybir

F32 = mybir.dt.float32
U32 = mybir.dt.uint32
ALU = mybir.AluOpType
ACT = mybir.ActivationFunctionType
AX = mybir.AxisListType

B, HH, WW, CI, CH, LAYERS, MX, MY = 32, 64, 64, 3, 32, 4, 12, 12
P = 128
BG = B // 4
CHUNKS = 8
CW = 512
KYR = 2 * MY
MODES = MX * MY
ROWS4 = 4
EPS = 1e-5
I1_GROUPS, G2_GROUPS = 3, 4
FRONT = I1_GROUPS + G2_GROUPS
AT_GROUPS, F2_GROUPS = 3, 2
BACK = AT_GROUPS + F2_GROUPS
HALF = MY // 2

NB, T, D = 32, 96, 64
TI = 64
NG, GB = 8, 4
GT = GB * T
HEADS = 8
NE, FF = 8, 256
HID, GATES = 128, 4
CAP = -(-5 * NB * T // (4 * NE))
NORMS = 4
QUARTERS = 4
FLT_MAX = float(np.finfo(np.float32).max)


def fno_constants():
    w = np.arange(WW)
    ang = lambda k, x: 2 * np.pi * k * x / 64.0
    f1 = np.zeros((2, WW, 64))
    for r in range(2):
        for ky in range(MY):
            f1[r, :, r * KYR + 2 * ky] = np.cos(ang(ky, w))
            f1[r, :, r * KYR + 2 * ky + 1] = -np.sin(ang(ky, w))
    f2 = np.zeros((2, HH, 64))
    i1 = np.zeros((64, 2, HH))
    h = np.arange(HH)
    for half in range(2):
        for kx in range(MX):
            f = kx + (HH - MX) * half
            c, s = np.cos(ang(f, h)), np.sin(ang(f, h))
            re, im = half * 24 + kx, half * 24 + 12 + kx
            f2[0, :, re], f2[1, :, re] = c, s
            f2[0, :, im], f2[1, :, im] = -s, c
            row = kx * 4 + half * 2
            i1[row, 0], i1[row, 1] = c / HH, s / HH
            i1[row + 1, 0], i1[row + 1, 1] = -s / HH, c / HH
    i2 = np.zeros((97, 2, 2, WW))
    for r4 in range(4):
        for ky in range(MY):
            a = (1.0 if ky == 0 else 2.0) / WW
            i2[r4 * KYR + 2 * ky, r4 // 2, r4 % 2] = a * np.cos(ang(ky, w))
            i2[r4 * KYR + 2 * ky + 1, r4 // 2, r4 % 2] = -a * np.sin(ang(ky, w))
    i2[96] = 1.0
    f = np.float32
    sign = np.ones((P, 1), f)
    sign[32:64] = sign[96:128] = -1
    return dict(k_f1=f1.reshape(P, 64).astype(f), k_f2=f2.reshape(P, 64).astype(f),
                k_i1=i1.reshape(64, P).astype(f), k_i2=i2.reshape(97, 256).astype(f),
                k_id=np.eye(P, dtype=f), k_sign=sign)


def build_fno(nc, sems, d, img):
    xs = nc.dram_tensor("x_planes", [B, CI, HH * WW], F32).ap()
    yd = nc.dram_tensor("y_modes", [ROWS4, CH, B, MODES], F32).ap()
    zd = nc.dram_tensor("z_modes", [BG, MX, ROWS4 * CH, 4 * MY], F32).ap()
    with ExitStack() as ctx:
        sb = lambda n, s: ctx.enter_context(nc.sbuf_tensor(n, s, F32))
        sem = lambda n: sems.enter_context(nc.semaphore(n))
        conv_all = sb("conv_all", [P, BG * CHUNKS, CW])
        w_raw = sb("w_raw", [P, CH * MODES])
        share = sb("share", [P, 3 * 1536])
        y_in = share[:, :].rearrange("p (b m) -> p b m", b=B)
        at = share[:, 0:1536]
        a_buf = share[:, 1536:3072]
        g_buf = share[:, 3072:4608]
        before = sb("before", [P, 2 * 2048])
        g2 = before[0:97, 0:2048].rearrange("p (a n) -> p a n", a=16)
        zpp = before[0:64, 2048:3584]
        xc = before[0:64, :].rearrange("p (r n) -> p r n", r=2)
        y_st = sb("y_st", [P, ROWS4 * MODES])
        zs = sb("zs", [P, 2, CW])
        work = sb("work", [P, 3 * CW + 16])
        t = work[:, 0:2 * CW].rearrange("p (r n) -> p r n", r=2)
        sq = work[:, 2 * CW:].rearrange("p (a c) -> p a c", c=CH + 1)
        w2 = work[:, 0:3 * CW].rearrange("p (r m n) -> p r m n", r=2, m=HALF)
        ht = sb("ht", [P, 2, CW])
        turned = sb("turned", [P, 2 * CW])
        hc = turned[:, :].rearrange("p (r n) -> p r n", r=2)
        z_row = turned[:, 0:2 * B * MY].rearrange("p (r n) -> p r n", r=2)
        w_mean = turned[:, 2 * B * MY:2 * B * MY + MODES]
        vs = sb("vs", [P, 2, 16])
        rstd = sb("rstd", [P, 2, 16])
        nhalf = sb("nhalf", [P, 16])
        f1, f2, ident = sb("f1", [P, 64]), sb("f2", [P, 64]), sb("ident", [P, P])
        i1, i2, sign = sb("i1", [64, P]), sb("i2", [97, 2 * P]), sb("sign", [P, 1])
        w0 = sb("w0", [64, P])
        w0m = sb("w0m", [64, 4])
        wc = sb("wc", [P, LAYERS, P])
        cwn = conv_all[:, 12, 0:CH]
        cwt = conv_all[0:CH, 13, 0:LAYERS * CH].rearrange("p (l c) -> p l c", l=LAYERS)
        cwm = conv_all[0:CH, 14, 0:LAYERS]
        cb = sb("cb", [97, LAYERS, CH])
        cbm = sb("cbm", [97, LAYERS])
        lng, lnb = sb("lng", [P, LAYERS + 1, CH]), sb("lnb", [P, LAYERS + 1, CH])
        fc1 = y_st[:, 0:512].rearrange("p (b f) -> p b f", b=4)
        fc2 = y_st[:, 512:576]
        fc3 = sb("fc3", [P, 64])
        fb = sb("fb", [P, 3])
        g1 = w_raw[:, 0:2 * CW].rearrange("p (r n) -> p r n", r=2)
        g2l = w_raw[:, 2 * CW:4 * CW].rearrange("p (r n) -> p r n", r=2)
        o1 = w_raw[:, 4 * CW:4 * CW + P]
        o2 = w_raw[:, 5 * CW:5 * CW + P]
        xraw = conv_all[:, 0:6, :].rearrange("p a n -> p (a n)")
        xpl = conv_all[:, 6:12, :].rearrange("p a n -> p (a n)")
        ps = [ctx.enter_context(nc.psum_tensor(f"ps{i}", [P, CW], F32)) for i in range(8)]
        pz, pt, pc, pf, pg, pb, px = ps[0:2], ps[2], ps[3], ps[4], ps[5], ps[6], ps[7]

        names = """consts_in filled zeroed params_in x_in x_split x_stored xc0_in xc1_in w0_ready wc_raw wc_t wc_ready prep
            z_done z_added squared var_sum nhalf_set rstd_ready t_scaled t_gained t_ready gelu_done tr_done hc_ready
            conv_done conv_kept f1_done a_written zpp_in fr_done fr_evac bk_done bk_evac y_stored xc_used
            w_in w_meaned w_scaled w_centred y_in w2_clear w2_dve w2_act mix_half zrow_ready z_stored0 z_stored1
            bias_set fc_clear fc_in fc1_done g1_ready fc2_done g2_ready fc3_done o1_ready o_tr o2_ready img_stored""".split()
        s = {n: sem(n) for n in names}
        xc_in, z_stored = [s["xc0_in"], s["xc1_in"]], [s["z_stored0"], s["z_stored1"]]
        N_CONST = 6
        block = ctx.enter_context(nc.Block())

        @block.sync
        def _(sp):
            for dst, name in ((f1, "k_f1"), (f2, "k_f2"), (ident, "k_id"), (i1, "k_i1"), (i2, "k_i2"), (sign, "k_sign")):
                sp.dma_start(dst[:, :], d[name]).then_inc(s["consts_in"], 16)
            xv = d["x"].rearrange("(i b) h w c -> (b h) i (w c)", b=2)
            sp.dma_start(xraw.rearrange("p (i n) -> p i n", i=16), xv).then_inc(s["x_in"], 16)
            sp.dma_start(cwn, d["L0_tok_conv_w"].rearrange("l o c -> (l o) c")).then_inc(s["params_in"], 16)
            sp.dma_start(cb[96:97, :, :], d["L0_tok_conv_b"].rearrange("(a l) c -> a l c", a=1)).then_inc(s["params_in"], 16)
            sp.wait_ge(s["zeroed"], 1)
            for b in range(4):
                sp.dma_start(w0[3 * b:3 * b + 3, 32 * b:32 * b + 32], d["L0_tok_fc0_w"]).then_inc(s["params_in"], 16)
                sp.dma_start(w0[32:33, 32 * b:32 * b + 32], d["L0_tok_fc0_b"].rearrange("(a c) -> a c", a=1)).then_inc(s["params_in"], 16)
            for b in range(2):
                with nc.allow_non_contiguous_dma(reason="a column of 64 weights"):
                    sp.dma_start(fc3[64 * b:64 * b + 64, b:b + 1], d["L0_tok_fc3_w"]).then_inc(s["params_in"], 16)
                    sp.dma_start(fb[64 * b:64 * b + 64, 1:2], d["L0_tok_fc2_b"].rearrange("(c a) -> c a", a=1)).then_inc(s["params_in"], 16)
            with nc.allow_non_contiguous_dma(reason="a column of biases"):
                sp.dma_start(fb[:, 0:1], d["L0_tok_fc1_b"].rearrange("(c a) -> c a", a=1)).then_inc(s["params_in"], 16)
                sp.dma_start(fb[:, 2:3], d["L0_tok_fc3_b"].rearrange("(a c) -> a c", a=1).broadcast_to([P, 1])).then_inc(s["params_in"], 16)
            for dst, first, rest in ((lng, "L0_tok_ln0_g", "L0_tok_ln_g"), (lnb, "L0_tok_ln0_b", "L0_tok_ln_b")):
                sp.dma_start(dst[:, 0, :], d[first].rearrange("(a c) -> a c", a=1).broadcast_to([P, CH])).then_inc(s["params_in"], 16)
                sp.dma_start(dst[:, 1:, :].rearrange("p l c -> p (l c)"),
                             d[rest].rearrange("(a l) c -> a (l c)", a=1).broadcast_to([P, LAYERS * CH])).then_inc(s["params_in"], 16)
            sp.wait_ge(s["x_split"], 1)
            for b in range(2):
                for c in range(CI):
                    sp.dma_start(xs.rearrange("(i b) c (h w) -> b c h i w", b=2, w=WW)[b, c],
                                 xpl.rearrange("p (i c w) -> p i c w", i=16, c=CI)[64 * b:64 * b + 64, :, c, :]).then_inc(s["x_stored"], 16)
            sp.wait_ge(s["x_stored"], 16 * 6)

            def load_xc(g, part):
                sp.wait_ge(s["xc_used"], 2 * g + part + 1)
                src = xs.rearrange("(g b) c n -> g (b c) n", b=4)[g]
                sp.dma_start(xc[0:12, part, :], src[:, part * 2048:part * 2048 + 2048]).then_inc(xc_in[part], 16)

            def load_w(l):
                for q, name in enumerate(("w1r", "w1i", "w2r", "w2i")):
                    src = d["L0_tok_" + name].rearrange("l i o x y -> l i (o x y)")
                    sp.dma_start(w_raw[32 * q:32 * q + 32, :], src[l]).then_inc(s["w_in"], 16)

            def store_y(n, g):
                sp.wait_ge(s["bk_evac"], BACK * n + BACK + 1)
                dst = yd.rearrange("q c (g b) m -> g b c q m", b=4)[g]
                for b in range(4):
                    sp.dma_start(dst[b], y_st[32 * b:32 * b + 32, :].rearrange("p (q m) -> p q m", q=ROWS4)).then_inc(s["y_stored"], 16)

            def load_zpp(u, g):
                sp.wait_ge(s["fr_done"], u * FRONT + 1)
                sp.dma_start(zpp[0:48], zd.rearrange("g x (q o) r -> g (x q) (o r)", q=ROWS4)[g]).then_inc(s["zpp_in"], 16)

            def mix(l):
                sp.wait_ge(s["y_stored"], 64 * BG * (l + 1) + 1)
                sp.dma_start(share[:, :], yd.rearrange("q c b m -> (q c) (b m)")).then_inc(s["y_in"], 16)
                with sp.Fori(0, MX // 2) as it:
                    for half in range(2):
                        row = l * MX + it * 2 + half
                        sp.wait_ge(s["zrow_ready"], row + 3)
                        sp.dma_start(zd.rearrange("g x p r -> x p g r")[it * 2 + half],
                                     z_row[:, half, :].rearrange("p (g r) -> p g r", g=BG)).then_inc(z_stored[half], 16)
                for half in range(2):
                    sp.wait_ge(z_stored[half], 96 * (l + 1) + 16)

            load_w(0)
            for part in range(2):
                load_xc(0, part)
            with sp.Fori(0, BG - 1) as g:
                for part in range(2):
                    load_xc(g + 1, part)
                store_y(g, g)
            store_y(BG - 1, BG - 1)
            with sp.Fori(0, LAYERS - 1) as l:
                mix(l)
                sp.wait_ge(s["mix_half"], 2 * MX * (l + 1) + 2)
                load_w(l + 1)
                load_zpp(l * BG, 0)
                with sp.Fori(0, BG - 1) as g:
                    load_zpp(l * BG + g + 1, g + 1)
                    store_y(BG + l * BG + g, g)
                store_y(2 * BG + l * BG - 1, BG - 1)
            mix(LAYERS - 1)
            last = (LAYERS - 1) * BG
            load_zpp(last, 0)
            sp.wait_ge(s["fc_clear"], 1)
            for b in range(4):
                sp.dma_start(fc1[32 * b:32 * b + 32, b, :], d["L0_tok_fc1_w"]).then_inc(s["fc_in"], 16)
            sp.dma_start(fc2, d["L0_tok_fc2_w"]).then_inc(s["fc_in"], 16)

            def store_img(g):
                sp.wait_ge(s["o2_ready"], g + 2)
                sp.dma_start(img.rearrange("(g b) (j r) w -> g (b j) (r w)", b=4, r=2)[g], o2).then_inc(s["img_stored"], 16)

            with sp.Fori(0, BG - 1) as g:
                load_zpp(last + g + 1, g + 1)
                store_img(g)
            store_img(BG - 1)
            sp.wait_ge(s["img_stored"], 16 * BG + 16)

        @block.gpsimd
        def _(pool):
            pool.memset(nhalf[:, :], -0.5).then_inc(s["nhalf_set"], 1)
            pool.wait_ge(s["nhalf_set"], 1)

            def unit(n):
                for k in range(CHUNKS):
                    q = n * CHUNKS + k
                    pool.wait_ge(s["var_sum"], q + 2)
                    pool.tensor_tensor(rstd[:, k % 2, :], vs[:, k % 2, :], nhalf[:, :], ALU.pow).then_inc(s["rstd_ready"], 1)
            with pool.Fori(0, LAYERS * BG) as n:
                unit(n)
            pool.wait_ge(s["y_stored"], 64 * LAYERS * BG + 1)
            pool.memset(fc1, 0.0).then_inc(s["fc_clear"], 1)
            with pool.Fori(LAYERS * BG, (LAYERS + 1) * BG) as n:
                unit(n)

        @block.tensor
        def _(pe):
            pe.wait_ge(s["consts_in"], 16 * N_CONST)
            pe.wait_ge(s["wc_raw"], 1)
            pe.transpose(pz[0][0:CH, 0:P], cwn, ident[:, :]).then_inc(s["wc_t"], 1)
            pe.wait_ge(s["prep"], 1)

            def z_first(g, q, k):
                part = k // 4
                if k % 4 == 0:
                    pe.wait_ge(xc_in[part], 16 * (g + 1))
                pe.wait_ge(s["z_added"], q + 1)
                for j in range(4):
                    mm = pe.matmul(pz[k % 2][:, P * j:P * j + P], xc[:, part, (k % 4) * CW + P * j:(k % 4) * CW + P * j + P],
                                   w0[:, :], start=True, stop=True)
                mm.then_inc(s["z_done"], 1)

            def z_mid(u, q, k):
                pe.wait_ge(s["fr_evac"], u * FRONT + I1_GROUPS + k // 2 + 2)
                pe.wait_ge(s["z_added"], q + 1)
                for j in range(4):
                    mm = pe.matmul(pz[k % 2][:, P * j:P * j + P], i2[:, (j % 2) * P:(j % 2) * P + P],
                                   g2[:, 2 * k + j // 2, :], start=True, stop=True)
                mm.then_inc(s["z_done"], 1)

            def front(u, l):
                pe.wait_ge(s["bias_set"], l)
                pe.wait_ge(s["zpp_in"], 16 * (u + 1))
                for i in range(FRONT):
                    pe.wait_ge(s["fr_evac"], u * FRONT + i + 1)
                    for j in range(4):
                        if i < I1_GROUPS:
                            ky = 4 * i + j
                            mm = pe.matmul(pg[:, P * j:P * j + P], zpp[:, ky::MY], i1[:, :], start=True, stop=True)
                        else:
                            hb = 4 * (i - I1_GROUPS) + j
                            mm = pe.transpose(pg[0:96, P * j:P * j + P], g_buf[:, 96 * hb:96 * hb + 96], ident[:, :])
                    mm.then_inc(s["fr_done"], 1)

            def turn(q, k):
                pe.wait_ge(s["gelu_done"], q + 1)
                pe.wait_ge(s["hc_ready"], q + 1)
                for j in range(4):
                    mm = pe.transpose(pt[:, P * j:P * j + P], ht[:, k % 2, P * j:P * j + P], ident[:, :])
                mm.then_inc(s["tr_done"], 1)

            def along_w(q, k):
                pe.wait_ge(s["a_written"], q + 1)
                for j in range(4):
                    mm = pe.matmul(pf[:, 64 * j:64 * j + 64], ht[:, k % 2, P * j:P * j + P], f1[:, :], start=True, stop=True)
                mm.then_inc(s["f1_done"], 1)

            def conv(q, k, l):
                pe.wait_ge(s["hc_ready"], q + 2)
                pe.wait_ge(s["conv_kept"], q + 1)
                for j in range(4):
                    mm = pe.matmul(pc[:, P * j:P * j + P], hc[:, k % 2, P * j:P * j + P], wc[:, l, :], start=True, stop=True)
                mm.then_inc(s["conv_done"], 1)

            def back(n):
                pe.wait_ge(s["a_written"], (n + 1) * CHUNKS + 1)
                for i in range(BACK):
                    pe.wait_ge(s["bk_evac"], n * BACK + i + 1)
                    if i < AT_GROUPS:
                        for j in range(4):
                            c = P * (4 * i + j)
                            mm = pe.transpose(pb[:, P * j:P * j + P], a_buf[:, c:c + P], ident[:, :])
                    else:
                        for j in range(6):
                            c = P * (6 * (i - AT_GROUPS) + j)
                            mm = pe.matmul(pb[:, 64 * j:64 * j + 64], at[:, c:c + P], f2[:, :], start=True, stop=True)
                    mm.then_inc(s["bk_done"], 1)

            def unit(n, g, l, first):
                q0 = n * CHUNKS
                if not first:
                    front(n - BG, l)
                for k in range(CHUNKS + 3):
                    if k < CHUNKS:
                        z_first(g, q0 + k, k) if first else z_mid(n - BG, q0 + k, k)
                    if 2 <= k < CHUNKS + 2:
                        turn(q0 + k - 2, k - 2)
                        along_w(q0 + k - 2, k - 2)
                    if k >= 3:
                        conv(q0 + k - 3, k - 3, l)
                back(n)

            def mix(l):
                with pe.Fori(0, MX // 2) as it:
                    for r in range(2):
                        row = l * MX + it * 2 + r
                        pe.wait_ge(s["zrow_ready"], row + 1)
                        for hf in range(2):
                            hq = l * 2 * MX + it * 4 + 2 * r + hf
                            pe.wait_ge(s["w2_dve"], hq + 1)
                            pe.wait_ge(s["w2_act"], hq + 1)
                            pe.wait_ge(s["y_in"], 16 * (l + 1))
                            for m in range(HALF):
                                mode = it * 2 * MY + r * MY + hf * HALF + m
                                c = (hf * HALF + m) * B
                                mm = pe.matmul(pz[r][:, c:c + B], w2[:, hf, m, :], y_in[:, :, mode], start=True, stop=True)
                            mm.then_inc(s["mix_half"], 1)

            with pe.Fori(0, BG) as g:
                unit(g, g, 0, True)
            with pe.Fori(0, LAYERS - 1) as l:
                mix(l)
                with pe.Fori(0, BG) as g:
                    unit(BG + l * BG + g, g, l + 1, False)
            mix(LAYERS - 1)
            pe.wait_ge(s["fc_in"], 16 * 5)

            def last_chunk(q, k, c):
                turn(q, k)
                pe.wait_ge(s["hc_ready"], q + 2)
                for b in range(4):
                    pe.wait_ge(s["g1_ready"], 4 * c + b + 1)
                    bank = (pc, pf)[b % 2]
                    pe.matmul(bank[:, :], fc1[:, b, :], hc[:, k % 2, :], start=True, stop=True).then_inc(s["fc1_done"], 1)
                    if b >= 1:
                        second(c, b - 1)
                second(c, 3)

            def second(c, b):
                pe.wait_ge(s["g1_ready"], 4 * c + b + 3)
                if b % 2 == 0:
                    pe.wait_ge(s["g2_ready"], 2 * c + b // 2 + 1)
                mm = pe.matmul(px[64 * (b % 2):64 * (b % 2) + 64, :], fc2, g1[:, b % 2, :], start=True, stop=True)
                mm.then_inc(s["fc2_done"], 1)

            def third(c):
                pe.wait_ge(s["o1_ready"], c + 1)
                for pair in range(2):
                    pe.wait_ge(s["g2_ready"], 2 * c + pair + 2)
                    for j in range(4):
                        o = 256 * pair + 64 * j
                        mm = pe.matmul(pb[:, o:o + 64], g2l[:, pair, P * j:P * j + P], fc3[:, :], start=True, stop=True)
                mm.then_inc(s["fc3_done"], 1)

            with pe.Fori(0, BG) as g:
                n = LAYERS * BG + g
                q0 = n * CHUNKS
                front(n - BG, LAYERS)
                for k in range(CHUNKS + 3):
                    if k < CHUNKS:
                        z_mid(n - BG, q0 + k, k)
                    if k >= 3:
                        third(g * CHUNKS + k - 3)
                    if 2 <= k < CHUNKS + 2:
                        last_chunk(q0 + k - 2, k - 2, g * CHUNKS + k - 2)
                pe.wait_ge(s["o1_ready"], (g + 1) * CHUNKS + 1)
                pe.transpose(pg[:, 0:P], o1, ident[:, :]).then_inc(s["o_tr"], 1)
                pe.wait_ge(s["o2_ready"], g + 2)

        @block.scalar
        def _(act):
            act.sem_inc(s["hc_ready"], 1)
            act.sem_inc(s["conv_kept"], 1)
            act.sem_inc(s["fr_evac"], 1)

            def square(q, k):
                act.wait_ge(s["z_added"], q + 3)
                act.wait_ge(s["var_sum"], q + 1)
                act.activation(sq[:, :, 0:CH], zs[:, k % 2, :].rearrange("p (a c) -> p a c", c=CH), ACT.Square, scale=CH ** -0.5).then_inc(s["squared"], 1)

            def gelu(q, k, first):
                act.wait_ge(s["t_ready"], q + 1)
                act.activation(ht[:, k % 2, :], t[:, k % 2, :], ACT.Copy if first else ACT.Gelu).then_inc(s["gelu_done"], 1)

            def hc_evac(q, k):
                act.wait_ge(s["tr_done"], q + 1)
                act.copy(hc[:, k % 2, :], pt[:, :]).then_inc(s["hc_ready"], 1)

            def conv_evac(q, k, g):
                act.wait_ge(s["conv_done"], q + 1)
                act.copy(conv_all[:, g * CHUNKS + k, :], pc[:, :]).then_inc(s["conv_kept"], 1)

            def front(u):
                for i in range(FRONT):
                    act.wait_ge(s["fr_done"], u * FRONT + i + 6)
                    if i < I1_GROUPS:
                        dst = g_buf.rearrange("p (h r) -> p r h", r=KYR)[:, 8 * i:8 * i + 8, :]
                        act.copy(dst, pg[:, :].rearrange("p (r h) -> p r h", r=8)).then_inc(s["fr_evac"], 1)
                    else:
                        o = 4 * (i - I1_GROUPS)
                        dst = g2[0:96, o:o + 4, :].rearrange("p j (b c) -> p j c b", b=4)
                        act.copy(dst, pg[0:96, :].rearrange("p (j c b) -> p j c b", j=4, b=4)).then_inc(s["fr_evac"], 1)

            def unit(n, g, first):
                q0 = n * CHUNKS
                if not first:
                    front(n - BG)
                for k in range(CHUNKS + 3):
                    if k < CHUNKS:
                        square(q0 + k, k)
                    if 2 <= k < CHUNKS + 2:
                        hc_evac(q0 + k - 2, k - 2)
                    if 1 <= k < CHUNKS + 1:
                        gelu(q0 + k - 1, k - 1, first)
                    if k >= 3:
                        conv_evac(q0 + k - 3, k - 3, g)

            def mix(l):
                act.wait_ge(s["w_centred"], l + 1)
                act.wait_ge(s["w2_clear"], l + 1)
                wv = w_raw[:, :].rearrange("p (o m) -> p m o", m=MODES)
                with act.Fori(0, MX) as row:
                    for hf in range(2):
                        hq = l * 2 * MX + row * 2 + hf
                        act.wait_ge(s["mix_half"], hq + 1)
                        for half in range(2):
                            for im in range(2):
                                dst = 64 * half + 32 * im
                                src = 64 * half + 32 * (1 - im)
                                cp = act.copy(w2[dst:dst + 32, hf, :, 64 * half + 32:64 * half + 64],
                                              wv[src:src + 32, bass.ds(row * MY + hf * HALF, HALF), :])
                        cp.then_inc(s["w2_act"], 1)

            with act.Fori(0, BG) as g:
                unit(g, g, True)
            with act.Fori(0, LAYERS - 1) as l:
                mix(l)
                with act.Fori(0, BG) as g:
                    unit(BG + l * BG + g, g, False)
            mix(LAYERS - 1)
            act.sem_inc(s["g1_ready"], 2)
            act.sem_inc(s["g2_ready"], 1)

            def dense(c):
                for b in range(4):
                    act.wait_ge(s["fc1_done"], 4 * c + b + 1)
                    act.wait_ge(s["fc2_done"], 4 * c + b + 1)
                    act.activation(g1[:, b % 2, :], (pc, pf)[b % 2][:, :], ACT.Gelu, bias=fb[:, 0:1]).then_inc(s["g1_ready"], 1)
                    if b % 2 == 0 and b:
                        pair(c, 0)
                pair(c, 1)

            def pair(c, i):
                act.wait_ge(s["fc2_done"], 4 * c + 2 * i + 4)
                act.wait_ge(s["fc3_done"], c + 1)
                act.activation(g2l[:, i, :], px[:, :], ACT.Gelu, bias=fb[:, 1:2]).then_inc(s["g2_ready"], 1)

            with act.Fori(0, BG) as g:
                n = LAYERS * BG + g
                q0 = n * CHUNKS
                front(n - BG)
                for k in range(CHUNKS + 2):
                    if k < CHUNKS:
                        square(q0 + k, k)
                    if k >= 2:
                        act.wait_ge(s["tr_done"], q0 + k - 2 + 1)
                        act.copy(hc[:, k % 2, :], pt[:, :]).then_inc(s["hc_ready"], 1)
                        dense(g * CHUNKS + k - 2)

        @block.vector
        def _(dve):
            dve.sem_inc(s["z_added"], 2)
            dve.sem_inc(s["var_sum"], 1)
            dve.sem_inc(s["a_written"], 1)
            dve.sem_inc(s["bk_evac"], 1)
            dve.sem_inc(s["y_stored"], 1)
            dve.sem_inc(s["z_stored0"], 16)
            dve.sem_inc(s["z_stored1"], 16)
            dve.sem_inc(s["xc_used"], 2)
            dve.sem_inc(s["mix_half"], 2)
            dve.sem_inc(s["fr_done"], 5)
            dve.sem_inc(s["fc2_done"], 2)
            dve.sem_inc(s["fc3_done"], 1)
            dve.sem_inc(s["img_stored"], 16)
            dve.sem_inc(s["zrow_ready"], 2)
            for buf in (w0, fc3, wc, before):
                fill = dve.memset(buf[:], 0.0)
            fill.then_inc(s["filled"], 1)
            dve.wait_ge(s["filled"], 1)
            dve.memset(xc[32:33], 1.0)
            dve.memset(sq[:, :, CH:], EPS)
            dve.memset(fb[:], 0.0).then_inc(s["zeroed"], 1)
            dve.wait_ge(s["x_in"], 16)
            dve.tensor_copy(xpl.rearrange("p (i c w) -> p i c w", i=16, c=CI),
                            xraw.rearrange("p (i w c) -> p i c w", i=16, c=CI)).then_inc(s["x_split"], 1)
            n_prep = [0]

            def step(ins):
                n_prep[0] += 1
                ins.then_inc(s["w0_ready"], 1)
                dve.wait_ge(s["w0_ready"], n_prep[0])

            dve.wait_ge(s["params_in"], 16 * 20)
            dve.sem_inc(s["wc_raw"], 1)

            def centre(x, mean, c):
                step(dve.reduce_sum(mean, x, AX.X))
                step(dve.tensor_scalar(mean, mean, 1.0 / c, None, ALU.mult))
                step(dve.tensor_tensor(x, x, mean.unsqueeze(2).broadcast_to(x.shape), ALU.subtract))

            centre(w0[:, :].rearrange("p (b c) -> p b c", b=4), w0m[:, :], CH)
            centre(cb[96:97, :, :], cbm[96:97, :], CH)
            dve.wait_ge(s["wc_t"], 1)
            step(dve.tensor_copy(cwt[:, :, :], pz[0][0:CH, 0:P].rearrange("c (l o) -> c l o", l=LAYERS)))
            centre(cwt[:, :, :], cwm, CH)
            for b in range(4):
                step(dve.tensor_copy(wc[32 * b:32 * b + 32, :, 32 * b:32 * b + 32], cwt[:, :, :]))
            dve.wait_ge(s["consts_in"], 16 * N_CONST)
            dve.sem_inc(s["prep"], 1)

            def z_add(q, k, g, first):
                dve.wait_ge(s["z_done"], q + 1)
                if first:
                    add = dve.tensor_copy(zs[:, k % 2, :], pz[k % 2][:, :])
                else:
                    dve.wait_ge(s["conv_kept"], q - BG * CHUNKS + 2)
                    add = dve.tensor_tensor(zs[:, k % 2, :], pz[k % 2][:, :], conv_all[:, g * CHUNKS + k, :], ALU.add)
                add.then_inc(s["z_added"], 1)

            def var_sum(q, k):
                dve.wait_ge(s["squared"], q + 1)
                dve.reduce_sum(vs[:, k % 2, :], sq, AX.X).then_inc(s["var_sum"], 1)

            def scale(q, k, l, dst):
                groups = lambda x: x[:, k % 2, :].rearrange("p (a c) -> p a c", c=CH)
                dve.wait_ge(s["rstd_ready"], q + 1)
                dve.tensor_tensor(groups(t), groups(zs), rstd[:, k % 2, :].unsqueeze(2).broadcast_to([P, 16, CH]), ALU.mult).then_inc(s["t_scaled"], 1)
                dve.wait_ge(s["t_scaled"], q + 1)
                dve.tensor_tensor(groups(t), groups(t), lng[:, l, :].unsqueeze(1).broadcast_to([P, 16, CH]), ALU.mult).then_inc(s["t_gained"], 1)
                dve.wait_ge(s["t_gained"], q + 1)
                if dst is ht:
                    dve.wait_ge(s["tr_done"], q - 1)
                add = dve.tensor_tensor(groups(dst), groups(t), lnb[:, l, :].unsqueeze(1).broadcast_to([P, 16, CH]), ALU.add)
                add.then_inc(s["t_ready"], 1) if dst is t else add.then_inc(s["gelu_done"], 1)

            def a_evac(q, k):
                dve.wait_ge(s["f1_done"], q + 1)
                src = pf[:, 0:256].rearrange("p (j x) -> p j x", j=4)[:, :, 0:48].rearrange("p j (h r) -> p r j h", h=2)
                dst = a_buf.rearrange("p (r j h) -> p r j h", r=KYR, h=2)[:, :, 4 * k:4 * k + 4, :]
                dve.tensor_copy(dst, src).then_inc(s["a_written"], 1)

            def back(n):
                for i in range(BACK):
                    dve.wait_ge(s["bk_done"], n * BACK + i + 1)
                    if i < AT_GROUPS:
                        cp = dve.tensor_copy(at[:, CW * i:CW * i + CW], pb[:, :])
                    else:
                        if i == AT_GROUPS:
                            dve.wait_ge(s["y_stored"], 64 * n + 1)
                        src = pb[:, 0:384].rearrange("p (y x) -> p x y", x=64)[:, 0:48, :]
                        dst = y_st[:, :].rearrange("p (x y) -> p x y", y=MY)[:, :, 6 * (i - AT_GROUPS):6 * (i - AT_GROUPS) + 6]
                        cp = dve.tensor_copy(dst, src)
                    cp.then_inc(s["bk_evac"], 1)

            def unit(n, g, l, first):
                q0 = n * CHUNKS
                for k in range(CHUNKS + 2):
                    if k < CHUNKS:
                        z_add(q0 + k, k, g, first)
                    if first and k in (3, 7):
                        dve.sem_inc(s["xc_used"], 1)
                    if 1 <= k < CHUNKS + 1:
                        scale(q0 + k - 1, k - 1, l, t)
                    if k < CHUNKS:
                        var_sum(q0 + k, k)
                    if k >= 2:
                        a_evac(q0 + k - 2, k - 2)
                back(n)

            def mix(l):
                dve.wait_ge(s["w_in"], 64 * (l + 1))
                ov = w_raw[:, :].rearrange("p (o m) -> p m o", m=MODES)
                dve.reduce_sum(w_mean, ov, AX.X).then_inc(s["w_meaned"], 1)
                dve.wait_ge(s["w_meaned"], l + 1)
                dve.tensor_scalar(w_mean, w_mean, 1.0 / CH, None, ALU.mult).then_inc(s["w_scaled"], 1)
                dve.wait_ge(s["w_scaled"], l + 1)
                om = w_raw[:, :].rearrange("p (o m) -> p o m", m=MODES)
                dve.tensor_tensor(om, om, w_mean.unsqueeze(1).broadcast_to([P, CH, MODES]), ALU.subtract).then_inc(s["w_centred"], 1)
                dve.wait_ge(s["w_centred"], l + 1)
                dve.memset(w2, 0.0).then_inc(s["w2_clear"], 1)
                dve.wait_ge(s["w2_clear"], l + 1)
                bias = g2[96:97, :, :].rearrange("p a (b c) -> p (a b) c", c=CH)
                dve.tensor_copy(bias, cb[96:97, l, :].unsqueeze(1).broadcast_to([1, 64, CH])).then_inc(s["bias_set"], 1)
                with dve.Fori(0, MX // 2) as it:
                    for r in range(2):
                        row = l * MX + it * 2 + r
                        for hf in range(2):
                            hq = l * 2 * MX + it * 4 + 2 * r + hf
                            dve.wait_ge(s["mix_half"], hq + 1)
                            for half in range(2):
                                p0 = 64 * half
                                cp = dve.tensor_scalar(w2[p0:p0 + 64, hf, :, 64 * half:64 * half + 32],
                                                       ov[p0:p0 + 64, bass.ds(it * 2 * MY + r * MY + hf * HALF, HALF), :],
                                                       sign[p0:p0 + 64, :], None, ALU.mult)
                            cp.then_inc(s["w2_dve"], 1)
                        dve.wait_ge(s["mix_half"], 2 * row + 4)
                        dve.wait_ge(z_stored[r], 16 * (l * (MX // 2) + it) + 16)
                        dve.tensor_copy(z_row[:, r, :].rearrange("p (b y) -> p y b", y=MY),
                                        pz[r][:, 0:B * MY].rearrange("p (y b) -> p y b", y=MY)).then_inc(s["zrow_ready"], 1)
                dve.memset(sq[:, :, CH:], EPS)

            with dve.Fori(0, BG) as g:
                unit(g, g, 0, True)
            with dve.Fori(0, LAYERS - 1) as l:
                mix(l)
                with dve.Fori(0, BG) as g:
                    unit(BG + l * BG + g, g, l + 1, False)
            mix(LAYERS - 1)
            dve.sem_inc(s["o1_ready"], 1)
            dve.sem_inc(s["o2_ready"], 1)

            def o1_evac(c, k):
                dve.wait_ge(s["fc3_done"], c + 2)
                src = pb[:, :].rearrange("p (a j x) -> p a j x", a=2, j=4)[:, :, :, 0:2].rearrange("p a j b -> p a b j")
                dst = o1.rearrange("p (a b j) -> p a b j", a=2, b=2)[:, :, :, 4 * k:4 * k + 4]
                dve.tensor_scalar(dst, src, fb[:, 2:3], None, ALU.add).then_inc(s["o1_ready"], 1)

            with dve.Fori(0, BG) as g:
                q0 = (LAYERS * BG + g) * CHUNKS
                for k in range(CHUNKS + 3):
                    if k < CHUNKS:
                        z_add(q0 + k, k, g, False)
                    if 1 <= k < CHUNKS + 1:
                        scale(q0 + k - 1, k - 1, LAYERS, ht)
                    if k < CHUNKS:
                        var_sum(q0 + k, k)
                    if k >= 3:
                        o1_evac(g * CHUNKS + k - 3, k - 3)
                dve.wait_ge(s["o_tr"], g + 1)
                dve.wait_ge(s["img_stored"], 16 * g + 16)
                dve.tensor_copy(o2, pg[:, 0:P]).then_inc(s["o2_ready"], 1)


def tail_constants():
    u = np.arange(T)
    f = np.float32
    return dict(k_tri=(u[:, None] <= u[None, :]).astype(f),
                k_below=np.broadcast_to((np.arange(NE)[None, :] < np.arange(NE)[:, None]).reshape(1, 64), (T, 64)).astype(f).copy())


def build_tail(nc, sems, d, img, out):
    with ExitStack() as ctx:
        sb = lambda n, s, t=F32: ctx.enter_context(nc.sbuf_tensor(n, s, t))
        x = sb("x_tok", [T, NB, D])
        xc_ = sb("x_centred", [T, NB, D])
        sq_ = sb("x_squares", [T, NB, D])
        mean, var, rs, nh = sb("mean_t", [T, NB]), sb("var_t", [T, NB]), sb("rstd_t", [T, NB]), sb("nhalf_t", [T, NB])
        norm = sb("norm_t", [T, 2, GB, D])
        xg = sb("xg", [D + 1, 2, GT])
        xt = sb("xt", [D + 1, NG, GT])
        ident = sb("ident_t", [P, P])
        tri, ones = sb("tri", [T, T]), sb("ones_t", [T, T])
        below = sb("below", [T, NE, NE])
        big = sb("big", [P, 2 * T * P])
        qst = big[0:D, 0:HEADS * GT].rearrange("p (h n) -> p h n", h=HEADS)
        es = big[0:T, 3072:4096].rearrange("p (r n) -> p r n", r=2)
        om = big[0:T, 4096:5632].rearrange("p (r h n) -> p r h n", r=2, h=HEADS)
        wq, we, wet = sb("wq", [D, HEADS, D]), sb("we", [P, 4, D]), sb("wet", [D, HEADS * D])
        hid = big[:, 0:2 * 16 * GT].rearrange("p (r c n) -> p r c n", r=2, c=16)
        w1 = [sb(f"w1_{i}", [D + 1, NE, FF]) for i in range(2)]
        w2 = [sb(f"w2_{i}", [P, 2 * NE, D]) for i in range(2)]
        b2 = [sb(f"b2_{i}", [T, NE, D]) for i in range(2)]
        wg = [sb(f"wg_{i}", [D + 1, NE]) for i in range(2)]
        logit = sb("logit", [T, NB, NE])
        gate = sb("gate", [T, NB, NE])
        picked = sb("picked", [T, NB, NE])
        place = sb("place", [T, 2, NB, NE])
        top, total = sb("top", [T, NB]), sb("total", [T, NB])
        above = sq_[:, :, :].rearrange("p b (e f) -> p b e f", e=NE)
        equal = xc_[:, :, :].rearrange("p b (e f) -> p b e f", e=NE)
        mixed = big[0:T, 15392:16416].rearrange("p (r n) -> p r n", r=2)
        weighed = big[0:T, 16416:17440].rearrange("p (r n) -> p r n", r=2)
        y = sb("y_t", [T, 2, GB * D])
        y_all = sq_
        odd = sb("odd", [T, 2, 8 * D], U32)
        fills = big[0:T, 17440:17440 + 3 * 8 * D].rearrange("p (m n) -> p m n", m=3)
        xw = big[:, :].rearrange("p (r t n) -> p r t n", r=2, t=T)
        lw = [sb(f"lw_{i}", [D + 1, GATES * HID]) for i in range(2)]
        lu = [sb(f"lu_{i}", [HID, GATES * HID]) for i in range(3)]
        lwd = sb("lwd", [HID, 2, GATES * HID])
        lbd = sb("lbd", [1, GATES * HID])
        hs = sb("hs", [HID, 2, 2, NB])
        cs = sb("cs", [HID, 3, NB])
        sig = sb("sig", [HID, 3, 3 * NB])
        tg, tc_, fc_, ig = sb("tg", [HID, 3, NB]), sb("tc", [HID, 3, NB]), sb("fc", [HID, 3, NB]), sb("ig", [HID, 3, NB])
        zc = sb("zc", [HID, GATES * NB])
        hd = big[:, 12288:12288 + (T + 1) * NB].rearrange("p (t n) -> p t n", t=T + 1)
        wo, bo = sb("wo", [HID, D]), sb("bo", [T, D])
        ps = [ctx.enter_context(nc.psum_tensor(f"pt{i}", [P, 512], F32)) for i in range(8)]
        names = """loaded setup_done sums meaned centred squared varied powed rstd normed turned turned_out
            we_in we_turned wet_done q_done q_out es_done es_out om_done om_out r_done r_added
            logit_done logit_out up_done hid_done down_done added weighted summed y_added gate_step exp_in exp_done tri_in tri_done
            xw_done xw_act xw_dve z0 z1 z2 s0 s1 s2 c0 c1 c2 tc0 tc1 tc2 h0 h1 h2 fg0 fg1 fg2 ig0 ig1 ig2
            zc_done zc_out dec_done dec_out out_sent xt_kept """.split()
        s = {n: sems.enter_context(nc.semaphore("t_" + n)) for n in names}
        N_LOADS = 7 + 12 + 4 + 3 + 4
        GATE_AT = (0, 1, 3, 2)
        block = ctx.enter_context(nc.Block())

        def row(ap):
            return ap.rearrange("(a n) -> a n", a=1)

        @block.sync
        def _(sp):
            def ld(dst, src):
                sp.dma_start(dst, src).then_inc(s["loaded"], 16)
            ld(x[0:TI, :, :], img.rearrange("b t w -> t b w"))
            ld(x[TI:T, :, :], d["txt"].rearrange("b t w -> t b w"))
            ld(ident[:, :], d["k_id"])
            ld(tri[:, :], d["k_tri"])
            ld(below[:, :, :].rearrange("p a b -> p (a b)"), d["k_below"])
            ld(wq[:, :, :], d["L0_attn_Q"].rearrange("h i j -> i h j"))
            ld(we[:, :, :], d["L0_attn_E"].rearrange("(a h) i j -> (h i) a j", h=2))
            for i, (g, bg, a, b, c, e) in enumerate((("L0_ffn_Wg", "L0_ffn_bg", "L0_ffn_W1", "L0_ffn_b1", "L0_ffn_W2", "L0_ffn_b2"),
                                                     ("L1_ffn_gate_w", "L1_ffn_gate_b", "L1_ffn_w1", "L1_ffn_b1", "L1_ffn_w2", "L1_ffn_b2"))):
                ld(wg[i][0:D, :], d[g])
                ld(wg[i][D:D + 1, :], row(d[bg]))
                ld(w1[i][0:D, :, :], d[a].rearrange("e d f -> d e f"))
                ld(w1[i][D:D + 1, :, :], d[b].rearrange("(a e) f -> a e f", a=1))
                ld(w2[i][:, :, :], d[c].rearrange("e (k f) d -> f (e k) d", f=P))
                ld(b2[i][:, :, :].rearrange("p e d -> p (e d)"), d[e].rearrange("(a e) d -> a (e d)", a=1).broadcast_to([T, NE * D]))
            for i, (w, b) in enumerate((("Wf", "bf"), ("Wb", "bb"))):
                ld(lw[i][0:D, :], d["L1_attn_" + w])
                ld(lw[i][D:D + 1, :], row(d["L1_attn_" + b]))
            for i, u in enumerate(("Uf", "Ub", "Ud")):
                ld(lu[i][:, :], d["L1_attn_" + u])
            ld(lwd[:, :, :], d["L1_attn_Wd"].rearrange("(k p) n -> p k n", p=HID))
            ld(lbd[:, :], row(d["L1_attn_bd"]))
            ld(wo[:, :], d["L1_attn_Wo"])
            ld(bo[:, :], row(d["L1_attn_bo"]).broadcast_to([T, D]))
            for v in range(QUARTERS):
                sp.wait_ge(s["y_added"], NG + v + 1)
                sp.dma_start(out.rearrange("b t w -> t b w")[:, 8 * v:8 * v + 8], x[:, 8 * v:8 * v + 8, :]).then_inc(s["out_sent"], 16)
            sp.wait_ge(s["out_sent"], 16 * QUARTERS)

        @block.gpsimd
        def _(pool):
            pool.memset(nh[:, :], -0.5).then_inc(s["powed"], 1)
            for n in range(NORMS):
                pool.wait_ge(s["varied"], n + 1)
                pool.tensor_scalar(var[:, :], var[:, :], 1.0 / D, EPS, ALU.mult, ALU.add).then_inc(s["powed"], 1)
                pool.wait_ge(s["powed"], n + 2)
                pool.tensor_tensor(rs[:, :], var[:, :], nh[:, :], ALU.pow).then_inc(s["rstd"], 1)

        @block.tensor
        def _(pe):
            pe.wait_ge(s["loaded"], 16 * N_LOADS)
            pe.wait_ge(s["setup_done"], 1)
            for a in range(4):
                mm = pe.transpose(ps[0][0:D, P * a:P * a + P], we[:, a, :], ident[:, :])
            mm.then_inc(s["we_turned"], 1)
            pe.wait_ge(s["wet_done"], 1)

            def turn(n, par, g):
                k = n * NG + g
                pe.wait_ge(s["normed"], k + 1)
                pe.wait_ge(s["turned_out"], k + 1)
                for b2_ in range(GB // 2):
                    mm = pe.transpose(ps[0][:, T * b2_:T * b2_ + T], norm[:, par, 2 * b2_:2 * b2_ + 2, :], ident[0:T, 0:T])
                mm.then_inc(s["turned"], 1)
                pe.wait_ge(s["turned_out"], k + 2)

            def attend(b, k4):
                pe.wait_ge(s["es_out"], k4 + 1)
                sT = xg[0:D, par, T * b:T * b + T]
                pe.matmul(ps[3][0:T, :], sT, wet[:, :], start=True, stop=True).then_inc(s["es_done"], 1)
                pe.wait_ge(s["om_out"], k4 + 1)
                for hh in range(2):
                    mm = pe.matmul(ps[4 + hh][0:T, 0:GT], sT, qst[:, 4 * hh:4 * hh + 4, T * b:T * b + T], start=True, stop=True)
                mm.then_inc(s["om_done"], 1)

            def gather(b, k4):
                pe.wait_ge(s["om_out"], k4 + 2)
                pe.wait_ge(s["es_out"], k4 + 2)
                for h in range(HEADS):
                    mm = pe.matmul(ps[6][0:T, D * b:D * b + D], om[:, b % 2, h, :], es[:, b % 2, D * h:D * h + D],
                                   start=(h == 0), stop=(h == HEADS - 1))
                mm.then_inc(s["r_done"], 1)

            with pe.Fori(0, NG // 2) as it:
                for par in range(2):
                    g = it * 2 + par
                    turn(0, par, g)
                    for a in range(4):
                        pe.wait_ge(s["q_out"], 4 * g + a + 1)
                        pe.matmul(ps[1 + a % 2][:, 0:GT], wq[:, 2 * a:2 * a + 2, :], xg[0:D, par, :], start=True, stop=True).then_inc(s["q_done"], 1)
                    pe.wait_ge(s["q_out"], 4 * g + 6)
                    pe.wait_ge(s["r_added"], g + 1)
                    for b in range(GB):
                        attend(b, g * GB + b)
                        if b:
                            gather(b - 1, g * GB + b - 1)
                    gather(GB - 1, g * GB + GB - 1)

            def experts(i, n):
                with pe.Fori(0, NG // 2) as it:
                    for par in range(2):
                        g = it * 2 + par
                        turn(n, par, g)
                        pe.wait_ge(s["logit_out"], i * NG + g + 1)
                        for b in range(GB):
                            mm = pe.matmul(ps[1][0:T, NE * b:NE * b + NE], xg[:, par, T * b:T * b + T], wg[i][:, :], start=True, stop=True)
                        mm.then_inc(s["logit_done"], 1)
                if i:
                    pe.wait_ge(s["tri_in"], 1)
                    picks = picked[:, :, :].rearrange("p b e -> p (b e)")
                    pe.wait_ge(s["logit_out"], 2 * NG + 1)
                    pe.matmul(ps[1][0:T, 0:NB * NE], tri[:, :], picks, start=True, stop=True)
                    pe.matmul(ps[1][0:T, NB * NE:2 * NB * NE], ones[:, :], picks, start=True, stop=True).then_inc(s["tri_done"], 1)
                pe.wait_ge(s["xt_kept"], (i + 1) * NG)
                with pe.Fori(0, NG // 2) as it:
                    for par in range(2):
                        g = it * 2 + par
                        k = (i * NG + g) * 2 * NE
                        for c in range(2 * NE):
                            pe.wait_ge(s["hid_done"], k + c + 1)
                            pe.matmul(ps[2 + c % 2][:, 0:GT], w1[i][:, c // 2, (c % 2) * P:(c % 2) * P + P], xt[:, g, :],
                                      start=True, stop=True).then_inc(s["up_done"], 1)
                        pe.wait_ge(s["hid_done"], k + 2 * NE + 2)
                        for b in range(GB):
                            pe.wait_ge(s["added"], (i * NG + g) * GB + b + 1)
                            for e in range(NE):
                                for f in range(2):
                                    mm = pe.matmul(ps[4 + b % 2][0:T, D * e:D * e + D], hid[:, par, 2 * e + f, T * b:T * b + T],
                                                   w2[i][:, 2 * e + f, :], start=(f == 0), stop=(f == 1))
                            mm.then_inc(s["down_done"], 1)

            experts(0, 1)

            with pe.Fori(0, NG // 2) as it:
                for par in range(2):
                    g = it * 2 + par
                    turn(2, par, g)
                    for r in range(2):
                        for q in range(GATES):
                            pe.wait_ge(s[("xw_act", "xw_dve")[q % 2]], g * 4 + r * 2 + q // 2 + 1)
                            pe.matmul(ps[2 + q % 2][:, 0:GT], lw[r][:, HID * q:HID * q + HID], xg[:, par, :], start=True, stop=True).then_inc(s["xw_done"], 1)
            pe.wait_ge(s["xw_act"], NG * 4 + 1)
            pe.wait_ge(s["xw_dve"], NG * 4 + 1)

            def gates(r, bank, share, state):
                pe.matmul(bank[:, 0:P], ident[:, :], share, start=True, stop=False, skip_group_check=True)
                pe.wait_ge(s[f"h{r}"], state[1])
                for q in range(GATES):
                    mm = pe.matmul(bank[:, NB * GATE_AT[q]:NB * GATE_AT[q] + NB], lu[r][:, HID * q:HID * q + HID], state[0],
                                   start=False, stop=(q == GATES - 1), skip_group_check=True)
                mm.then_inc(s[f"z{r}"], 1)

            with pe.Fori(0, T // 2) as it:
                for par in range(2):
                    st = it * 2 + par
                    for r in range(2):
                        at = st if r == 0 else (T - 1) - st
                        gates(r, ps[2 * r + par], xw[:, r, at, :], (hs[:, r, par, :], st + 1))
            for r in range(2):
                pe.wait_ge(s[f"h{r}"], T + 1)
            for q in range(GATES):
                o = NB * GATE_AT[q]
                for k in range(2):
                    pe.matmul(ps[4][:, o:o + NB], lwd[:, k, HID * q:HID * q + HID], hs[:, k, 0, :], start=(k == 0), stop=False)
                mm = pe.matmul(ps[4][:, o:o + NB], lbd[:, HID * q:HID * q + HID], ones[0:1, 0:NB], start=False, stop=True)
            mm.then_inc(s["zc_done"], 1)
            pe.wait_ge(s["zc_out"], 1)
            with pe.Fori(0, T // 2) as it:
                for par in range(2):
                    st = it * 2 + par
                    gates(2, ps[par], zc[:, :], (hd[:, st, :], st + 1))
            pe.wait_ge(s["h2"], T + 1)
            for b in range(NB):
                if b % 8 == 0:
                    pe.wait_ge(s["dec_out"], b // 8 + 1)
                mm = pe.matmul(ps[2 + (b // 8) % 2][0:T, D * (b % 8):D * (b % 8) + D], hd[:, 1:T + 1, b], wo[:, :], start=True, stop=True)
                if b % 8 == 7:
                    mm.then_inc(s["dec_done"], 1)
            experts(1, 3)

        @block.scalar
        def _(act):
            act.sem_inc(s["turned_out"], 1)
            act.sem_inc(s["q_out"], 2)
            act.sem_inc(s["es_out"], 1)
            act.sem_inc(s["xw_act"], 1)
            act.sem_inc(s["hid_done"], 2)

            def squares(n):
                act.wait_ge(s["centred"], n + 1)
                act.activation(sq_[:, :, :], xc_[:, :, :], ACT.Square).then_inc(s["squared"], 1)

            def turned(n, par, g, keep=False):
                act.wait_ge(s["turned"], n * NG + g + 1)
                dsts = ((xt[0:D, g, :], "xt_kept"),) if keep else ()
                for dst, done in dsts + ((xg[0:D, par, :], "turned_out"),):
                    for h in range(2):
                        cp = act.copy(dst.rearrange("p (b h t) -> p h b t", h=2, t=T)[:, h],
                                      ps[0][D * h:D * h + D, 0:2 * T].rearrange("p (b t) -> p b t", t=T))
                    cp.then_inc(s[done], 1)

            squares(0)
            with act.Fori(0, NG // 2) as it:
                for par in range(2):
                    g = it * 2 + par
                    turned(0, par, g)
                    for a in range(4):
                        act.wait_ge(s["q_done"], 4 * g + a + 1)
                        for hh in range(2):
                            cp = act.copy(qst[:, 2 * a + hh, :], ps[1 + a % 2][D * hh:D * hh + D, 0:GT])
                        cp.then_inc(s["q_out"], 1)
                    for b in range(GB):
                        k4 = g * GB + b
                        act.wait_ge(s["es_done"], k4 + 1)
                        act.copy(es[:, b % 2, :], ps[3][0:T, :]).then_inc(s["es_out"], 1)

            def experts(i, n):
                squares(n)
                with act.Fori(0, NG // 2) as it:
                    for par in range(2):
                        g = it * 2 + par
                        turned(n, par, g, True)
                act.wait_ge(s["exp_in"], i + 1)
                act.activation(gate[:, :, :], gate[:, :, :], ACT.Exp).then_inc(s["exp_done"], 1)
                with act.Fori(0, NG // 2) as it:
                    for par in range(2):
                        g = it * 2 + par
                        k = (i * NG + g) * 2 * NE
                        for c in range(2 * NE):
                            act.wait_ge(s["up_done"], k + c + 1)
                            act.activation(hid[:, par, c, :], ps[2 + c % 2][:, 0:GT], ACT.Relu if i else ACT.Gelu).then_inc(s["hid_done"], 1)

            experts(0, 1)
            squares(2)
            with act.Fori(0, NG // 2) as it:
                for par in range(2):
                    g = it * 2 + par
                    turned(2, par, g)
                    for r in range(2):
                        for q in (0, 2):
                            act.wait_ge(s["xw_done"], g * 8 + r * 4 + q + 1)
                            o = NB * GATE_AT[q]
                            act.copy(xw[:, r, :, o:o + NB].rearrange("p t (g b) -> p g b t", b=GB)[:, g],
                                     ps[2 + q % 2][:, 0:GT].rearrange("p (b t) -> p b t", b=GB)).then_inc(s["xw_act"], 1)

            def cell(r, bank, st):
                act.wait_ge(s[f"z{r}"], st + 1)
                act.activation(sig[:, r, :], bank[:, 0:3 * NB], ACT.Sigmoid)
                act.activation(tg[:, r, :], bank[:, 3 * NB:4 * NB], ACT.Tanh).then_inc(s[f"s{r}"], 1)

            def cell_out(r, st):
                act.wait_ge(s[f"c{r}"], st + 1)
                act.activation(tc_[:, r, :], cs[:, r, :], ACT.Tanh).then_inc(s[f"tc{r}"], 1)

            with act.Fori(0, T // 2) as it:
                for par in range(2):
                    st = it * 2 + par
                    for r in range(2):
                        cell(r, ps[2 * r + par], st)
                    for r in range(2):
                        cell_out(r, st)
            with act.Fori(0, T // 2) as it:
                for par in range(2):
                    st = it * 2 + par
                    cell(2, ps[par], st)
                    cell_out(2, st)
            experts(1, 3)

        @block.vector
        def _(dve):
            dve.sem_inc(s["om_out"], 1)
            dve.sem_inc(s["r_added"], 1)
            dve.sem_inc(s["logit_out"], 1)
            dve.sem_inc(s["added"], 2)
            dve.sem_inc(s["xw_dve"], 1)
            dve.sem_inc(s["dec_out"], 2)
            dve.memset(xg[D:D + 1], 1.0)
            dve.memset(xt[D:D + 1], 1.0)
            dve.memset(ones[:, :], 1.0)
            dve.memset(hs[:], 0.0)
            dve.memset(cs[:], 0.0).then_inc(s["setup_done"], 1)
            for r in range(3):
                dve.sem_inc(s[f"h{r}"], 1)
            dve.wait_ge(s["loaded"], 16 * N_LOADS)
            dve.wait_ge(s["we_turned"], 1)
            dve.tensor_copy(wet[:, :], ps[0][0:D, :]).then_inc(s["wet_done"], 1)

            def wide(v):
                return v.unsqueeze(2).broadcast_to([T, NB, D])

            def normalise(n):
                dve.reduce_sum(mean[:, :], x[:, :, :], AX.X).then_inc(s["sums"], 1)
                dve.wait_ge(s["sums"], n + 1)
                dve.tensor_scalar(mean[:, :], mean[:, :], 1.0 / D, None, ALU.mult).then_inc(s["meaned"], 1)
                dve.wait_ge(s["meaned"], n + 1)
                dve.tensor_tensor(xc_[:, :, :], x[:, :, :], wide(mean[:, :]), ALU.subtract).then_inc(s["centred"], 1)
                dve.wait_ge(s["squared"], n + 1)
                dve.reduce_sum(var[:, :], sq_[:, :, :], AX.X).then_inc(s["varied"], 1)
                dve.wait_ge(s["rstd"], n + 1)

            def scale(n, par, g):
                k = n * NG + g
                dve.wait_ge(s["turned_out"], k + 1)
                xb = xc_[:, bass.ts(g, GB), :]
                dve.tensor_tensor(norm[:, par, :, :], xb, rs[:, bass.ts(g, GB)].unsqueeze(2).broadcast_to([T, GB, D]), ALU.mult).then_inc(s["normed"], 1)

            normalise(0)
            with dve.Fori(0, NG // 2) as it:
                for par in range(2):
                    g = it * 2 + par
                    scale(0, par, g)
                    for b in range(GB):
                        k4 = g * GB + b
                        dve.wait_ge(s["om_done"], k4 + 1)
                        for hh in range(2):
                            mk = dve.tensor_tensor(om[:, b % 2, 4 * hh:4 * hh + 4, :], ps[4 + hh][0:T, 0:GT].rearrange("p (h t) -> p h t", h=4),
                                                   tri[:, :].unsqueeze(1).broadcast_to([T, 4, T]), ALU.mult)
                        mk.then_inc(s["om_out"], 1)
                    dve.wait_ge(s["r_done"], (g + 1) * GB)
                    xb = x[:, bass.ts(g, GB), :]
                    dve.tensor_tensor(xb, ps[6][0:T, 0:GB * D].rearrange("p (b d) -> p b d", b=GB), xb, ALU.add).then_inc(s["r_added"], 1)
            dve.wait_ge(s["r_added"], NG + 1)
            steps = [0]

            def step(ins):
                steps[0] += 1
                ins.then_inc(s["gate_step"], 1)
                dve.wait_ge(s["gate_step"], steps[0])

            def by_token(v):
                return v.unsqueeze(2).broadcast_to([T, NB, NE])

            def experts(i, n):
                normalise(n)
                with dve.Fori(0, NG // 2) as it:
                    for par in range(2):
                        g = it * 2 + par
                        scale(n, par, g)
                        dve.wait_ge(s["logit_done"], i * NG + g + 1)
                        dve.tensor_copy(logit[:, bass.ts(g, GB), :], ps[1][0:T, 0:GB * NE].rearrange("p (b e) -> p b e", b=GB)).then_inc(s["logit_out"], 1)
                dve.wait_ge(s["logit_out"], (i + 1) * NG + 1)
                step(dve.reduce_max(top[:, :], logit[:, :, :], AX.X))
                dve.tensor_tensor(gate[:, :, :], logit[:, :, :], by_token(top[:, :]), ALU.subtract).then_inc(s["exp_in"], 1)
                dve.wait_ge(s["exp_done"], i + 1)
                if i:
                    step(dve.reduce_sum(total[:, :], gate[:, :, :], AX.X))
                    step(dve.reciprocal(total[:, :], total[:, :]))
                    step(dve.tensor_tensor(gate[:, :, :], gate[:, :, :], by_token(total[:, :]), ALU.mult))
                key = gate if i else logit
                other = key[:, :, :].unsqueeze(2).broadcast_to([T, NB, NE, NE])
                own = key[:, :, :].unsqueeze(3).broadcast_to([T, NB, NE, NE])
                step(dve.tensor_tensor(above, other, own, ALU.is_gt))
                step(dve.tensor_tensor(equal, other, own, ALU.is_equal))
                step(dve.tensor_tensor(xc_[:, :, :], xc_[:, :, :], below[:, :, :].rearrange("p a b -> p (a b)").unsqueeze(1).broadcast_to([T, NB, 64]), ALU.mult))
                step(dve.tensor_tensor(sq_[:, :, :], sq_[:, :, :], xc_[:, :, :], ALU.add))
                step(dve.reduce_sum(picked[:, :, :], above, AX.X))
                step(dve.tensor_scalar(picked[:, :, :], picked[:, :, :], 1.5 - i, None, ALU.is_lt))
                step(dve.tensor_tensor(gate[:, :, :], gate[:, :, :], picked[:, :, :], ALU.mult))
                if i == 0:
                    step(dve.reduce_sum(total[:, :], gate[:, :, :], AX.X))
                    step(dve.reciprocal(total[:, :], total[:, :]))
                    step(dve.tensor_tensor(gate[:, :, :], gate[:, :, :], by_token(total[:, :]), ALU.mult))
                else:
                    dve.sem_inc(s["tri_in"], 1)
                    dve.wait_ge(s["tri_done"], 1)
                    flat = lambda v: v.rearrange("p b e -> p (b e)")
                    n_all = NB * NE
                    step(dve.memset(place[:, 0, 0:1, :], 0.0))
                    step(dve.tensor_copy(flat(place[:, 0, :, :])[:, NE:], ps[1][0:T, n_all:2 * n_all - NE]))
                    step_b, cur = 1, 0
                    while step_b < NB:
                        a, b = flat(place[:, cur, :, :]), flat(place[:, 1 - cur, :, :])
                        w = step_b * NE
                        step(dve.tensor_copy(b[:, 0:w], a[:, 0:w]))
                        step(dve.tensor_tensor(b[:, w:], a[:, w:], a[:, 0:n_all - w], ALU.add))
                        step_b, cur = 2 * step_b, 1 - cur
                    step(dve.tensor_tensor(flat(place[:, 1 - cur, :, :]), ps[1][0:T, 0:n_all], flat(place[:, cur, :, :]), ALU.add))
                    step(dve.tensor_scalar(place[:, cur, :, :], place[:, 1 - cur, :, :], CAP + 0.5, None, ALU.is_lt))
                    step(dve.tensor_tensor(gate[:, :, :], gate[:, :, :], place[:, cur, :, :], ALU.mult))
                with dve.Fori(0, NG // 2) as it:
                    for par in range(2):
                        g = it * 2 + par
                        for b in range(GB):
                            k4 = (i * NG + g) * GB + b
                            r = b % 2
                            eye = lambda v: v.rearrange("p (e d) -> p e d", e=NE)
                            dve.wait_ge(s["down_done"], k4 + 1)
                            dve.tensor_tensor(mixed[:, r, :], ps[4 + r][0:T, :], b2[i][:, :, :].rearrange("p e d -> p (e d)"), ALU.add).then_inc(s["added"], 1)
                            dve.wait_ge(s["added"], k4 + 3)
                            w = gate[:, bass.ds(g * GB + b, 1), :].rearrange("p a e -> p (a e)").unsqueeze(2).broadcast_to([T, NE, D])
                            dve.tensor_tensor(eye(weighed[:, r, :]), eye(mixed[:, r, :]), w, ALU.mult).then_inc(s["weighted"], 1)
                            dve.wait_ge(s["weighted"], k4 + 1)
                            to = y_all[:, bass.ds(g * GB + b, 1), :].rearrange("p a d -> p (a d)") if i else y[:, par, D * b:D * b + D]
                            dve.reduce_sum(to, weighed[:, r, :].rearrange("p (e d) -> p d e", e=NE), AX.X).then_inc(s["summed"], 1)
                        dve.wait_ge(s["summed"], (i * NG + g) * GB + GB)
                        if i == 0:
                            xb = x[:, bass.ts(g, GB), :]
                            dve.tensor_tensor(xb, xb, y[:, par, :].rearrange("p (b d) -> p b d", b=GB), ALU.add).then_inc(s["y_added"], 1)
                if i == 0:
                    dve.wait_ge(s["y_added"], NG)

            experts(0, 1)
            normalise(2)
            with dve.Fori(0, NG // 2) as it:
                for par in range(2):
                    g = it * 2 + par
                    scale(2, par, g)
                    for r in range(2):
                        for q in (1, 3):
                            dve.wait_ge(s["xw_done"], g * 8 + r * 4 + q + 1)
                            o = NB * GATE_AT[q]
                            dve.tensor_copy(xw[:, r, :, o:o + NB].rearrange("p t (g b) -> p g b t", b=GB)[:, g],
                                            ps[2 + q % 2][:, 0:GT].rearrange("p (b t) -> p b t", b=GB)).then_inc(s["xw_dve"], 1)

            def cell(r, st):
                dve.wait_ge(s[f"s{r}"], st + 1)
                dve.tensor_tensor(fc_[:, r, :], sig[:, r, NB:2 * NB], cs[:, r, :], ALU.mult)
                dve.tensor_tensor(ig[:, r, :], sig[:, r, 0:NB], tg[:, r, :], ALU.mult).then_inc(s[f"ig{r}"], 1)
                dve.wait_ge(s[f"ig{r}"], st + 1)
                dve.tensor_tensor(cs[:, r, :], fc_[:, r, :], ig[:, r, :], ALU.add).then_inc(s[f"c{r}"], 1)

            def cell_out(r, st, dst):
                dve.wait_ge(s[f"tc{r}"], st + 1)
                dve.tensor_tensor(dst, sig[:, r, 2 * NB:3 * NB], tc_[:, r, :], ALU.mult).then_inc(s[f"h{r}"], 1)

            with dve.Fori(0, T // 2) as it:
                for par in range(2):
                    st = it * 2 + par
                    for r in range(2):
                        cell(r, st)
                    for r in range(2):
                        cell_out(r, st, hs[:, r, 1 - par, :])
            dve.wait_ge(s["zc_done"], 1)
            dve.memset(hd[:, 0, :], 0.0)
            dve.memset(cs[:, 2, :], 0.0)
            dve.tensor_copy(zc[:, :], ps[4][:, 0:P]).then_inc(s["zc_out"], 1)
            with dve.Fori(0, T // 2) as it:
                for par in range(2):
                    st = it * 2 + par
                    cell(2, st)
                    cell_out(2, st, hd[:, bass.ds(st + 1, 1), :].rearrange("p a b -> p (a b)"))
            for b8 in range(QUARTERS):
                xb = x[:, 8 * b8:8 * b8 + 8, :]
                step(dve.tensor_tensor(xb, xb, bo[:, :].unsqueeze(1).broadcast_to([T, 8, D]), ALU.add))
                dve.wait_ge(s["dec_done"], b8 + 1)
                dve.tensor_tensor(xb, ps[2 + b8 % 2][0:T, :].rearrange("p (b d) -> p b d", b=8), xb, ALU.add).then_inc(s["dec_out"], 1)
            dve.wait_ge(s["dec_out"], 6)
            experts(1, 3)
            for m, v in enumerate((0.0, 1e4, -1e4)):
                fill = dve.memset(fills[:, m, :], v)
            step(fill)
            for v in range(QUARTERS):
                yq, xq = (a[:, 8 * v:8 * v + 8, :].rearrange("p b d -> p (b d)") for a in (y_all, x))
                for m, (border, op) in enumerate(((None, ALU.not_equal), (FLT_MAX, ALU.is_gt), (-FLT_MAX, ALU.is_lt))):
                    o_ = odd[:, m % 2, :]
                    if border is None:
                        step(dve.tensor_tensor(o_, yq, yq, op))
                    else:
                        step(dve.tensor_scalar(o_, yq, border, None, op))
                    step(dve.copy_predicated(yq, o_, fills[:, m, :]))
                dve.tensor_tensor(xq, xq, yq, ALU.add).then_inc(s["y_added"], 1)


def build(nc, d, out):
    img = nc.dram_tensor("img_tokens", [NB, HH, WW], F32).ap()
    with ExitStack() as sems:
        build_fno(nc, sems, d, img)
        build_tail(nc, sems, d, img, out)


def kernel(**inputs):
    import concourse.bacc as bacc
    from concourse.bass_utils import run_bass_kernel_spmd

    nc = bacc.Bacc("TRN2", target_bir_lowering=False, num_devices=1)
    arrays = {name: np.ascontiguousarray(a) for name, a in inputs.items()}
    arrays.update(fno_constants())
    arrays.update(tail_constants())
    d = {name: nc.dram_tensor(name, a.shape, mybir.dt.from_np(a.dtype), kind="ExternalInput").ap() for name, a in arrays.items()}
    out = nc.dram_tensor("out", [NB, T, D], F32, kind="ExternalOutput").ap()
    build(nc, d, out)
    return run_bass_kernel_spmd(nc, [arrays], core_ids=[0]).results[0]["out"]
```

```python
from contextlib import ExitStack

import numpy as np
import concourse.bass as bass
from concourse import mybir

F32 = mybir.dt.float32
U32 = mybir.dt.uint32
ALU = mybir.AluOpType
ACT = mybir.ActivationFunctionType
AX = mybir.AxisListType

B, HH, WW, CI, CH, LAYERS, MX, MY = 32, 64, 64, 3, 32, 4, 12, 12
P = 128
BG = B // 4
CHUNKS = 8
CW = 512
KYR = 2 * MY
MODES = MX * MY
ROWS4 = 4
EPS = 1e-5
I1_GROUPS, G2_GROUPS = 3, 4
FRONT = I1_GROUPS + G2_GROUPS
AT_GROUPS, F2_GROUPS = 3, 2
BACK = AT_GROUPS + F2_GROUPS
HALF = MY // 2
LAG = 3
FRONT_SLOTS = (0, 1, 2, 4, 5, 6, 7)
AT_SLOT, F2_SLOTS = 3, (5, 6)

NB, T, D = 32, 96, 64
TI = 64
NG, GB = 8, 4
GT = GB * T
HEADS = 8
NE, FF = 8, 256
HID, GATES = 128, 4
CAP = -(-5 * NB * T // (4 * NE))
NORMS = 4
QUARTERS = 4
FLT_MAX = float(np.finfo(np.float32).max)


def fno_constants():
    w = np.arange(WW)
    ang = lambda k, x: 2 * np.pi * k * x / 64.0
    f1 = np.zeros((2, WW, 64))
    for r in range(2):
        for ky in range(MY):
            f1[r, :, r * KYR + 2 * ky] = np.cos(ang(ky, w))
            f1[r, :, r * KYR + 2 * ky + 1] = -np.sin(ang(ky, w))
    f2 = np.zeros((2, HH, 64))
    i1 = np.zeros((64, 2, HH))
    h = np.arange(HH)
    for half in range(2):
        for kx in range(MX):
            f = kx + (HH - MX) * half
            c, s = np.cos(ang(f, h)), np.sin(ang(f, h))
            re, im = half * 24 + kx, half * 24 + 12 + kx
            f2[0, :, re], f2[1, :, re] = c, s
            f2[0, :, im], f2[1, :, im] = -s, c
            row = kx * 4 + half * 2
            i1[row, 0], i1[row, 1] = c / HH, s / HH
            i1[row + 1, 0], i1[row + 1, 1] = -s / HH, c / HH
    i2 = np.zeros((97, 2, 2, WW))
    for r4 in range(4):
        for ky in range(MY):
            a = (1.0 if ky == 0 else 2.0) / WW
            i2[r4 * KYR + 2 * ky, r4 // 2, r4 % 2] = a * np.cos(ang(ky, w))
            i2[r4 * KYR + 2 * ky + 1, r4 // 2, r4 % 2] = -a * np.sin(ang(ky, w))
    i2[96] = 1.0
    f = np.float32
    sign = np.ones((P, 1), f)
    sign[32:64] = sign[96:128] = -1
    return dict(k_f1=f1.reshape(P, 64).astype(f), k_f2=f2.reshape(P, 64).astype(f),
                k_i1=i1.reshape(64, P).astype(f), k_i2=i2.reshape(97, 256).astype(f),
                k_id=np.eye(P, dtype=f), k_sign=sign)


def build_fno(nc, sems, d, img):
    xs = nc.dram_tensor("x_planes", [B, CI, HH * WW], F32).ap()
    yd = nc.dram_tensor("y_modes", [ROWS4, CH, B, MODES], F32).ap()
    zd = nc.dram_tensor("z_modes", [BG, MX, ROWS4 * CH, 4 * MY], F32).ap()
    with ExitStack() as ctx:
        sb = lambda n, s: ctx.enter_context(nc.sbuf_tensor(n, s, F32))
        sem = lambda n: sems.enter_context(nc.semaphore(n))
        act_all = sb("act_all", [P, BG * CHUNKS, CW])
        w_raw = sb("w_raw", [P, CH * MODES])
        share = sb("share", [P, 3 * 1536])
        y_in = share[:, :].rearrange("p (b m) -> p b m", b=B)
        at = share[:, 0:1536]
        a_buf = share[:, 1536:3072]
        g_buf = share[:, 3072:4608]
        before = sb("before", [P, 2 * 2048])
        g2 = before[0:97, 0:2048].rearrange("p (a n) -> p a n", a=16)
        zpp = before[0:64, 2048:3584]
        xc = before[0:64, :].rearrange("p (r n) -> p r n", r=2)
        y_st = sb("y_st", [P, ROWS4 * MODES])
        work = sb("work", [P, 3 * CW + 16])
        t = work[:, 0:2 * CW].rearrange("p (r n) -> p r n", r=2)
        sq = work[:, 2 * CW:].rearrange("p (a c) -> p a c", c=CH + 1)
        w2 = work[:, 0:3 * CW].rearrange("p (r m n) -> p r m n", r=2, m=HALF)
        ht = sb("ht", [P, 2, CW])
        hin = sb("hin", [P, 2, CW])
        z_row = sb("z_row", [P, 2, B * MY])
        w_mean = sb("w_mean", [P, MODES])[:, :]
        vs = sb("vs", [P, 4, 16])
        rstd = sb("rstd", [P, 4, 16])
        nhalf = sb("nhalf", [P, 16])
        f1, f2, ident = sb("f1", [P, 64]), sb("f2", [P, 64]), sb("ident", [P, P])
        i1, i2, sign = sb("i1", [64, P]), sb("i2", [97, 2 * P]), sb("sign", [P, 1])
        w0 = sb("w0", [64, P])
        w0m = sb("w0m", [64, 4])
        wc = sb("wc", [P, LAYERS, P])
        cwn = act_all[:, 12, 0:CH]
        cwt = act_all[0:CH, 13, 0:LAYERS * CH].rearrange("p (l c) -> p l c", l=LAYERS)
        cwm = act_all[0:CH, 14, 0:LAYERS]
        cb = sb("cb", [97, LAYERS, CH])
        cbm = sb("cbm", [97, LAYERS])
        lng, lnb = sb("lng", [P, LAYERS + 1, CH]), sb("lnb", [P, LAYERS + 1, CH])
        fc1 = y_st[:, 0:512].rearrange("p (b f) -> p b f", b=4)
        fc2 = y_st[:, 512:576]
        fc3 = sb("fc3", [P, 64])
        fb = sb("fb", [P, 3])
        g1 = w_raw[:, 0:2 * CW].rearrange("p (r n) -> p r n", r=2)
        g2l = w_raw[:, 2 * CW:4 * CW].rearrange("p (r n) -> p r n", r=2)
        hc = w_raw[:, 6 * CW:8 * CW].rearrange("p (r n) -> p r n", r=2)
        o1 = w_raw[:, 4 * CW:4 * CW + P]
        o2 = w_raw[:, 5 * CW:5 * CW + P]
        xraw = act_all[:, 0:6, :].rearrange("p a n -> p (a n)")
        xpl = act_all[:, 6:12, :].rearrange("p a n -> p (a n)")
        ps = [ctx.enter_context(nc.psum_tensor(f"ps{i}", [P, CW], F32)) for i in range(8)]
        pt, pf, pg, pb = ps[2], ps[4], ps[5], ps[6]
        pz = [ps[0], ps[1], ps[3], ps[7]]
        pc, px = ps[3], ps[7]

        names = """consts_in filled zeroed params_in x_in x_split x_stored xc0_in xc1_in w0_ready wc_raw wc_t wc_ready prep
            z_done hin_ready squared var_sum nhalf_set rstd_ready t_scaled t_gained t_ready gelu_done tr_done hc_ready
            f1_done a_written zpp_in fr_done fr_evac bk_done bk_evac y_stored
            w_in w_meaned w_scaled w_centred y_in w2_clear guard_set w2_dve w2_act mix_half zrow_ready z_stored0 z_stored1
            bias_set fc_clear fc_in fc1_done g1_ready fc2_done g2_ready fc3_done o1_ready o_tr o2_ready img_stored""".split()
        s = {n: sem(n) for n in names}
        xc_in, z_stored = [s["xc0_in"], s["xc1_in"]], [s["z_stored0"], s["z_stored1"]]
        N_CONST = 6
        block = ctx.enter_context(nc.Block())

        @block.sync
        def _(sp):
            for dst, name in ((f1, "k_f1"), (f2, "k_f2"), (ident, "k_id"), (i1, "k_i1"), (i2, "k_i2"), (sign, "k_sign")):
                sp.dma_start(dst[:, :], d[name]).then_inc(s["consts_in"], 16)
            xv = d["x"].rearrange("(i b) h w c -> (b h) i (w c)", b=2)
            sp.dma_start(xraw.rearrange("p (i n) -> p i n", i=16), xv).then_inc(s["x_in"], 16)
            sp.dma_start(cwn, d["L0_tok_conv_w"].rearrange("l o c -> (l o) c")).then_inc(s["params_in"], 16)
            sp.dma_start(cb[96:97, :, :], d["L0_tok_conv_b"].rearrange("(a l) c -> a l c", a=1)).then_inc(s["params_in"], 16)
            sp.wait_ge(s["zeroed"], 1)
            for b in range(4):
                sp.dma_start(w0[3 * b:3 * b + 3, 32 * b:32 * b + 32], d["L0_tok_fc0_w"]).then_inc(s["params_in"], 16)
                sp.dma_start(w0[32:33, 32 * b:32 * b + 32], d["L0_tok_fc0_b"].rearrange("(a c) -> a c", a=1)).then_inc(s["params_in"], 16)
            for b in range(2):
                with nc.allow_non_contiguous_dma(reason="a column of 64 weights"):
                    sp.dma_start(fc3[64 * b:64 * b + 64, b:b + 1], d["L0_tok_fc3_w"]).then_inc(s["params_in"], 16)
                    sp.dma_start(fb[64 * b:64 * b + 64, 1:2], d["L0_tok_fc2_b"].rearrange("(c a) -> c a", a=1)).then_inc(s["params_in"], 16)
            with nc.allow_non_contiguous_dma(reason="a column of biases"):
                sp.dma_start(fb[:, 0:1], d["L0_tok_fc1_b"].rearrange("(c a) -> c a", a=1)).then_inc(s["params_in"], 16)
                sp.dma_start(fb[:, 2:3], d["L0_tok_fc3_b"].rearrange("(a c) -> a c", a=1).broadcast_to([P, 1])).then_inc(s["params_in"], 16)
            for dst, first, rest in ((lng, "L0_tok_ln0_g", "L0_tok_ln_g"), (lnb, "L0_tok_ln0_b", "L0_tok_ln_b")):
                sp.dma_start(dst[:, 0, :], d[first].rearrange("(a c) -> a c", a=1).broadcast_to([P, CH])).then_inc(s["params_in"], 16)
                sp.dma_start(dst[:, 1:, :].rearrange("p l c -> p (l c)"),
                             d[rest].rearrange("(a l) c -> a (l c)", a=1).broadcast_to([P, LAYERS * CH])).then_inc(s["params_in"], 16)
            sp.wait_ge(s["x_split"], 1)
            for b in range(2):
                for c in range(CI):
                    sp.dma_start(xs.rearrange("(i b) c (h w) -> b c h i w", b=2, w=WW)[b, c],
                                 xpl.rearrange("p (i c w) -> p i c w", i=16, c=CI)[64 * b:64 * b + 64, :, c, :]).then_inc(s["x_stored"], 16)
            sp.wait_ge(s["x_stored"], 16 * 6)

            def load_xc(g, part):
                src = xs.rearrange("(g b) c n -> g (b c) n", b=4)[g]
                sp.dma_start(xc[0:12, part, :], src[:, part * 2048:part * 2048 + 2048]).then_inc(xc_in[part], 16)

            def load_w(l):
                for q, name in enumerate(("w1r", "w1i", "w2r", "w2i")):
                    src = d["L0_tok_" + name].rearrange("l i o x y -> l i (o x y)")
                    sp.dma_start(w_raw[32 * q:32 * q + 32, :], src[l]).then_inc(s["w_in"], 16)

            def store_y(n, g):
                sp.wait_ge(s["bk_evac"], BACK * n + BACK + 1)
                dst = yd.rearrange("q c (g b) m -> g b c q m", b=4)[g]
                for b in range(4):
                    sp.dma_start(dst[b], y_st[32 * b:32 * b + 32, :].rearrange("p (q m) -> p q m", q=ROWS4)).then_inc(s["y_stored"], 16)

            def load_zpp(u, g):
                sp.dma_start(zpp[0:48], zd.rearrange("g x (q o) r -> g (x q) (o r)", q=ROWS4)[g]).then_inc(s["zpp_in"], 16)

            def mix(l):
                sp.wait_ge(s["y_stored"], 64 * BG * (l + 1) + 1)
                sp.dma_start(share[:, :], yd.rearrange("q c b m -> (q c) (b m)")).then_inc(s["y_in"], 16)
                with sp.Fori(0, MX // 2) as it:
                    for half in range(2):
                        row = l * MX + it * 2 + half
                        sp.wait_ge(s["zrow_ready"], row + 3)
                        sp.dma_start(zd.rearrange("g x p r -> x p g r")[it * 2 + half],
                                     z_row[:, half, :].rearrange("p (g r) -> p g r", g=BG)).then_inc(z_stored[half], 16)
                for half in range(2):
                    sp.wait_ge(z_stored[half], 96 * (l + 1) + 16)

            def next_xc(g, part):
                sp.wait_ge(s["z_done"], g * CHUNKS + 4 * part + 4)
                load_xc(g + 1, part)

            load_w(0)
            for part in range(2):
                load_xc(0, part)
            for part in range(2):
                next_xc(0, part)
            with sp.Fori(1, BG - 1) as g:
                next_xc(g, 0)
                store_y(g - 1, g - 1)
                next_xc(g, 1)
            store_y(BG - 2, BG - 2)
            store_y(BG - 1, BG - 1)

            def next_zpp(u, g):
                sp.wait_ge(s["fr_done"], (u - 1) * FRONT + I1_GROUPS + 5)
                load_zpp(u, g)

            with sp.Fori(0, LAYERS - 1) as l:
                mix(l)
                sp.wait_ge(s["mix_half"], 2 * MX * (l + 1) + 2)
                load_w(l + 1)
                load_zpp(l * BG, 0)
                next_zpp(l * BG + 1, 1)
                next_zpp(l * BG + 2, 2)
                with sp.Fori(0, BG - 3) as g:
                    next_zpp(l * BG + g + 3, g + 3)
                    store_y(BG + l * BG + g, g)
                for g in range(BG - 3, BG):
                    store_y(BG + l * BG + g, g)
            mix(LAYERS - 1)
            last = (LAYERS - 1) * BG
            load_zpp(last, 0)
            sp.wait_ge(s["fc_clear"], 1)
            for b in range(4):
                sp.dma_start(fc1[32 * b:32 * b + 32, b, :], d["L0_tok_fc1_w"]).then_inc(s["fc_in"], 16)
            sp.dma_start(fc2, d["L0_tok_fc2_w"]).then_inc(s["fc_in"], 16)

            def store_img(g):
                sp.wait_ge(s["o2_ready"], g + 2)
                sp.dma_start(img.rearrange("(g b) (j r) w -> g (b j) (r w)", b=4, r=2)[g], o2).then_inc(s["img_stored"], 16)

            next_zpp(last + 1, 1)
            next_zpp(last + 2, 2)
            with sp.Fori(0, BG - 3) as g:
                next_zpp(last + g + 3, g + 3)
                store_img(g)
            for g in range(BG - 3, BG):
                store_img(g)
            sp.wait_ge(s["img_stored"], 16 * BG + 16)

        @block.gpsimd
        def _(pool):
            pool.memset(nhalf[:, :], -0.5).then_inc(s["nhalf_set"], 1)
            pool.wait_ge(s["nhalf_set"], 1)

            def unit(n):
                for k in range(CHUNKS):
                    q = n * CHUNKS + k
                    pool.wait_ge(s["var_sum"], q + 2)
                    pool.tensor_tensor(rstd[:, k % 4, :], vs[:, k % 4, :], nhalf[:, :], ALU.pow).then_inc(s["rstd_ready"], 1)
            with pool.Fori(0, LAYERS * BG) as n:
                unit(n)
            pool.wait_ge(s["y_stored"], 64 * LAYERS * BG + 1)
            pool.memset(fc1, 0.0).then_inc(s["fc_clear"], 1)
            with pool.Fori(LAYERS * BG, (LAYERS + 1) * BG) as n:
                unit(n)

        @block.tensor
        def _(pe):
            pe.wait_ge(s["consts_in"], 16 * N_CONST)
            pe.wait_ge(s["wc_raw"], 1)
            pe.transpose(pz[0][0:CH, 0:P], cwn, ident[:, :]).then_inc(s["wc_t"], 1)
            pe.wait_ge(s["prep"], 1)

            def z_first(g, q, k):
                part = k // 4
                if k % 4 == 0:
                    pe.wait_ge(xc_in[part], 16 * (g + 1))
                pe.wait_ge(s["t_scaled"], q + 1)
                for j in range(4):
                    mm = pe.matmul(pz[k % 4][:, P * j:P * j + P], xc[:, part, (k % 4) * CW + P * j:(k % 4) * CW + P * j + P],
                                   w0[:, :], start=True, stop=True)
                mm.then_inc(s["z_done"], 1)

            def z_mid(u, q, k, l, banks=4):
                pe.wait_ge(s["fr_evac"], u * FRONT + I1_GROUPS + k // 2 + 2)
                pe.wait_ge(s["hin_ready"], q - BG * CHUNKS + 1)
                pe.wait_ge(s["t_scaled"], q + 5 - banks)
                for j in range(4):
                    z = pz[k % banks][:, P * j:P * j + P]
                    pe.matmul(z, i2[:, (j % 2) * P:(j % 2) * P + P], g2[:, 2 * k + j // 2, :], start=True, stop=False)
                    mm = pe.matmul(z, hin[:, k % 2, P * j:P * j + P], wc[:, l - 1, :], start=False, stop=True)
                mm.then_inc(s["z_done"], 1)

            def front(u, i):
                if i == 0:
                    pe.wait_ge(s["zpp_in"], 16 * (u + 1))
                pe.wait_ge(s["fr_evac"], u * FRONT + i + 1)
                for j in range(4):
                    if i < I1_GROUPS:
                        ky = 4 * i + j
                        mm = pe.matmul(pg[:, P * j:P * j + P], zpp[:, ky::MY], i1[:, :], start=True, stop=True)
                    else:
                        hb = 4 * (i - I1_GROUPS) + j
                        mm = pe.transpose(pg[0:96, P * j:P * j + P], g_buf[:, 96 * hb:96 * hb + 96], ident[:, :])
                mm.then_inc(s["fr_done"], 1)

            def turn(q, k):
                pe.wait_ge(s["gelu_done"], q + 3)
                pe.wait_ge(s["hc_ready"], q + 1)
                for j in range(4):
                    mm = pe.transpose(pt[:, P * j:P * j + P], ht[:, k % 2, P * j:P * j + P], ident[:, :])
                mm.then_inc(s["tr_done"], 1)

            def along_w(q, k):
                pe.wait_ge(s["a_written"], q + 1)
                for j in range(4):
                    mm = pe.matmul(pf[:, 64 * j:64 * j + 64], ht[:, k % 2, P * j:P * j + P], f1[:, :], start=True, stop=True)
                mm.then_inc(s["f1_done"], 1)

            def back(n, i):
                if i == 0:
                    pe.wait_ge(s["a_written"], (n + 1) * CHUNKS + 1)
                pe.wait_ge(s["bk_evac"], n * BACK + i + 1 - (i == 1))
                for j in range(4 if i < AT_GROUPS else 6):
                    if i < AT_GROUPS:
                        c = P * (4 * i + j)
                        mm = pe.transpose((pg if i == 1 else pb)[:, P * j:P * j + P], a_buf[:, c:c + P], ident[:, :])
                    else:
                        c = P * (6 * (i - AT_GROUPS) + j)
                        mm = pe.matmul(pb[:, 64 * j:64 * j + 64], at[:, c:c + P], f2[:, :], start=True, stop=True)
                mm.then_inc(s["bk_done"], 1)

            def slots(n, g, l, z, ahead, behind, ks=range(CHUNKS)):
                q0 = n * CHUNKS
                for k in ks:
                    if z == "first":
                        z_first(g, q0 + k, k)
                    if z == "mid":
                        z_mid(n - BG, q0 + k, k, l)
                    if k == AT_SLOT and behind:
                        back(n - 1, 0)
                        if z == "mid":
                            pe.wait_ge(s["fr_evac"], (n - BG + 1) * FRONT + (I1_GROUPS if ahead else 0) + 1)
                        back(n - 1, 1)
                    if behind or k >= LAG:
                        turn(q0 + k - LAG, (k - LAG) % CHUNKS)
                    if k == AT_SLOT and behind:
                        back(n - 1, 2)
                    if behind or k >= LAG:
                        along_w(q0 + k - LAG, (k - LAG) % CHUNKS)
                    if behind and k in F2_SLOTS:
                        back(n - 1, AT_GROUPS + F2_SLOTS.index(k))
                    if ahead and k in FRONT_SLOTS:
                        if behind and k == AT_SLOT + 1:
                            pe.wait_ge(s["bk_evac"], (n - 1) * BACK + 3)
                        front(n - BG + 1, FRONT_SLOTS.index(k))

            def stage(n0, l, first=False):
                z = "first" if first else "mid"
                if not first:
                    pe.wait_ge(s["bias_set"], l)
                    for i in range(FRONT):
                        front(n0 - BG, i)
                slots(n0, 0, l, z, not first, False)
                with pe.Fori(1, BG - 1) as g:
                    slots(n0 + g, g, l, z, not first, True)
                slots(n0 + BG - 1, BG - 1, l, z, False, True)
                slots(n0 + BG, 0, l, None, False, True, range(LAG))
                for i in range(BACK):
                    back(n0 + BG - 1, i)

            def mix(l):
                with pe.Fori(0, MX // 2) as it:
                    for r in range(2):
                        row = l * MX + it * 2 + r
                        pe.wait_ge(s["zrow_ready"], row + 1)
                        for hf in range(2):
                            hq = l * 2 * MX + it * 4 + 2 * r + hf
                            pe.wait_ge(s["w2_dve"], hq + 1)
                            pe.wait_ge(s["w2_act"], hq + 1)
                            pe.wait_ge(s["y_in"], 16 * (l + 1))
                            for m in range(HALF):
                                mode = it * 2 * MY + r * MY + hf * HALF + m
                                c = (hf * HALF + m) * B
                                mm = pe.matmul(pz[r][:, c:c + B], w2[:, hf, m, :], y_in[:, :, mode], start=True, stop=True)
                            mm.then_inc(s["mix_half"], 1)

            stage(0, 0, True)
            with pe.Fori(0, LAYERS - 1) as l:
                mix(l)
                stage(BG + l * BG, l + 1)
            mix(LAYERS - 1)
            pe.wait_ge(s["fc_in"], 16 * 5)

            def last_chunk(q, k, c):
                turn(q, k)
                pe.wait_ge(s["hc_ready"], q + 2)
                for b in range(4):
                    pe.wait_ge(s["g1_ready"], 4 * c + b + 1)
                    bank = (pc, pf)[b % 2]
                    pe.matmul(bank[:, :], fc1[:, b, :], hc[:, k % 2, :], start=True, stop=True).then_inc(s["fc1_done"], 1)
                    if b >= 1:
                        second(c, b - 1)
                second(c, 3)

            def second(c, b):
                pe.wait_ge(s["g1_ready"], 4 * c + b + 3)
                if b % 2 == 0:
                    pe.wait_ge(s["g2_ready"], 2 * c + b // 2 + 1)
                mm = pe.matmul(px[64 * (b % 2):64 * (b % 2) + 64, :], fc2, g1[:, b % 2, :], start=True, stop=True)
                mm.then_inc(s["fc2_done"], 1)

            def third(c):
                pe.wait_ge(s["o1_ready"], c + 1)
                for pair in range(2):
                    pe.wait_ge(s["g2_ready"], 2 * c + pair + 2)
                    for j in range(4):
                        o = 256 * pair + 64 * j
                        mm = pe.matmul(pb[:, o:o + 64], g2l[:, pair, P * j:P * j + P], fc3[:, :], start=True, stop=True)
                mm.then_inc(s["fc3_done"], 1)

            def turn_out(g):
                pe.wait_ge(s["o1_ready"], (g + 1) * CHUNKS + 1)
                pe.wait_ge(s["o2_ready"], g + 1)
                pe.transpose(pg[:, 0:P], o1, ident[:, :]).then_inc(s["o_tr"], 1)

            def last_slots(g, z, ahead, behind, ks=range(CHUNKS)):
                n = LAYERS * BG + g
                q0 = n * CHUNKS
                for k in ks:
                    if z:
                        z_mid(n - BG, q0 + k, k, LAYERS, 2)
                    if ahead and k in FRONT_SLOTS:
                        if behind and k == AT_SLOT + 1:
                            pe.wait_ge(s["o2_ready"], g + 1)
                        front(n - BG + 1, FRONT_SLOTS.index(k))
                    if behind and k == AT_SLOT:
                        if z:
                            pe.wait_ge(s["fr_evac"], (n - BG + 1) * FRONT + (I1_GROUPS if ahead else 0) + 1)
                        turn_out(g - 1)
                    if k >= 3 or behind:
                        third(g * CHUNKS + k - 3)
                    if (k >= 2 or behind) and (z or k < 2):
                        last_chunk(q0 + k - 2, k % 2, g * CHUNKS + k - 2)

            pe.wait_ge(s["bias_set"], LAYERS)
            for i in range(FRONT):
                front((LAYERS - 1) * BG, i)
            last_slots(0, True, True, False)
            with pe.Fori(1, BG - 1) as g:
                last_slots(g, True, True, True)
            last_slots(BG - 1, True, False, True)
            last_slots(BG, False, False, True, range(3))
            turn_out(BG - 1)

        @block.scalar
        def _(act):
            act.sem_inc(s["hc_ready"], 1)
            act.sem_inc(s["fr_evac"], 1)
            act.sem_inc(s["gelu_done"], 2)

            def square(q, k, banks=4):
                act.wait_ge(s["z_done"], q + 1)
                act.wait_ge(s["var_sum"], q + 1)
                act.activation(sq[:, :, 0:CH], pz[k % banks][:, :].rearrange("p (a c) -> p a c", c=CH), ACT.Square, scale=CH ** -0.5).then_inc(s["squared"], 1)

            def gelu(q, k, first):
                act.wait_ge(s["t_ready"], q + 1)
                act.wait_ge(s["f1_done"], q + 1)
                act.activation(ht[:, k % 2, :], t[:, k % 2, :], ACT.Copy if first else ACT.Gelu).then_inc(s["gelu_done"], 1)

            def keep(c):
                act.copy(act_all[:, c, :], pt[:, :]).then_inc(s["hc_ready"], 1)

            def fetch(q, c, k, again=True):
                if again:
                    act.wait_ge(s["z_done"], q - 1)
                act.wait_ge(s["hc_ready"], q - BG * CHUNKS + 2)
                act.copy(hin[:, k % 2, :], act_all[:, c, :]).then_inc(s["hin_ready"], 1)

            def front(u, i):
                act.wait_ge(s["fr_done"], u * FRONT + i + 6)
                if i < I1_GROUPS:
                    dst = g_buf.rearrange("p (h r) -> p r h", r=KYR)[:, 8 * i:8 * i + 8, :]
                    act.copy(dst, pg[:, :].rearrange("p (r h) -> p r h", r=8)).then_inc(s["fr_evac"], 1)
                else:
                    o = 4 * (i - I1_GROUPS)
                    dst = g2[0:96, o:o + 4, :].rearrange("p j (b c) -> p j c b", b=4)
                    act.copy(dst, pg[0:96, :].rearrange("p (j c b) -> p j c b", j=4, b=4)).then_inc(s["fr_evac"], 1)

            def slots(n, g, first, z, ahead, behind, more=True, ks=range(CHUNKS)):
                q0 = n * CHUNKS
                for k in ks:
                    c = g * CHUNKS + k
                    if z and not first and (more or k < CHUNKS - 1):
                        fetch(q0 + k + 1, c + 1, k + 1)
                    if z:
                        square(q0 + k, k)
                    if behind or k >= LAG:
                        act.wait_ge(s["tr_done"], q0 + k - LAG + 1)
                    if (behind or k >= 2) and (z or k < 2):
                        gelu(q0 + k - 2, k, first)
                    if behind or k >= LAG:
                        keep(c - LAG)
                    if ahead and k in FRONT_SLOTS:
                        front(n - BG + 1, FRONT_SLOTS.index(k))

            def stage(n0, first=False):
                if not first:
                    fetch(n0 * CHUNKS, 0, 0, False)
                    for i in range(FRONT):
                        front(n0 - BG, i)
                slots(n0, 0, first, True, not first, False)
                with act.Fori(1, BG - 1) as g:
                    slots(n0 + g, g, first, True, not first, True)
                slots(n0 + BG - 1, BG - 1, first, True, False, True, False)
                slots(n0 + BG, BG, first, False, False, True, ks=range(LAG))

            def mix(l):
                act.wait_ge(s["w_centred"], l + 1)
                act.wait_ge(s["w2_clear"], l + 1)
                wv = w_raw[:, :].rearrange("p (o m) -> p m o", m=MODES)
                with act.Fori(0, MX) as row:
                    for hf in range(2):
                        hq = l * 2 * MX + row * 2 + hf
                        act.wait_ge(s["mix_half"], hq + 1)
                        for half in range(2):
                            for im in range(2):
                                dst = 64 * half + 32 * im
                                src = 64 * half + 32 * (1 - im)
                                cp = act.copy(w2[dst:dst + 32, hf, :, 64 * half + 32:64 * half + 64],
                                              wv[src:src + 32, bass.ds(row * MY + hf * HALF, HALF), :])
                        cp.then_inc(s["w2_act"], 1)

            stage(0, True)
            with act.Fori(0, LAYERS - 1) as l:
                mix(l)
                stage(BG + l * BG)
            mix(LAYERS - 1)
            act.sem_inc(s["g1_ready"], 2)
            act.sem_inc(s["g2_ready"], 1)

            def dense(c):
                for b in range(4):
                    act.wait_ge(s["fc1_done"], 4 * c + b + 1)
                    act.wait_ge(s["fc2_done"], 4 * c + b + 1)
                    act.activation(g1[:, b % 2, :], (pc, pf)[b % 2][:, :], ACT.Gelu, bias=fb[:, 0:1]).then_inc(s["g1_ready"], 1)
                    if b % 2 == 0 and b:
                        pair(c, 0)
                pair(c, 1)

            def pair(c, i):
                act.wait_ge(s["fc2_done"], 4 * c + 2 * i + 4)
                act.wait_ge(s["fc3_done"], c + 1)
                act.activation(g2l[:, i, :], px[:, :], ACT.Gelu, bias=fb[:, 1:2]).then_inc(s["g2_ready"], 1)

            def last_slots(g, z, ahead, behind, more=True, ks=range(CHUNKS)):
                n = LAYERS * BG + g
                q0 = n * CHUNKS
                for k in ks:
                    if z and (more or k < CHUNKS - 1):
                        fetch(q0 + k + 1, g * CHUNKS + k + 1, k + 1)
                    if z:
                        square(q0 + k, k, 2)
                    if ahead and k in FRONT_SLOTS:
                        front(n - BG + 1, FRONT_SLOTS.index(k))
                    if behind or k >= 2:
                        act.wait_ge(s["tr_done"], q0 + k - 1)
                        act.copy(hc[:, k % 2, :], pt[:, :]).then_inc(s["hc_ready"], 1)
                        dense(g * CHUNKS + k - 2)

            fetch(LAYERS * BG * CHUNKS, 0, 0, False)
            for i in range(FRONT):
                front((LAYERS - 1) * BG, i)
            last_slots(0, True, True, False)
            with act.Fori(1, BG - 1) as g:
                last_slots(g, True, True, True)
            last_slots(BG - 1, True, False, True, False)
            last_slots(BG, False, False, True, ks=range(2))

        @block.vector
        def _(dve):
            dve.sem_inc(s["t_scaled"], 4)
            dve.sem_inc(s["f1_done"], 2)
            dve.sem_inc(s["var_sum"], 1)
            dve.sem_inc(s["a_written"], 1)
            dve.sem_inc(s["bk_evac"], 1)
            dve.sem_inc(s["y_stored"], 1)
            dve.sem_inc(s["z_stored0"], 16)
            dve.sem_inc(s["z_stored1"], 16)
            dve.sem_inc(s["mix_half"], 2)
            dve.sem_inc(s["fr_done"], 5)
            dve.sem_inc(s["fc2_done"], 2)
            dve.sem_inc(s["fc3_done"], 1)
            dve.sem_inc(s["img_stored"], 16)
            dve.sem_inc(s["zrow_ready"], 2)
            for buf in (w0, fc3, wc, before):
                fill = dve.memset(buf[:], 0.0)
            fill.then_inc(s["filled"], 1)
            dve.wait_ge(s["filled"], 1)
            dve.memset(xc[32:33], 1.0)
            dve.memset(sq[:, :, CH:], EPS)
            dve.memset(fb[:], 0.0).then_inc(s["zeroed"], 1)
            dve.wait_ge(s["x_in"], 16)
            dve.tensor_copy(xpl.rearrange("p (i c w) -> p i c w", i=16, c=CI),
                            xraw.rearrange("p (i w c) -> p i c w", i=16, c=CI)).then_inc(s["x_split"], 1)
            n_prep = [0]

            def step(ins):
                n_prep[0] += 1
                ins.then_inc(s["w0_ready"], 1)
                dve.wait_ge(s["w0_ready"], n_prep[0])

            dve.wait_ge(s["params_in"], 16 * 20)
            dve.sem_inc(s["wc_raw"], 1)

            def centre(x, mean, c):
                step(dve.reduce_sum(mean, x, AX.X))
                step(dve.tensor_scalar(mean, mean, 1.0 / c, None, ALU.mult))
                step(dve.tensor_tensor(x, x, mean.unsqueeze(2).broadcast_to(x.shape), ALU.subtract))

            centre(w0[:, :].rearrange("p (b c) -> p b c", b=4), w0m[:, :], CH)
            centre(cb[96:97, :, :], cbm[96:97, :], CH)
            dve.wait_ge(s["wc_t"], 1)
            step(dve.tensor_copy(cwt[:, :, :], pz[0][0:CH, 0:P].rearrange("c (l o) -> c l o", l=LAYERS)))
            centre(cwt[:, :, :], cwm, CH)
            for b in range(4):
                step(dve.tensor_copy(wc[32 * b:32 * b + 32, :, 32 * b:32 * b + 32], cwt[:, :, :]))
            dve.wait_ge(s["consts_in"], 16 * N_CONST)
            dve.sem_inc(s["prep"], 1)

            def var_sum(q, k):
                dve.wait_ge(s["squared"], q + 1)
                dve.reduce_sum(vs[:, k % 4, :], sq, AX.X).then_inc(s["var_sum"], 1)

            def scale(q, k, l, dst, banks=4):
                groups = lambda x: x[:, k % 2, :].rearrange("p (a c) -> p a c", c=CH)
                dve.wait_ge(s["rstd_ready"], q + 1)
                dve.wait_ge(s["gelu_done"], q + 1)
                dve.tensor_tensor(groups(t), pz[k % banks][:, :].rearrange("p (a c) -> p a c", c=CH),
                                  rstd[:, k % 4, :].unsqueeze(2).broadcast_to([P, 16, CH]), ALU.mult).then_inc(s["t_scaled"], 1)
                dve.wait_ge(s["t_scaled"], q + 5)
                dve.tensor_tensor(groups(t), groups(t), lng[:, l, :].unsqueeze(1).broadcast_to([P, 16, CH]), ALU.mult).then_inc(s["t_gained"], 1)
                dve.wait_ge(s["t_gained"], q + 1)
                if dst is ht:
                    dve.wait_ge(s["tr_done"], q - 1)
                add = dve.tensor_tensor(groups(dst), groups(t), lnb[:, l, :].unsqueeze(1).broadcast_to([P, 16, CH]), ALU.add)
                add.then_inc(s["t_ready"], 1) if dst is t else add.then_inc(s["gelu_done"], 1)

            def a_evac(q, k):
                dve.wait_ge(s["f1_done"], q + 3)
                src = pf[:, 0:256].rearrange("p (j x) -> p j x", j=4)[:, :, 0:48].rearrange("p j (h r) -> p r j h", h=2)
                dst = a_buf.rearrange("p (r j h) -> p r j h", r=KYR, h=2)[:, :, 4 * k:4 * k + 4, :]
                dve.tensor_copy(dst, src).then_inc(s["a_written"], 1)

            def back(n, i):
                dve.wait_ge(s["bk_done"], n * BACK + i + 1)
                if i < AT_GROUPS:
                    cp = dve.tensor_copy(at[:, CW * i:CW * i + CW], (pg if i == 1 else pb)[:, :])
                else:
                    if i == AT_GROUPS:
                        dve.wait_ge(s["y_stored"], 64 * n + 1)
                    src = pb[:, 0:384].rearrange("p (y x) -> p x y", x=64)[:, 0:48, :]
                    dst = y_st[:, :].rearrange("p (x y) -> p x y", y=MY)[:, :, 6 * (i - AT_GROUPS):6 * (i - AT_GROUPS) + 6]
                    cp = dve.tensor_copy(dst, src)
                cp.then_inc(s["bk_evac"], 1)

            def slots(n, l, z, behind, ks=range(CHUNKS)):
                q0 = n * CHUNKS
                for k in ks:
                    if (behind or k >= 2) and (z or k < 2):
                        scale(q0 + k - 2, (k - 2) % CHUNKS, l, t)
                    if behind and k == AT_SLOT:
                        for i in range(AT_GROUPS):
                            back(n - 1, i)
                    if behind or k >= LAG:
                        a_evac(q0 + k - LAG, (k - LAG) % CHUNKS)
                    if behind and k in F2_SLOTS:
                        back(n - 1, AT_GROUPS + F2_SLOTS.index(k))
                    if z:
                        var_sum(q0 + k, k)

            def stage(n0, l):
                slots(n0, l, True, False)
                with dve.Fori(1, BG) as g:
                    slots(n0 + g, l, True, True)
                slots(n0 + BG, l, False, True, range(LAG))
                for i in range(BACK):
                    back(n0 + BG - 1, i)

            def mix(l):
                dve.wait_ge(s["w_in"], 64 * (l + 1))
                ov = w_raw[:, :].rearrange("p (o m) -> p m o", m=MODES)
                dve.reduce_sum(w_mean, ov, AX.X).then_inc(s["w_meaned"], 1)
                dve.wait_ge(s["w_meaned"], l + 1)
                dve.tensor_scalar(w_mean, w_mean, 1.0 / CH, None, ALU.mult).then_inc(s["w_scaled"], 1)
                dve.wait_ge(s["w_scaled"], l + 1)
                om = w_raw[:, :].rearrange("p (o m) -> p o m", m=MODES)
                dve.tensor_tensor(om, om, w_mean.unsqueeze(1).broadcast_to([P, CH, MODES]), ALU.subtract).then_inc(s["w_centred"], 1)
                dve.wait_ge(s["w_centred"], l + 1)
                dve.memset(w2, 0.0).then_inc(s["w2_clear"], 1)
                dve.wait_ge(s["w2_clear"], l + 1)
                bias = g2[96:97, :, :].rearrange("p a (b c) -> p (a b) c", c=CH)
                dve.tensor_copy(bias, cb[96:97, l, :].unsqueeze(1).broadcast_to([1, 64, CH])).then_inc(s["bias_set"], 1)
                with dve.Fori(0, MX // 2) as it:
                    for r in range(2):
                        row = l * MX + it * 2 + r
                        for hf in range(2):
                            hq = l * 2 * MX + it * 4 + 2 * r + hf
                            dve.wait_ge(s["mix_half"], hq + 1)
                            for half in range(2):
                                p0 = 64 * half
                                cp = dve.tensor_scalar(w2[p0:p0 + 64, hf, :, 64 * half:64 * half + 32],
                                                       ov[p0:p0 + 64, bass.ds(it * 2 * MY + r * MY + hf * HALF, HALF), :],
                                                       sign[p0:p0 + 64, :], None, ALU.mult)
                            cp.then_inc(s["w2_dve"], 1)
                        dve.wait_ge(s["mix_half"], 2 * row + 4)
                        dve.wait_ge(z_stored[r], 16 * (l * (MX // 2) + it) + 16)
                        dve.tensor_copy(z_row[:, r, :].rearrange("p (b y) -> p y b", y=MY),
                                        pz[r][:, 0:B * MY].rearrange("p (y b) -> p y b", y=MY)).then_inc(s["zrow_ready"], 1)
                dve.memset(sq[:, :, CH:], EPS).then_inc(s["guard_set"], 1)
                dve.wait_ge(s["guard_set"], l + 1)

            stage(0, 0)
            with dve.Fori(0, LAYERS - 1) as l:
                mix(l)
                stage(BG + l * BG, l + 1)
            mix(LAYERS - 1)
            dve.sem_inc(s["o1_ready"], 1)
            dve.sem_inc(s["o2_ready"], 1)

            def o1_evac(c, k):
                dve.wait_ge(s["fc3_done"], c + 2)
                src = pb[:, :].rearrange("p (a j x) -> p a j x", a=2, j=4)[:, :, :, 0:2].rearrange("p a j b -> p a b j")
                dst = o1.rearrange("p (a b j) -> p a b j", a=2, b=2)[:, :, :, 4 * k:4 * k + 4]
                dve.tensor_scalar(dst, src, fb[:, 2:3], None, ALU.add).then_inc(s["o1_ready"], 1)

            def turned_out(g):
                dve.wait_ge(s["o_tr"], g + 1)
                dve.wait_ge(s["img_stored"], 16 * g + 16)
                dve.tensor_copy(o2, pg[:, 0:P]).then_inc(s["o2_ready"], 1)

            def last_slots(g, z, behind, ks=range(CHUNKS)):
                q0 = (LAYERS * BG + g) * CHUNKS
                for k in ks:
                    if (behind or k >= 1) and (z or k < 1):
                        scale(q0 + k - 1, (k - 1) % CHUNKS, LAYERS, ht, 2)
                    if z:
                        var_sum(q0 + k, k)
                    if behind and k == AT_SLOT:
                        turned_out(g - 1)
                    if behind or k >= 3:
                        o1_evac(g * CHUNKS + k - 3, (k - 3) % CHUNKS)

            last_slots(0, True, False)
            with dve.Fori(1, BG) as g:
                last_slots(g, True, True)
            last_slots(BG, False, True, range(3))
            turned_out(BG - 1)


def tail_constants():
    u = np.arange(T)
    f = np.float32
    return dict(k_tri=(u[:, None] <= u[None, :]).astype(f),
                k_below=np.broadcast_to((np.arange(NE)[None, :] < np.arange(NE)[:, None]).reshape(1, 64), (T, 64)).astype(f).copy())


def build_tail(nc, sems, d, img, out):
    with ExitStack() as ctx:
        sb = lambda n, s, t=F32: ctx.enter_context(nc.sbuf_tensor(n, s, t))
        x = sb("x_tok", [T, NB, D])
        xc_ = sb("x_centred", [T, NB, D])
        sq_ = sb("x_squares", [T, NB, D])
        mean, var, rs, nh = sb("mean_t", [T, NB]), sb("var_t", [T, NB]), sb("rstd_t", [T, NB]), sb("nhalf_t", [T, NB])
        norm = sb("norm_t", [T, 2, GB, D])
        xg = sb("xg", [D + 1, 2, GT])
        xt = sb("xt", [D + 1, NG, GT])
        ident = sb("ident_t", [P, P])
        tri, ones = sb("tri", [T, T]), sb("ones_t", [T, T])
        below = sb("below", [T, NE, NE])
        big = sb("big", [P, 2 * T * P])
        qst = big[0:D, 0:HEADS * GT].rearrange("p (h n) -> p h n", h=HEADS)
        es = big[0:T, 3072:4096].rearrange("p (r n) -> p r n", r=2)
        om = big[0:T, 4096:5632].rearrange("p (r h n) -> p r h n", r=2, h=HEADS)
        wq, we, wet = sb("wq", [D, HEADS, D]), sb("we", [P, 4, D]), sb("wet", [D, HEADS * D])
        hid = big[:, 0:2 * 16 * GT].rearrange("p (r c n) -> p r c n", r=2, c=16)
        w1 = [sb(f"w1_{i}", [D + 1, NE, FF]) for i in range(2)]
        w2 = [sb(f"w2_{i}", [P, 2 * NE, D]) for i in range(2)]
        b2 = [sb(f"b2_{i}", [T, NE, D]) for i in range(2)]
        wg = [sb(f"wg_{i}", [D + 1, NE]) for i in range(2)]
        logit = sb("logit", [T, NB, NE])
        gate = sb("gate", [T, NB, NE])
        picked = sb("picked", [T, NB, NE])
        place = sb("place", [T, 2, NB, NE])
        top, total = sb("top", [T, NB]), sb("total", [T, NB])
        above = sq_[:, :, :].rearrange("p b (e f) -> p b e f", e=NE)
        equal = xc_[:, :, :].rearrange("p b (e f) -> p b e f", e=NE)
        mixed = big[0:T, 15392:16416].rearrange("p (r n) -> p r n", r=2)
        weighed = big[0:T, 16416:17440].rearrange("p (r n) -> p r n", r=2)
        y = sb("y_t", [T, 2, GB * D])
        y_all = sq_
        odd = sb("odd", [T, 2, 8 * D], U32)
        fills = big[0:T, 17440:17440 + 3 * 8 * D].rearrange("p (m n) -> p m n", m=3)
        xw = big[:, :].rearrange("p (r t n) -> p r t n", r=2, t=T)
        lw = [sb(f"lw_{i}", [D + 1, GATES * HID]) for i in range(2)]
        lu = [sb(f"lu_{i}", [HID, GATES * HID]) for i in range(3)]
        lwd = sb("lwd", [HID, 2, GATES * HID])
        lbd = sb("lbd", [1, GATES * HID])
        hs = sb("hs", [HID, 2, 2, NB])
        cs = sb("cs", [HID, 3, NB])
        sig = sb("sig", [HID, 3, 3 * NB])
        tg, tc_, fc_, ig = sb("tg", [HID, 3, NB]), sb("tc", [HID, 3, NB]), sb("fc", [HID, 3, NB]), sb("ig", [HID, 3, NB])
        zc = sb("zc", [HID, GATES * NB])
        hd = big[:, 12288:12288 + (T + 1) * NB].rearrange("p (t n) -> p t n", t=T + 1)
        wo, bo = sb("wo", [HID, D]), sb("bo", [T, D])
        ps = [ctx.enter_context(nc.psum_tensor(f"pt{i}", [P, 512], F32)) for i in range(8)]
        names = """loaded setup_done sums meaned centred squared varied powed rstd normed turned turned_out
            we_in we_turned wet_done q_done q_out es_done es_out om_done om_out r_done r_added
            logit_done logit_out up_done hid_done down_done added weighted summed y_added gate_step exp_in exp_done tri_in tri_done
            xw_done xw_act xw_dve z0 z1 z2 s0 s1 s2 c0 c1 c2 tc0 tc1 tc2 h0 h1 h2 fg0 fg1 fg2 ig0 ig1 ig2
            zc_done zc_out dec_done dec_out out_sent xt_kept """.split()
        s = {n: sems.enter_context(nc.semaphore("t_" + n)) for n in names}
        N_LOADS = 7 + 12 + 4 + 3 + 4
        GATE_AT = (0, 1, 3, 2)
        block = ctx.enter_context(nc.Block())

        def row(ap):
            return ap.rearrange("(a n) -> a n", a=1)

        @block.sync
        def _(sp):
            def ld(dst, src):
                sp.dma_start(dst, src).then_inc(s["loaded"], 16)
            ld(x[0:TI, :, :], img.rearrange("b t w -> t b w"))
            ld(x[TI:T, :, :], d["txt"].rearrange("b t w -> t b w"))
            ld(ident[:, :], d["k_id"])
            ld(tri[:, :], d["k_tri"])
            ld(below[:, :, :].rearrange("p a b -> p (a b)"), d["k_below"])
            ld(wq[:, :, :], d["L0_attn_Q"].rearrange("h i j -> i h j"))
            ld(we[:, :, :], d["L0_attn_E"].rearrange("(a h) i j -> (h i) a j", h=2))
            for i, (g, bg, a, b, c, e) in enumerate((("L0_ffn_Wg", "L0_ffn_bg", "L0_ffn_W1", "L0_ffn_b1", "L0_ffn_W2", "L0_ffn_b2"),
                                                     ("L1_ffn_gate_w", "L1_ffn_gate_b", "L1_ffn_w1", "L1_ffn_b1", "L1_ffn_w2", "L1_ffn_b2"))):
                ld(wg[i][0:D, :], d[g])
                ld(wg[i][D:D + 1, :], row(d[bg]))
                ld(w1[i][0:D, :, :], d[a].rearrange("e d f -> d e f"))
                ld(w1[i][D:D + 1, :, :], d[b].rearrange("(a e) f -> a e f", a=1))
                ld(w2[i][:, :, :], d[c].rearrange("e (k f) d -> f (e k) d", f=P))
                ld(b2[i][:, :, :].rearrange("p e d -> p (e d)"), d[e].rearrange("(a e) d -> a (e d)", a=1).broadcast_to([T, NE * D]))
            for i, (w, b) in enumerate((("Wf", "bf"), ("Wb", "bb"))):
                ld(lw[i][0:D, :], d["L1_attn_" + w])
                ld(lw[i][D:D + 1, :], row(d["L1_attn_" + b]))
            for i, u in enumerate(("Uf", "Ub", "Ud")):
                ld(lu[i][:, :], d["L1_attn_" + u])
            ld(lwd[:, :, :], d["L1_attn_Wd"].rearrange("(k p) n -> p k n", p=HID))
            ld(lbd[:, :], row(d["L1_attn_bd"]))
            ld(wo[:, :], d["L1_attn_Wo"])
            ld(bo[:, :], row(d["L1_attn_bo"]).broadcast_to([T, D]))
            for v in range(QUARTERS):
                sp.wait_ge(s["y_added"], NG + v + 1)
                sp.dma_start(out.rearrange("b t w -> t b w")[:, 8 * v:8 * v + 8], x[:, 8 * v:8 * v + 8, :]).then_inc(s["out_sent"], 16)
            sp.wait_ge(s["out_sent"], 16 * QUARTERS)

        @block.gpsimd
        def _(pool):
            pool.memset(nh[:, :], -0.5).then_inc(s["powed"], 1)
            for n in range(NORMS):
                pool.wait_ge(s["varied"], n + 1)
                pool.tensor_scalar(var[:, :], var[:, :], 1.0 / D, EPS, ALU.mult, ALU.add).then_inc(s["powed"], 1)
                pool.wait_ge(s["powed"], n + 2)
                pool.tensor_tensor(rs[:, :], var[:, :], nh[:, :], ALU.pow).then_inc(s["rstd"], 1)

        @block.tensor
        def _(pe):
            pe.wait_ge(s["loaded"], 16 * N_LOADS)
            pe.wait_ge(s["setup_done"], 1)
            for a in range(4):
                mm = pe.transpose(ps[0][0:D, P * a:P * a + P], we[:, a, :], ident[:, :])
            mm.then_inc(s["we_turned"], 1)
            pe.wait_ge(s["wet_done"], 1)

            def turn(n, par, g):
                k = n * NG + g
                pe.wait_ge(s["normed"], k + 1)
                pe.wait_ge(s["turned_out"], k + 1)
                for b2_ in range(GB // 2):
                    mm = pe.transpose(ps[0][:, T * b2_:T * b2_ + T], norm[:, par, 2 * b2_:2 * b2_ + 2, :], ident[0:T, 0:T])
                mm.then_inc(s["turned"], 1)
                pe.wait_ge(s["turned_out"], k + 2)

            def attend(b, k4):
                pe.wait_ge(s["es_out"], k4 + 1)
                sT = xg[0:D, par, T * b:T * b + T]
                pe.matmul(ps[3][0:T, :], sT, wet[:, :], start=True, stop=True).then_inc(s["es_done"], 1)
                pe.wait_ge(s["om_out"], k4 + 1)
                for hh in range(2):
                    mm = pe.matmul(ps[4 + hh][0:T, 0:GT], sT, qst[:, 4 * hh:4 * hh + 4, T * b:T * b + T], start=True, stop=True)
                mm.then_inc(s["om_done"], 1)

            def gather(b, k4):
                pe.wait_ge(s["om_out"], k4 + 2)
                pe.wait_ge(s["es_out"], k4 + 2)
                for h in range(HEADS):
                    mm = pe.matmul(ps[6][0:T, D * b:D * b + D], om[:, b % 2, h, :], es[:, b % 2, D * h:D * h + D],
                                   start=(h == 0), stop=(h == HEADS - 1))
                mm.then_inc(s["r_done"], 1)

            with pe.Fori(0, NG // 2) as it:
                for par in range(2):
                    g = it * 2 + par
                    turn(0, par, g)
                    for a in range(4):
                        pe.wait_ge(s["q_out"], 4 * g + a + 1)
                        pe.matmul(ps[1 + a % 2][:, 0:GT], wq[:, 2 * a:2 * a + 2, :], xg[0:D, par, :], start=True, stop=True).then_inc(s["q_done"], 1)
                    pe.wait_ge(s["q_out"], 4 * g + 6)
                    pe.wait_ge(s["r_added"], g + 1)
                    for b in range(GB):
                        attend(b, g * GB + b)
                        if b:
                            gather(b - 1, g * GB + b - 1)
                    gather(GB - 1, g * GB + GB - 1)

            def experts(i, n):
                with pe.Fori(0, NG // 2) as it:
                    for par in range(2):
                        g = it * 2 + par
                        turn(n, par, g)
                        pe.wait_ge(s["logit_out"], i * NG + g + 1)
                        for b in range(GB):
                            mm = pe.matmul(ps[1][0:T, NE * b:NE * b + NE], xg[:, par, T * b:T * b + T], wg[i][:, :], start=True, stop=True)
                        mm.then_inc(s["logit_done"], 1)
                if i:
                    pe.wait_ge(s["tri_in"], 1)
                    picks = picked[:, :, :].rearrange("p b e -> p (b e)")
                    pe.wait_ge(s["logit_out"], 2 * NG + 1)
                    pe.matmul(ps[1][0:T, 0:NB * NE], tri[:, :], picks, start=True, stop=True)
                    pe.matmul(ps[1][0:T, NB * NE:2 * NB * NE], ones[:, :], picks, start=True, stop=True).then_inc(s["tri_done"], 1)
                pe.wait_ge(s["xt_kept"], (i + 1) * NG)
                with pe.Fori(0, NG // 2) as it:
                    for par in range(2):
                        g = it * 2 + par
                        k = (i * NG + g) * 2 * NE
                        for c in range(2 * NE):
                            pe.wait_ge(s["hid_done"], k + c + 1)
                            pe.matmul(ps[2 + c % 2][:, 0:GT], w1[i][:, c // 2, (c % 2) * P:(c % 2) * P + P], xt[:, g, :],
                                      start=True, stop=True).then_inc(s["up_done"], 1)
                        pe.wait_ge(s["hid_done"], k + 2 * NE + 2)
                        for b in range(GB):
                            pe.wait_ge(s["added"], (i * NG + g) * GB + b + 1)
                            for e in range(NE):
                                for f in range(2):
                                    mm = pe.matmul(ps[4 + b % 2][0:T, D * e:D * e + D], hid[:, par, 2 * e + f, T * b:T * b + T],
                                                   w2[i][:, 2 * e + f, :], start=(f == 0), stop=(f == 1))
                            mm.then_inc(s["down_done"], 1)

            experts(0, 1)

            with pe.Fori(0, NG // 2) as it:
                for par in range(2):
                    g = it * 2 + par
                    turn(2, par, g)
                    for r in range(2):
                        for q in range(GATES):
                            pe.wait_ge(s[("xw_act", "xw_dve")[q % 2]], g * 4 + r * 2 + q // 2 + 1)
                            pe.matmul(ps[2 + q % 2][:, 0:GT], lw[r][:, HID * q:HID * q + HID], xg[:, par, :], start=True, stop=True).then_inc(s["xw_done"], 1)
            pe.wait_ge(s["xw_act"], NG * 4 + 1)
            pe.wait_ge(s["xw_dve"], NG * 4 + 1)

            def gates(r, bank, share, state):
                pe.matmul(bank[:, 0:P], ident[:, :], share, start=True, stop=False, skip_group_check=True)
                pe.wait_ge(s[f"h{r}"], state[1])
                for q in range(GATES):
                    mm = pe.matmul(bank[:, NB * GATE_AT[q]:NB * GATE_AT[q] + NB], lu[r][:, HID * q:HID * q + HID], state[0],
                                   start=False, stop=(q == GATES - 1), skip_group_check=True)
                mm.then_inc(s[f"z{r}"], 1)

            with pe.Fori(0, T // 2) as it:
                for par in range(2):
                    st = it * 2 + par
                    for r in range(2):
                        at = st if r == 0 else (T - 1) - st
                        gates(r, ps[2 * r + par], xw[:, r, at, :], (hs[:, r, par, :], st + 1))
            for r in range(2):
                pe.wait_ge(s[f"h{r}"], T + 1)
            for q in range(GATES):
                o = NB * GATE_AT[q]
                for k in range(2):
                    pe.matmul(ps[4][:, o:o + NB], lwd[:, k, HID * q:HID * q + HID], hs[:, k, 0, :], start=(k == 0), stop=False)
                mm = pe.matmul(ps[4][:, o:o + NB], lbd[:, HID * q:HID * q + HID], ones[0:1, 0:NB], start=False, stop=True)
            mm.then_inc(s["zc_done"], 1)
            pe.wait_ge(s["zc_out"], 1)
            with pe.Fori(0, T // 2) as it:
                for par in range(2):
                    st = it * 2 + par
                    gates(2, ps[par], zc[:, :], (hd[:, st, :], st + 1))
            pe.wait_ge(s["h2"], T + 1)
            for b in range(NB):
                if b % 8 == 0:
                    pe.wait_ge(s["dec_out"], b // 8 + 1)
                mm = pe.matmul(ps[2 + (b // 8) % 2][0:T, D * (b % 8):D * (b % 8) + D], hd[:, 1:T + 1, b], wo[:, :], start=True, stop=True)
                if b % 8 == 7:
                    mm.then_inc(s["dec_done"], 1)
            experts(1, 3)

        @block.scalar
        def _(act):
            act.sem_inc(s["turned_out"], 1)
            act.sem_inc(s["q_out"], 2)
            act.sem_inc(s["es_out"], 1)
            act.sem_inc(s["xw_act"], 1)
            act.sem_inc(s["hid_done"], 2)

            def squares(n):
                act.wait_ge(s["centred"], n + 1)
                act.activation(sq_[:, :, :], xc_[:, :, :], ACT.Square).then_inc(s["squared"], 1)

            def turned(n, par, g, keep=False):
                act.wait_ge(s["turned"], n * NG + g + 1)
                dsts = ((xt[0:D, g, :], "xt_kept"),) if keep else ()
                for dst, done in dsts + ((xg[0:D, par, :], "turned_out"),):
                    for h in range(2):
                        cp = act.copy(dst.rearrange("p (b h t) -> p h b t", h=2, t=T)[:, h],
                                      ps[0][D * h:D * h + D, 0:2 * T].rearrange("p (b t) -> p b t", t=T))
                    cp.then_inc(s[done], 1)

            squares(0)
            with act.Fori(0, NG // 2) as it:
                for par in range(2):
                    g = it * 2 + par
                    turned(0, par, g)
                    for a in range(4):
                        act.wait_ge(s["q_done"], 4 * g + a + 1)
                        for hh in range(2):
                            cp = act.copy(qst[:, 2 * a + hh, :], ps[1 + a % 2][D * hh:D * hh + D, 0:GT])
                        cp.then_inc(s["q_out"], 1)
                    for b in range(GB):
                        k4 = g * GB + b
                        act.wait_ge(s["es_done"], k4 + 1)
                        act.copy(es[:, b % 2, :], ps[3][0:T, :]).then_inc(s["es_out"], 1)

            def experts(i, n):
                squares(n)
                with act.Fori(0, NG // 2) as it:
                    for par in range(2):
                        g = it * 2 + par
                        turned(n, par, g, True)
                act.wait_ge(s["exp_in"], i + 1)
                act.activation(gate[:, :, :], gate[:, :, :], ACT.Exp).then_inc(s["exp_done"], 1)
                with act.Fori(0, NG // 2) as it:
                    for par in range(2):
                        g = it * 2 + par
                        k = (i * NG + g) * 2 * NE
                        for c in range(2 * NE):
                            act.wait_ge(s["up_done"], k + c + 1)
                            act.activation(hid[:, par, c, :], ps[2 + c % 2][:, 0:GT], ACT.Relu if i else ACT.Gelu).then_inc(s["hid_done"], 1)

            experts(0, 1)
            squares(2)
            with act.Fori(0, NG // 2) as it:
                for par in range(2):
                    g = it * 2 + par
                    turned(2, par, g)
                    for r in range(2):
                        for q in (0, 2):
                            act.wait_ge(s["xw_done"], g * 8 + r * 4 + q + 1)
                            o = NB * GATE_AT[q]
                            act.copy(xw[:, r, :, o:o + NB].rearrange("p t (g b) -> p g b t", b=GB)[:, g],
                                     ps[2 + q % 2][:, 0:GT].rearrange("p (b t) -> p b t", b=GB)).then_inc(s["xw_act"], 1)

            def cell(r, bank, st):
                act.wait_ge(s[f"z{r}"], st + 1)
                act.activation(sig[:, r, :], bank[:, 0:3 * NB], ACT.Sigmoid)
                act.activation(tg[:, r, :], bank[:, 3 * NB:4 * NB], ACT.Tanh).then_inc(s[f"s{r}"], 1)

            def cell_out(r, st):
                act.wait_ge(s[f"c{r}"], st + 1)
                act.activation(tc_[:, r, :], cs[:, r, :], ACT.Tanh).then_inc(s[f"tc{r}"], 1)

            with act.Fori(0, T // 2) as it:
                for par in range(2):
                    st = it * 2 + par
                    for r in range(2):
                        cell(r, ps[2 * r + par], st)
                    for r in range(2):
                        cell_out(r, st)
            with act.Fori(0, T // 2) as it:
                for par in range(2):
                    st = it * 2 + par
                    cell(2, ps[par], st)
                    cell_out(2, st)
            experts(1, 3)

        @block.vector
        def _(dve):
            dve.sem_inc(s["om_out"], 1)
            dve.sem_inc(s["r_added"], 1)
            dve.sem_inc(s["logit_out"], 1)
            dve.sem_inc(s["added"], 2)
            dve.sem_inc(s["xw_dve"], 1)
            dve.sem_inc(s["dec_out"], 2)
            dve.memset(xg[D:D + 1], 1.0)
            dve.memset(xt[D:D + 1], 1.0)
            dve.memset(ones[:, :], 1.0)
            dve.memset(hs[:], 0.0)
            dve.memset(cs[:], 0.0).then_inc(s["setup_done"], 1)
            for r in range(3):
                dve.sem_inc(s[f"h{r}"], 1)
            dve.wait_ge(s["loaded"], 16 * N_LOADS)
            dve.wait_ge(s["we_turned"], 1)
            dve.tensor_copy(wet[:, :], ps[0][0:D, :]).then_inc(s["wet_done"], 1)

            def wide(v):
                return v.unsqueeze(2).broadcast_to([T, NB, D])

            def normalise(n):
                dve.reduce_sum(mean[:, :], x[:, :, :], AX.X).then_inc(s["sums"], 1)
                dve.wait_ge(s["sums"], n + 1)
                dve.tensor_scalar(mean[:, :], mean[:, :], 1.0 / D, None, ALU.mult).then_inc(s["meaned"], 1)
                dve.wait_ge(s["meaned"], n + 1)
                dve.tensor_tensor(xc_[:, :, :], x[:, :, :], wide(mean[:, :]), ALU.subtract).then_inc(s["centred"], 1)
                dve.wait_ge(s["squared"], n + 1)
                dve.reduce_sum(var[:, :], sq_[:, :, :], AX.X).then_inc(s["varied"], 1)
                dve.wait_ge(s["rstd"], n + 1)

            def scale(n, par, g):
                k = n * NG + g
                dve.wait_ge(s["turned_out"], k + 1)
                xb = xc_[:, bass.ts(g, GB), :]
                dve.tensor_tensor(norm[:, par, :, :], xb, rs[:, bass.ts(g, GB)].unsqueeze(2).broadcast_to([T, GB, D]), ALU.mult).then_inc(s["normed"], 1)

            normalise(0)
            with dve.Fori(0, NG // 2) as it:
                for par in range(2):
                    g = it * 2 + par
                    scale(0, par, g)
                    for b in range(GB):
                        k4 = g * GB + b
                        dve.wait_ge(s["om_done"], k4 + 1)
                        for hh in range(2):
                            mk = dve.tensor_tensor(om[:, b % 2, 4 * hh:4 * hh + 4, :], ps[4 + hh][0:T, 0:GT].rearrange("p (h t) -> p h t", h=4),
                                                   tri[:, :].unsqueeze(1).broadcast_to([T, 4, T]), ALU.mult)
                        mk.then_inc(s["om_out"], 1)
                    dve.wait_ge(s["r_done"], (g + 1) * GB)
                    xb = x[:, bass.ts(g, GB), :]
                    dve.tensor_tensor(xb, ps[6][0:T, 0:GB * D].rearrange("p (b d) -> p b d", b=GB), xb, ALU.add).then_inc(s["r_added"], 1)
            dve.wait_ge(s["r_added"], NG + 1)
            steps = [0]

            def step(ins):
                steps[0] += 1
                ins.then_inc(s["gate_step"], 1)
                dve.wait_ge(s["gate_step"], steps[0])

            def by_token(v):
                return v.unsqueeze(2).broadcast_to([T, NB, NE])

            def experts(i, n):
                normalise(n)
                with dve.Fori(0, NG // 2) as it:
                    for par in range(2):
                        g = it * 2 + par
                        scale(n, par, g)
                        dve.wait_ge(s["logit_done"], i * NG + g + 1)
                        dve.tensor_copy(logit[:, bass.ts(g, GB), :], ps[1][0:T, 0:GB * NE].rearrange("p (b e) -> p b e", b=GB)).then_inc(s["logit_out"], 1)
                dve.wait_ge(s["logit_out"], (i + 1) * NG + 1)
                step(dve.reduce_max(top[:, :], logit[:, :, :], AX.X))
                dve.tensor_tensor(gate[:, :, :], logit[:, :, :], by_token(top[:, :]), ALU.subtract).then_inc(s["exp_in"], 1)
                dve.wait_ge(s["exp_done"], i + 1)
                if i:
                    step(dve.reduce_sum(total[:, :], gate[:, :, :], AX.X))
                    step(dve.reciprocal(total[:, :], total[:, :]))
                    step(dve.tensor_tensor(gate[:, :, :], gate[:, :, :], by_token(total[:, :]), ALU.mult))
                key = gate if i else logit
                other = key[:, :, :].unsqueeze(2).broadcast_to([T, NB, NE, NE])
                own = key[:, :, :].unsqueeze(3).broadcast_to([T, NB, NE, NE])
                step(dve.tensor_tensor(above, other, own, ALU.is_gt))
                step(dve.tensor_tensor(equal, other, own, ALU.is_equal))
                step(dve.tensor_tensor(xc_[:, :, :], xc_[:, :, :], below[:, :, :].rearrange("p a b -> p (a b)").unsqueeze(1).broadcast_to([T, NB, 64]), ALU.mult))
                step(dve.tensor_tensor(sq_[:, :, :], sq_[:, :, :], xc_[:, :, :], ALU.add))
                step(dve.reduce_sum(picked[:, :, :], above, AX.X))
                step(dve.tensor_scalar(picked[:, :, :], picked[:, :, :], 1.5 - i, None, ALU.is_lt))
                step(dve.tensor_tensor(gate[:, :, :], gate[:, :, :], picked[:, :, :], ALU.mult))
                if i == 0:
                    step(dve.reduce_sum(total[:, :], gate[:, :, :], AX.X))
                    step(dve.reciprocal(total[:, :], total[:, :]))
                    step(dve.tensor_tensor(gate[:, :, :], gate[:, :, :], by_token(total[:, :]), ALU.mult))
                else:
                    dve.sem_inc(s["tri_in"], 1)
                    dve.wait_ge(s["tri_done"], 1)
                    flat = lambda v: v.rearrange("p b e -> p (b e)")
                    n_all = NB * NE
                    step(dve.memset(place[:, 0, 0:1, :], 0.0))
                    step(dve.tensor_copy(flat(place[:, 0, :, :])[:, NE:], ps[1][0:T, n_all:2 * n_all - NE]))
                    step_b, cur = 1, 0
                    while step_b < NB:
                        a, b = flat(place[:, cur, :, :]), flat(place[:, 1 - cur, :, :])
                        w = step_b * NE
                        step(dve.tensor_copy(b[:, 0:w], a[:, 0:w]))
                        step(dve.tensor_tensor(b[:, w:], a[:, w:], a[:, 0:n_all - w], ALU.add))
                        step_b, cur = 2 * step_b, 1 - cur
                    step(dve.tensor_tensor(flat(place[:, 1 - cur, :, :]), ps[1][0:T, 0:n_all], flat(place[:, cur, :, :]), ALU.add))
                    step(dve.tensor_scalar(place[:, cur, :, :], place[:, 1 - cur, :, :], CAP + 0.5, None, ALU.is_lt))
                    step(dve.tensor_tensor(gate[:, :, :], gate[:, :, :], place[:, cur, :, :], ALU.mult))
                with dve.Fori(0, NG // 2) as it:
                    for par in range(2):
                        g = it * 2 + par
                        for b in range(GB):
                            k4 = (i * NG + g) * GB + b
                            r = b % 2
                            eye = lambda v: v.rearrange("p (e d) -> p e d", e=NE)
                            dve.wait_ge(s["down_done"], k4 + 1)
                            dve.tensor_tensor(mixed[:, r, :], ps[4 + r][0:T, :], b2[i][:, :, :].rearrange("p e d -> p (e d)"), ALU.add).then_inc(s["added"], 1)
                            dve.wait_ge(s["added"], k4 + 3)
                            w = gate[:, bass.ds(g * GB + b, 1), :].rearrange("p a e -> p (a e)").unsqueeze(2).broadcast_to([T, NE, D])
                            dve.tensor_tensor(eye(weighed[:, r, :]), eye(mixed[:, r, :]), w, ALU.mult).then_inc(s["weighted"], 1)
                            dve.wait_ge(s["weighted"], k4 + 1)
                            to = y_all[:, bass.ds(g * GB + b, 1), :].rearrange("p a d -> p (a d)") if i else y[:, par, D * b:D * b + D]
                            dve.reduce_sum(to, weighed[:, r, :].rearrange("p (e d) -> p d e", e=NE), AX.X).then_inc(s["summed"], 1)
                        dve.wait_ge(s["summed"], (i * NG + g) * GB + GB)
                        if i == 0:
                            xb = x[:, bass.ts(g, GB), :]
                            dve.tensor_tensor(xb, xb, y[:, par, :].rearrange("p (b d) -> p b d", b=GB), ALU.add).then_inc(s["y_added"], 1)
                if i == 0:
                    dve.wait_ge(s["y_added"], NG)

            experts(0, 1)
            normalise(2)
            with dve.Fori(0, NG // 2) as it:
                for par in range(2):
                    g = it * 2 + par
                    scale(2, par, g)
                    for r in range(2):
                        for q in (1, 3):
                            dve.wait_ge(s["xw_done"], g * 8 + r * 4 + q + 1)
                            o = NB * GATE_AT[q]
                            dve.tensor_copy(xw[:, r, :, o:o + NB].rearrange("p t (g b) -> p g b t", b=GB)[:, g],
                                            ps[2 + q % 2][:, 0:GT].rearrange("p (b t) -> p b t", b=GB)).then_inc(s["xw_dve"], 1)

            def cell(r, st):
                dve.wait_ge(s[f"s{r}"], st + 1)
                dve.tensor_tensor(fc_[:, r, :], sig[:, r, NB:2 * NB], cs[:, r, :], ALU.mult)
                dve.tensor_tensor(ig[:, r, :], sig[:, r, 0:NB], tg[:, r, :], ALU.mult).then_inc(s[f"ig{r}"], 1)
                dve.wait_ge(s[f"ig{r}"], st + 1)
                dve.tensor_tensor(cs[:, r, :], fc_[:, r, :], ig[:, r, :], ALU.add).then_inc(s[f"c{r}"], 1)

            def cell_out(r, st, dst):
                dve.wait_ge(s[f"tc{r}"], st + 1)
                dve.tensor_tensor(dst, sig[:, r, 2 * NB:3 * NB], tc_[:, r, :], ALU.mult).then_inc(s[f"h{r}"], 1)

            with dve.Fori(0, T // 2) as it:
                for par in range(2):
                    st = it * 2 + par
                    for r in range(2):
                        cell(r, st)
                    for r in range(2):
                        cell_out(r, st, hs[:, r, 1 - par, :])
            dve.wait_ge(s["zc_done"], 1)
            dve.memset(hd[:, 0, :], 0.0)
            dve.memset(cs[:, 2, :], 0.0)
            dve.tensor_copy(zc[:, :], ps[4][:, 0:P]).then_inc(s["zc_out"], 1)
            with dve.Fori(0, T // 2) as it:
                for par in range(2):
                    st = it * 2 + par
                    cell(2, st)
                    cell_out(2, st, hd[:, bass.ds(st + 1, 1), :].rearrange("p a b -> p (a b)"))
            for b8 in range(QUARTERS):
                xb = x[:, 8 * b8:8 * b8 + 8, :]
                step(dve.tensor_tensor(xb, xb, bo[:, :].unsqueeze(1).broadcast_to([T, 8, D]), ALU.add))
                dve.wait_ge(s["dec_done"], b8 + 1)
                dve.tensor_tensor(xb, ps[2 + b8 % 2][0:T, :].rearrange("p (b d) -> p b d", b=8), xb, ALU.add).then_inc(s["dec_out"], 1)
            dve.wait_ge(s["dec_out"], 6)
            experts(1, 3)
            for m, v in enumerate((0.0, 1e4, -1e4)):
                fill = dve.memset(fills[:, m, :], v)
            step(fill)
            for v in range(QUARTERS):
                yq, xq = (a[:, 8 * v:8 * v + 8, :].rearrange("p b d -> p (b d)") for a in (y_all, x))
                for m, (border, op) in enumerate(((None, ALU.not_equal), (FLT_MAX, ALU.is_gt), (-FLT_MAX, ALU.is_lt))):
                    o_ = odd[:, m % 2, :]
                    if border is None:
                        step(dve.tensor_tensor(o_, yq, yq, op))
                    else:
                        step(dve.tensor_scalar(o_, yq, border, None, op))
                    step(dve.copy_predicated(yq, o_, fills[:, m, :]))
                dve.tensor_tensor(xq, xq, yq, ALU.add).then_inc(s["y_added"], 1)


def build(nc, d, out):
    img = nc.dram_tensor("img_tokens", [NB, HH, WW], F32).ap()
    with ExitStack() as sems:
        build_fno(nc, sems, d, img)
        build_tail(nc, sems, d, img, out)


def kernel(**inputs):
    import concourse.bacc as bacc
    from concourse.bass_utils import run_bass_kernel_spmd

    nc = bacc.Bacc("TRN2", target_bir_lowering=False, num_devices=1)
    arrays = {name: np.ascontiguousarray(a) for name, a in inputs.items()}
    arrays.update(fno_constants())
    arrays.update(tail_constants())
    d = {name: nc.dram_tensor(name, a.shape, mybir.dt.from_np(a.dtype), kind="ExternalInput").ap() for name, a in arrays.items()}
    out = nc.dram_tensor("out", [NB, T, D], F32, kind="ExternalOutput").ap()
    build(nc, d, out)
    return run_bass_kernel_spmd(nc, [arrays], core_ids=[0]).results[0]["out"]
```

```python
from contextlib import ExitStack

import numpy as np
import concourse.bass as bass
from concourse import mybir

F32 = mybir.dt.float32
U32 = mybir.dt.uint32
ALU = mybir.AluOpType
ACT = mybir.ActivationFunctionType
AX = mybir.AxisListType

B, HH, WW, CI, CH, LAYERS, MX, MY = 32, 64, 64, 3, 32, 4, 12, 12
P = 128
BG = B // 4
CHUNKS = 8
CW = 512
KYR = 2 * MY
MODES = MX * MY
ROWS4 = 4
EPS = 1e-5
I1_GROUPS, G2_GROUPS = 3, 4
FRONT = I1_GROUPS + G2_GROUPS
AT_GROUPS, F2_GROUPS = 3, 2
BACK = AT_GROUPS + F2_GROUPS
HALF = MY // 2
LAG = 3
FRONT_SLOTS = (0, 1, 2, 4, 5, 6, 7)
AT_SLOT, F2_SLOTS = 3, (5, 6)

NB, T, D = 32, 96, 64
TI = 64
NG, GB = 8, 4
GT = GB * T
HEADS = 8
NE, FF = 8, 256
HID, GATES = 128, 4
CAP = -(-5 * NB * T // (4 * NE))
START_FILLS = 4
ENCODER_FILL, DECODER_FILL = 128, 512
QUARTERS = 4
NORM_PARTS = [(0, GB), (GB, NB - GB)] + 2 * [(GB * g, GB) for g in range(NG)] + [(8 * v, 8) for v in range(QUARTERS)]
NORM_AT = (0, 2, 2 + NG, 2 + 2 * NG)
FLT_MAX = float(np.finfo(np.float32).max)


def fno_constants():
    w = np.arange(WW)
    ang = lambda k, x: 2 * np.pi * k * x / 64.0
    f1 = np.zeros((2, WW, 64))
    for r in range(2):
        for ky in range(MY):
            f1[r, :, r * KYR + 2 * ky] = np.cos(ang(ky, w))
            f1[r, :, r * KYR + 2 * ky + 1] = -np.sin(ang(ky, w))
    f2 = np.zeros((2, HH, 64))
    i1 = np.zeros((P, 2, HH))
    h = np.arange(HH)
    for half in range(2):
        for kx in range(MX):
            f = kx + (HH - MX) * half
            c, s = np.cos(ang(f, h)), np.sin(ang(f, h))
            re, im = half * 24 + kx, half * 24 + 12 + kx
            f2[0, :, re], f2[1, :, re] = c, s
            f2[0, :, im], f2[1, :, im] = -s, c
            row = kx * 4 + half * 2
            i1[row, 0], i1[row, 1] = c / HH, s / HH
            i1[row + 1, 0], i1[row + 1, 1] = -s / HH, c / HH
    i2 = np.zeros((97, 2, 2, WW))
    for r4 in range(4):
        for ky in range(MY):
            a = (1.0 if ky == 0 else 2.0) / WW
            i2[r4 * KYR + 2 * ky, r4 // 2, r4 % 2] = a * np.cos(ang(ky, w))
            i2[r4 * KYR + 2 * ky + 1, r4 // 2, r4 % 2] = -a * np.sin(ang(ky, w))
    i2[96] = 1.0
    f = np.float32
    sign = np.ones((P, 1), f)
    sign[32:64] = sign[96:128] = -1
    return dict(k_f1=f1.reshape(P, 64).astype(f), k_f2=f2.reshape(P, 64).astype(f),
                k_i1=i1.reshape(P, P).astype(f), k_i2=i2.reshape(97, 256).astype(f),
                k_id=np.eye(P, dtype=f), k_sign=sign)


def build_fno(nc, sems, d, img):
    xs = nc.dram_tensor("x_planes", [B, CI, HH * WW], F32).ap()
    yd = nc.dram_tensor("y_modes", [ROWS4, CH, B, MODES], F32).ap()
    zd = nc.dram_tensor("z_modes", [B, MX, ROWS4 * CH * MY], F32).ap()
    with ExitStack() as ctx:
        sb = lambda n, s: ctx.enter_context(nc.sbuf_tensor(n, s, F32))
        sem = lambda n: sems.enter_context(nc.semaphore(n))
        act_all = sb("act_all", [P, BG * CHUNKS, CW])
        w_raw = sb("w_raw", [P, CH * MODES])
        share = sb("share", [P, 3 * 1536])
        y_in = share[:, :].rearrange("p (b m) -> p b m", b=B)
        g_buf = share[:, 0:1536]
        a_buf = share[:, 1536:3072]
        at = share[:, 3072:4608]
        in_g_buf, in_a_buf = 1536 // MODES, 3072 // MODES // 4 * 4
        before = sb("before", [P, 2 * 2048])
        g2 = before[0:97, 0:2048].rearrange("p (a n) -> p a n", a=16)
        zpp = before[:, 2048:3584]
        z_row = before[0:B, 0:2 * ROWS4 * CH * MY].rearrange("p (r n) -> p r n", r=2)
        xc = before[:, :].rearrange("p (r n) -> p r n", r=2)
        y_st = sb("y_st", [P, ROWS4 * MODES])
        work = sb("work", [P, 3 * CW + 16])
        t = work[:, 0:2 * CW].rearrange("p (r n) -> p r n", r=2)
        sq = work[:, 2 * CW:].rearrange("p (a c) -> p a c", c=CH + 1)
        ht = sb("ht", [P, 2, CW])
        hin = sb("hin", [P, 2, CW])
        blk = lambda a: a.rearrange("p (m n) -> p m n", m=HALF)
        w2 = [[blk(work[:, 0:HALF * P]), blk(work[:, HALF * P:2 * HALF * P])],
              [blk(ht[:, :, :].rearrange("p r n -> p (r n)")[:, 0:HALF * P]), blk(hin[:, :, :].rearrange("p r n -> p (r n)")[:, 0:HALF * P])]]
        y_row = sb("y_row", [P, 2, MY * B])
        w_mean = sb("w_mean", [P, MODES])[:, :]
        vs = sb("vs", [P, 4, 16])
        rstd = sb("rstd", [P, 4, 16])
        nhalf = sb("nhalf", [P, 16])
        table = sb("table_f", [1, 1])
        f1, f2, ident = sb("f1", [P, 64]), sb("f2", [P, 64]), sb("ident", [P, P])
        i1, i2, sign = sb("i1", [P, P]), sb("i2", [97, 2 * P]), sb("sign", [P, 1])
        w0 = sb("w0", [P, P])
        w0m = sb("w0m", [P, 4])
        wc = sb("wc", [P, LAYERS, P])
        cwn = act_all[:, 12, 0:CH]
        cwt = act_all[0:CH, 13, 0:LAYERS * CH].rearrange("p (l c) -> p l c", l=LAYERS)
        cwm = act_all[0:CH, 14, 0:LAYERS]
        cb = sb("cb", [97, LAYERS, CH])
        cbm = sb("cbm", [97, LAYERS])
        lng, lnb = sb("lng", [P, LAYERS + 1, CH]), sb("lnb", [P, LAYERS + 1, CH])
        fc1 = y_st[:, 0:512].rearrange("p (b f) -> p b f", b=4)
        fc2 = y_st[:, 512:576]
        fc3 = sb("fc3", [P, 64])
        fb = sb("fb", [P, 3])
        g1 = w_raw[:, 0:2 * CW].rearrange("p (r n) -> p r n", r=2)
        g2l = w_raw[:, 2 * CW:4 * CW].rearrange("p (r n) -> p r n", r=2)
        hc = w_raw[:, 6 * CW:8 * CW].rearrange("p (r n) -> p r n", r=2)
        o1 = w_raw[:, 4 * CW:4 * CW + P]
        o2 = w_raw[:, 5 * CW:5 * CW + P]
        xraw = act_all[:, 0:6, :].rearrange("p a n -> p (a n)")
        xpl = act_all[:, 6:12, :].rearrange("p a n -> p (a n)")
        ps = [ctx.enter_context(nc.psum_tensor(f"ps{i}", [P, CW], F32)) for i in range(8)]
        pt, pf, pg, pb = ps[2], ps[4], ps[5], ps[6]
        pz = [ps[0], ps[1], ps[3], ps[7]]
        pm = [[ps[0], ps[1], ps[3]], [ps[7], ps[2], ps[4]]]
        pc, px = ps[3], ps[7]

        names = """consts_in filled zeroed params_in x_in x_split x_stored xc0_in xc1_in w0_ready wc_raw wc_t prep
            z_done hin_ready squared var_sum nhalf_set rstd_ready t_scaled t_gained t_ready gelu_done tr_done hc_ready
            f1_done a_written zpp_in fr_done fr_evac bk_done bk_evac y_stored
            w_in w_meaned w_scaled w_centred y_in w2_clear guard_set w2_dve w2_act mix_half y_row_in zrow_ready z_stored0 z_stored1
            bias_set fc_clear fc_in fc1_done g1_ready fc2_done g2_ready fc3_done o1_ready o_tr o2_ready img_stored""".split()
        s = {n: sem(n) for n in names}
        xc_in, z_stored = [s["xc0_in"], s["xc1_in"]], [s["z_stored0"], s["z_stored1"]]
        N_CONST = 6
        block = ctx.enter_context(nc.Block())

        @block.sync
        def _(sp):
            for dst, name in ((f1, "k_f1"), (f2, "k_f2"), (ident, "k_id"), (i1, "k_i1"), (i2, "k_i2"), (sign, "k_sign")):
                sp.dma_start(dst[:, :], d[name]).then_inc(s["consts_in"], 16)
            xv = d["x"].rearrange("(i b) h w c -> (b h) i (w c)", b=2)
            sp.dma_start(xraw.rearrange("p (i n) -> p i n", i=16), xv).then_inc(s["x_in"], 16)
            sp.wait_ge(s["x_split"], 1)
            for b in range(2):
                for c in range(CI):
                    sp.dma_start(xs.rearrange("(i b) c (h w) -> b c h i w", b=2, w=WW)[b, c],
                                 xpl.rearrange("p (i c w) -> p i c w", i=16, c=CI)[64 * b:64 * b + 64, :, c, :]).then_inc(s["x_stored"], 16)
            sp.wait_ge(s["x_stored"], 16 * 6)

            def load_xc(g, part):
                src = xs.rearrange("(g b) c n -> g (b c) n", b=4)[g]
                sp.dma_start(xc[0:12, part, :], src[:, part * 2048:part * 2048 + 2048]).then_inc(xc_in[part], 16)

            def load_w(l):
                for q, name in enumerate(("w1r", "w1i", "w2r", "w2i")):
                    src = d["L0_tok_" + name].rearrange("l i o x y -> l i (o x y)")
                    sp.dma_start(w_raw[32 * q:32 * q + 32, :], src[l]).then_inc(s["w_in"], 16)

            def store_y(n, g):
                sp.wait_ge(s["bk_evac"], BACK * n + BACK + 1)
                dst = yd.rearrange("q c (g b) m -> g b c q m", b=4)[g]
                for b in range(4):
                    sp.dma_start(dst[b], y_st[32 * b:32 * b + 32, :].rearrange("p (q m) -> p q m", q=ROWS4)).then_inc(s["y_stored"], 16)

            def load_zpp(u, g):
                sp.dma_start(zpp[0:MX * ROWS4].rearrange("p (b n) -> p b n", b=4),
                             zd.rearrange("(g b) x (q n) -> g (x q) b n", b=4, q=ROWS4)[g]).then_inc(s["zpp_in"], 16)

            def load_y(l, b0, b1):
                sp.wait_ge(s["y_stored"], 64 * (BG * l + -(-b1 // 4)) + 1)
                sp.dma_start(y_in[:, b0:b1, :], yd.rearrange("q c b m -> (q c) b m")[:, b0:b1]).then_inc(s["y_in"], 16)

            def last_stores(l):
                n = BG * l + BG - 1
                sp.wait_ge(s["fr_done"], l * BG * FRONT + 5)
                load_y(l, 0, in_g_buf)
                store_y(n - 1, BG - 2)
                sp.wait_ge(s["bk_done"], n * BACK + AT_GROUPS)
                load_y(l, in_g_buf, in_a_buf)
                store_y(n, BG - 1)

            def mix(l):
                load_y(l, in_a_buf, B)
                with sp.Fori(0, MX // 2) as it:
                    for half in range(2):
                        row = l * MX + it * 2 + half
                        sp.wait_ge(s["zrow_ready"], row + 3)
                        sp.dma_start(zd.rearrange("b x n -> x b n")[it * 2 + half], z_row[:, half, :]).then_inc(z_stored[half], 16)
                for half in range(2):
                    sp.wait_ge(z_stored[half], 96 * (l + 1) + 16)

            def next_xc(g, part):
                sp.wait_ge(s["z_done"], g * CHUNKS + 4 * part + 4)
                load_xc(g + 1, part)

            sp.wait_ge(s["filled"], 2)
            for part in range(2):
                load_xc(0, part)
            load_w(0)
            for part in range(2):
                next_xc(0, part)
            with sp.Fori(1, BG - 1) as g:
                next_xc(g, 0)
                store_y(g - 1, g - 1)
                next_xc(g, 1)
            last_stores(0)

            def next_zpp(u, g):
                sp.wait_ge(s["fr_done"], (u - 1) * FRONT + I1_GROUPS + 5)
                load_zpp(u, g)

            with sp.Fori(0, LAYERS - 1) as l:
                mix(l)
                sp.wait_ge(s["mix_half"], 2 * MX * (l + 1) + 4)
                load_zpp(l * BG, 0)
                next_zpp(l * BG + 1, 1)
                load_w(l + 1)
                next_zpp(l * BG + 2, 2)
                with sp.Fori(0, BG - 3) as g:
                    next_zpp(l * BG + g + 3, g + 3)
                    store_y(BG + l * BG + g, g)
                store_y(BG + l * BG + BG - 3, BG - 3)
                last_stores(l + 1)
            mix(LAYERS - 1)
            last = (LAYERS - 1) * BG
            load_zpp(last, 0)
            sp.wait_ge(s["fc_clear"], 1)
            for b in range(4):
                sp.dma_start(fc1[32 * b:32 * b + 32, b, :], d["L0_tok_fc1_w"]).then_inc(s["fc_in"], 16)
            sp.dma_start(fc2, d["L0_tok_fc2_w"]).then_inc(s["fc_in"], 16)

            def store_img(g):
                sp.wait_ge(s["o2_ready"], g + 2)
                sp.dma_start(img.rearrange("(g b) (j r) w -> g (b j) (r w)", b=4, r=2)[g], o2).then_inc(s["img_stored"], 16)

            next_zpp(last + 1, 1)
            next_zpp(last + 2, 2)
            with sp.Fori(0, BG - 3) as g:
                next_zpp(last + g + 3, g + 3)
                store_img(g)
            for g in range(BG - 3, BG):
                store_img(g)
            sp.wait_ge(s["img_stored"], 16 * BG + 16)

        @block.gpsimd
        def _(pool):
            pool.memset(nhalf[:, :], -0.5).then_inc(s["nhalf_set"], 1)
            pool.wait_ge(s["nhalf_set"], 1)

            def unit(n):
                for k in range(CHUNKS):
                    q = n * CHUNKS + k
                    pool.wait_ge(s["var_sum"], q + 2)
                    pool.tensor_tensor(rstd[:, k % 4, :], vs[:, k % 4, :], nhalf[:, :], ALU.pow).then_inc(s["rstd_ready"], 1)
            def mix(l):
                yv = y_in.rearrange("p b m -> p m b")
                with pool.Fori(0, MX // 2) as it:
                    for r in range(2):
                        pool.wait_ge(s["y_in"], 48 * (l + 1))
                        pool.wait_ge(s["mix_half"], (l * MX + it * 2 + r) * 2 + 2)
                        pool.tensor_copy(y_row[:, r, :].rearrange("p (y b) -> p y b", b=B),
                                         yv[:, bass.ds(it * 2 * MY + r * MY, MY), :]).then_inc(s["y_row_in"], 1)

            with pool.Fori(0, BG) as n:
                unit(n)
            with pool.Fori(0, LAYERS - 1) as l:
                mix(l)
                with pool.Fori(0, BG) as g:
                    unit(BG + l * BG + g)
            pool.wait_ge(s["y_stored"], 64 * LAYERS * BG + 1)
            pool.memset(fc1, 0.0).then_inc(s["fc_clear"], 1)
            mix(LAYERS - 1)
            with pool.Fori(LAYERS * BG, (LAYERS + 1) * BG) as n:
                unit(n)

        @block.tensor
        def _(pe):
            pe.wait_ge(s["consts_in"], 16 * N_CONST)
            pe.wait_ge(s["wc_raw"], 1)
            pe.transpose(pz[0][0:CH, 0:P], cwn, ident[:, :]).then_inc(s["wc_t"], 1)
            pe.wait_ge(s["prep"], 1)

            def z_first(g, q, k):
                part = k // 4
                if k % 4 == 0:
                    pe.wait_ge(xc_in[part], 16 * (g + 1))
                pe.wait_ge(s["t_scaled"], q + 1)
                for j in range(4):
                    mm = pe.matmul(pz[k % 4][:, P * j:P * j + P], xc[:, part, (k % 4) * CW + P * j:(k % 4) * CW + P * j + P],
                                   w0[:, :], start=True, stop=True)
                mm.then_inc(s["z_done"], 1)

            def z_mid(u, q, k, l, banks=4):
                pe.wait_ge(s["fr_evac"], u * FRONT + I1_GROUPS + k // 2 + 2)
                pe.wait_ge(s["hin_ready"], q - BG * CHUNKS + 1)
                pe.wait_ge(s["t_scaled"], q + 5 - banks)
                for j in range(4):
                    z = pz[k % banks][:, P * j:P * j + P]
                    pe.matmul(z, i2[:, (j % 2) * P:(j % 2) * P + P], g2[:, 2 * k + j // 2, :], start=True, stop=False)
                    mm = pe.matmul(z, hin[:, k % 2, P * j:P * j + P], wc[:, l - 1, :], start=False, stop=True)
                mm.then_inc(s["z_done"], 1)

            def front(u, i, two=False):
                if i == 0:
                    pe.wait_ge(s["zpp_in"], 16 * (u + 1))
                bank = (pg, pb)[i % 2] if two else pg
                pe.wait_ge(s["fr_evac"], u * FRONT + i + 1 - (two and i not in (0, I1_GROUPS)))
                for j in range(4):
                    if i < I1_GROUPS:
                        ky = 4 * i + j
                        mm = pe.matmul(bank[:, P * j:P * j + P], zpp[:, ky::MY], i1[:, :], start=True, stop=True)
                    else:
                        hb = 4 * (i - I1_GROUPS) + j
                        mm = pe.transpose(bank[0:96, P * j:P * j + P], g_buf[:, 96 * hb:96 * hb + 96], ident[:, :])
                mm.then_inc(s["fr_done"], 1)

            def turn(q, k):
                pe.wait_ge(s["gelu_done"], q + 3)
                pe.wait_ge(s["hc_ready"], q + 1)
                for j in range(4):
                    mm = pe.transpose(pt[:, P * j:P * j + P], ht[:, k % 2, P * j:P * j + P], ident[:, :])
                mm.then_inc(s["tr_done"], 1)

            def along_w(q, k):
                pe.wait_ge(s["a_written"], q + 1)
                for j in range(4):
                    mm = pe.matmul(pf[:, 64 * j:64 * j + 64], ht[:, k % 2, P * j:P * j + P], f1[:, :], start=True, stop=True)
                mm.then_inc(s["f1_done"], 1)

            def back(n, i):
                if i == 0:
                    pe.wait_ge(s["a_written"], (n + 1) * CHUNKS + 1)
                pe.wait_ge(s["bk_evac"], n * BACK + i + 1 - (i == 1))
                for j in range(4 if i < AT_GROUPS else 6):
                    if i < AT_GROUPS:
                        c = P * (4 * i + j)
                        mm = pe.transpose((pg if i == 1 else pb)[:, P * j:P * j + P], a_buf[:, c:c + P], ident[:, :])
                    else:
                        c = P * (6 * (i - AT_GROUPS) + j)
                        mm = pe.matmul(pb[:, 64 * j:64 * j + 64], at[:, c:c + P], f2[:, :], start=True, stop=True)
                mm.then_inc(s["bk_done"], 1)

            def slots(n, g, l, z, ahead, behind, ks=range(CHUNKS)):
                q0 = n * CHUNKS
                for k in ks:
                    if z == "first":
                        z_first(g, q0 + k, k)
                    if z == "mid":
                        z_mid(n - BG, q0 + k, k, l)
                    if k == AT_SLOT and behind:
                        back(n - 1, 0)
                        if z == "mid":
                            pe.wait_ge(s["fr_evac"], (n - BG + 1) * FRONT + (I1_GROUPS if ahead else 0) + 1)
                        back(n - 1, 1)
                    if behind or k >= LAG:
                        turn(q0 + k - LAG, (k - LAG) % CHUNKS)
                    if k == AT_SLOT and behind:
                        back(n - 1, 2)
                    if behind or k >= LAG:
                        along_w(q0 + k - LAG, (k - LAG) % CHUNKS)
                    if behind and k in F2_SLOTS:
                        back(n - 1, AT_GROUPS + F2_SLOTS.index(k))
                    if ahead and k in FRONT_SLOTS:
                        if behind and k == AT_SLOT + 1:
                            pe.wait_ge(s["bk_evac"], (n - 1) * BACK + 3)
                        front(n - BG + 1, FRONT_SLOTS.index(k))

            def stage(n0, l, first=False):
                z = "first" if first else "mid"
                if not first:
                    pe.wait_ge(s["bias_set"], l)
                    for i in range(FRONT):
                        front(n0 - BG, i, True)
                slots(n0, 0, l, z, not first, False)
                with pe.Fori(1, BG - 1) as g:
                    slots(n0 + g, g, l, z, not first, True)
                slots(n0 + BG - 1, BG - 1, l, z, False, True)
                slots(n0 + BG, 0, l, None, False, True, range(LAG))
                for i in range(BACK):
                    back(n0 + BG - 1, i)

            def mix(l):
                with pe.Fori(0, MX // 2) as it:
                    for r in range(2):
                        row = l * MX + it * 2 + r
                        pe.wait_ge(s["zrow_ready"], row + 1)
                        pe.wait_ge(s["y_row_in"], row + 1)
                        for hf in range(2):
                            hq = l * 2 * MX + it * 4 + 2 * r + hf
                            pe.wait_ge(s["w2_dve"], hq + 1)
                            pe.wait_ge(s["w2_act"], hq + 1)
                            for m in range(HALF):
                                y = hf * HALF + m
                                mm = pe.matmul(pm[r][y // 4][0:B, P * (y % 4):P * (y % 4) + P], y_row[:, r, B * y:B * y + B],
                                               w2[r][hf][:, m, :], start=True, stop=True)
                            mm.then_inc(s["mix_half"], 1)

            stage(0, 0, True)
            with pe.Fori(0, LAYERS - 1) as l:
                mix(l)
                stage(BG + l * BG, l + 1)
            mix(LAYERS - 1)
            pe.wait_ge(s["fc_in"], 16 * 5)

            def dense(q, k, c, behind):
                pe.wait_ge(s["hc_ready"], q + 2)
                for b in range(4):
                    pe.wait_ge(s["g1_ready"], 4 * c + b + 1)
                    bank = (pc, pf)[b % 2]
                    pe.matmul(bank[:, :], fc1[:, b, :], hc[:, k % 2, :], start=True, stop=True).then_inc(s["fc1_done"], 1)
                    if b == 1 and behind:
                        third(c - 1)
                    if b >= 1:
                        second(c, b - 1)

            def second(c, b):
                pe.wait_ge(s["g1_ready"], 4 * c + b + 3)
                if b % 2 == 0:
                    pe.wait_ge(s["g2_ready"], 2 * c + b // 2 + 1)
                mm = pe.matmul(px[64 * (b % 2):64 * (b % 2) + 64, :], fc2, g1[:, b % 2, :], start=True, stop=True)
                mm.then_inc(s["fc2_done"], 1)

            def third(c):
                pe.wait_ge(s["o1_ready"], c + 1)
                for pair in range(2):
                    pe.wait_ge(s["g2_ready"], 2 * c + pair + 2)
                    for j in range(4):
                        o = 256 * pair + 64 * j
                        mm = pe.matmul(pb[:, o:o + 64], g2l[:, pair, P * j:P * j + P], fc3[:, :], start=True, stop=True)
                mm.then_inc(s["fc3_done"], 1)

            def turn_out(g):
                pe.wait_ge(s["o1_ready"], (g + 1) * CHUNKS + 1)
                pe.wait_ge(s["o2_ready"], g + 1)
                pe.transpose(pg[:, 0:P], o1, ident[:, :]).then_inc(s["o_tr"], 1)

            def last_slots(g, z, ahead, behind, ks=range(CHUNKS)):
                n = LAYERS * BG + g
                q0 = n * CHUNKS
                for k in ks:
                    if (k >= 2 or behind) and (z or k < 2):
                        turn(q0 + k - 2, k)
                    if z:
                        z_mid(n - BG, q0 + k, k, LAYERS, 2)
                    if k >= 3 or behind:
                        second(g * CHUNKS + k - 3, 3)
                    if ahead and k in FRONT_SLOTS:
                        if behind and k == AT_SLOT + 1:
                            pe.wait_ge(s["o2_ready"], g + 1)
                        front(n - BG + 1, FRONT_SLOTS.index(k))
                    if behind and k == AT_SLOT:
                        if z:
                            pe.wait_ge(s["fr_evac"], (n - BG + 1) * FRONT + (I1_GROUPS if ahead else 0) + 1)
                        turn_out(g - 1)
                    if (k >= 2 or behind) and (z or k < 2):
                        dense(q0 + k - 2, k % 2, g * CHUNKS + k - 2, k >= 3 or behind)
                    if not z and k == 2:
                        third(g * CHUNKS + k - 3)

            pe.wait_ge(s["bias_set"], LAYERS)
            for i in range(FRONT):
                front((LAYERS - 1) * BG, i, True)
            last_slots(0, True, True, False)
            with pe.Fori(1, BG - 1) as g:
                last_slots(g, True, True, True)
            last_slots(BG - 1, True, False, True)
            last_slots(BG, False, False, True, range(3))
            turn_out(BG - 1)

        @block.scalar
        def _(act):
            act.sem_inc(s["hc_ready"], 1)
            act.sem_inc(s["fr_evac"], 1)
            act.sem_inc(s["gelu_done"], 2)
            act.dma_start(cwn, d["L0_tok_conv_w"].rearrange("l o c -> (l o) c")).then_inc(s["params_in"], 16)
            act.dma_start(cb[96:97, :, :], d["L0_tok_conv_b"].rearrange("(a l) c -> a l c", a=1)).then_inc(s["params_in"], 16)
            act.wait_ge(s["zeroed"], 1)
            for b in range(4):
                act.dma_start(w0[3 * b:3 * b + 3, 32 * b:32 * b + 32], d["L0_tok_fc0_w"]).then_inc(s["params_in"], 16)
                act.dma_start(w0[32:33, 32 * b:32 * b + 32], d["L0_tok_fc0_b"].rearrange("(a c) -> a c", a=1)).then_inc(s["params_in"], 16)
            for b in range(2):
                with nc.allow_non_contiguous_dma(reason="a column of 64 weights"):
                    act.dma_start(fc3[64 * b:64 * b + 64, b:b + 1], d["L0_tok_fc3_w"]).then_inc(s["params_in"], 16)
                    act.dma_start(fb[64 * b:64 * b + 64, 1:2], d["L0_tok_fc2_b"].rearrange("(c a) -> c a", a=1)).then_inc(s["params_in"], 16)
            with nc.allow_non_contiguous_dma(reason="a column of biases"):
                act.dma_start(fb[:, 0:1], d["L0_tok_fc1_b"].rearrange("(c a) -> c a", a=1)).then_inc(s["params_in"], 16)
                act.dma_start(fb[:, 2:3], d["L0_tok_fc3_b"].rearrange("(a c) -> a c", a=1).broadcast_to([P, 1])).then_inc(s["params_in"], 16)
            for dst, first, rest in ((lng, "L0_tok_ln0_g", "L0_tok_ln_g"), (lnb, "L0_tok_ln0_b", "L0_tok_ln_b")):
                act.dma_start(dst[:, 0, :], d[first].rearrange("(a c) -> a c", a=1).broadcast_to([P, CH])).then_inc(s["params_in"], 16)
                act.dma_start(dst[:, 1:, :].rearrange("p l c -> p (l c)"),
                             d[rest].rearrange("(a l) c -> a (l c)", a=1).broadcast_to([P, LAYERS * CH])).then_inc(s["params_in"], 16)
            act.wait_ge(s["nhalf_set"], 1)
            act.activation(table[:, :], nhalf[0:1, 0:1], ACT.Gelu)

            def square(q, k, banks=4):
                act.wait_ge(s["z_done"], q + 1)
                act.wait_ge(s["var_sum"], q + 1)
                act.activation(sq[:, :, 0:CH], pz[k % banks][:, :].rearrange("p (a c) -> p a c", c=CH), ACT.Square, scale=CH ** -0.5).then_inc(s["squared"], 1)

            def gelu(q, k, first):
                act.wait_ge(s["t_ready"], q + 1)
                act.wait_ge(s["f1_done"], q + 1)
                act.activation(ht[:, k % 2, :], t[:, k % 2, :], ACT.Copy if first else ACT.Gelu).then_inc(s["gelu_done"], 1)

            def keep(c):
                act.copy(act_all[:, c, :], pt[:, :]).then_inc(s["hc_ready"], 1)

            def a_evac(q, k):
                act.wait_ge(s["f1_done"], q + 3)
                src = pf[:, 0:256].rearrange("p (j x) -> p j x", j=4)[:, :, 0:48].rearrange("p j (h r) -> p r j h", h=2)
                dst = a_buf.rearrange("p (r j h) -> p r j h", r=KYR, h=2)[:, :, 4 * k:4 * k + 4, :]
                act.copy(dst, src).then_inc(s["a_written"], 1)

            def fetch(q, c, k, mixings=None):
                if mixings is None:
                    act.wait_ge(s["z_done"], q - 1)
                else:
                    act.wait_ge(s["mix_half"], mixings * 2 * MX + 4)
                act.wait_ge(s["hc_ready"], q - BG * CHUNKS + 2)
                act.copy(hin[:, k % 2, :], act_all[:, c, :]).then_inc(s["hin_ready"], 1)

            def front(u, i, two=False):
                bank = (pg, pb)[i % 2] if two else pg
                act.wait_ge(s["fr_done"], u * FRONT + i + 6)
                if i < I1_GROUPS:
                    dst = g_buf.rearrange("p (h r) -> p r h", r=KYR)[:, 8 * i:8 * i + 8, :]
                    act.copy(dst, bank[:, :].rearrange("p (r h) -> p r h", r=8)).then_inc(s["fr_evac"], 1)
                else:
                    o = 4 * (i - I1_GROUPS)
                    act.copy(g2[0:96, o:o + 4, :], bank[0:96, :].rearrange("p (j n) -> p j n", j=4)).then_inc(s["fr_evac"], 1)

            def slots(n, g, first, z, ahead, behind, more=True, ks=range(CHUNKS)):
                q0 = n * CHUNKS
                for k in ks:
                    c = g * CHUNKS + k
                    if z and not first and (more or k < CHUNKS - 1):
                        fetch(q0 + k + 1, c + 1, k + 1)
                    if z:
                        square(q0 + k, k)
                    if behind or k >= LAG:
                        act.wait_ge(s["tr_done"], q0 + k - LAG + 1)
                    if (behind or k >= 2) and (z or k < 2):
                        gelu(q0 + k - 2, k, first)
                    if behind or k >= LAG:
                        keep(c - LAG)
                        if behind and k == AT_SLOT:
                            act.wait_ge(s["bk_done"], (n - 1) * BACK + AT_GROUPS)
                        a_evac(q0 + k - LAG, (k - LAG) % CHUNKS)
                    if ahead and k in FRONT_SLOTS:
                        front(n - BG + 1, FRONT_SLOTS.index(k))

            def stage(n0, l=None):
                first = l is None
                if not first:
                    fetch(n0 * CHUNKS, 0, 0, l + 1)
                    for i in range(FRONT):
                        front(n0 - BG, i, True)
                slots(n0, 0, first, True, not first, False)
                with act.Fori(1, BG - 1) as g:
                    slots(n0 + g, g, first, True, not first, True)
                slots(n0 + BG - 1, BG - 1, first, True, False, True, False)
                slots(n0 + BG, BG, first, False, False, True, ks=range(LAG))

            def mix(l):
                act.wait_ge(s["w_centred"], CHUNKS * (l + 1))
                act.wait_ge(s["w2_clear"], l + 1)
                wv = w_raw[:, :].rearrange("p (o m) -> p m o", m=MODES)
                with act.Fori(0, MX // 2) as it:
                    for r in range(2):
                        row = it * 2 + r
                        for hf in range(2):
                            hq = (l * MX + row) * 2 + hf
                            act.wait_ge(s["mix_half"], hq + 1)
                            for half in range(2):
                                for im in range(2):
                                    dst = 64 * half + 32 * im
                                    src = 64 * half + 32 * (1 - im)
                                    cp = act.copy(w2[r][hf][dst:dst + 32, :, 64 * half + 32:64 * half + 64],
                                                  wv[src:src + 32, bass.ds(row * MY + hf * HALF, HALF), :])
                            cp.then_inc(s["w2_act"], 1)

            stage(0)
            with act.Fori(0, LAYERS - 1) as l:
                mix(l)
                stage(BG + l * BG, l)
            mix(LAYERS - 1)
            act.sem_inc(s["g1_ready"], 2)
            act.sem_inc(s["g2_ready"], 1)

            def dense(c):
                for b in range(4):
                    act.wait_ge(s["fc1_done"], 4 * c + b + 1)
                    act.wait_ge(s["fc2_done"], 4 * c + b + 1)
                    act.activation(g1[:, b % 2, :], (pc, pf)[b % 2][:, :], ACT.Gelu, bias=fb[:, 0:1]).then_inc(s["g1_ready"], 1)
                    if b == 2:
                        pair(c, 0)

            def pair(c, i):
                act.wait_ge(s["fc2_done"], 4 * c + 2 * i + 4)
                act.wait_ge(s["fc3_done"], c + 1)
                act.activation(g2l[:, i, :], px[:, :], ACT.Gelu, bias=fb[:, 1:2]).then_inc(s["g2_ready"], 1)

            def last_slots(g, z, ahead, behind, more=True, ks=range(CHUNKS)):
                n = LAYERS * BG + g
                q0 = n * CHUNKS
                for k in ks:
                    if z and (more or k < CHUNKS - 1):
                        fetch(q0 + k + 1, g * CHUNKS + k + 1, k + 1)
                    dense_too = (behind or k >= 2) and (z or k < 2)
                    if dense_too:
                        act.wait_ge(s["tr_done"], q0 + k - 1)
                        act.copy(hc[:, k % 2, :], pt[:, :]).then_inc(s["hc_ready"], 1)
                    if z:
                        square(q0 + k, k, 2)
                    if behind or k >= 3:
                        pair(g * CHUNKS + k - 3, 1)
                    if ahead and k in FRONT_SLOTS:
                        front(n - BG + 1, FRONT_SLOTS.index(k))
                    if dense_too:
                        dense(g * CHUNKS + k - 2)

            fetch(LAYERS * BG * CHUNKS, 0, 0, LAYERS)
            for i in range(FRONT):
                front((LAYERS - 1) * BG, i, True)
            last_slots(0, True, True, False)
            with act.Fori(1, BG - 1) as g:
                last_slots(g, True, True, True)
            last_slots(BG - 1, True, False, True, False)
            last_slots(BG, False, False, True, ks=range(3))

        @block.vector
        def _(dve):
            dve.sem_inc(s["t_scaled"], 4)
            dve.sem_inc(s["f1_done"], 2)
            dve.sem_inc(s["var_sum"], 1)
            dve.sem_inc(s["a_written"], 1)
            dve.sem_inc(s["bk_evac"], 1)
            dve.sem_inc(s["y_stored"], 1)
            dve.sem_inc(s["z_stored0"], 16)
            dve.sem_inc(s["z_stored1"], 16)
            dve.sem_inc(s["mix_half"], 4)
            dve.sem_inc(s["fr_done"], 5)
            dve.sem_inc(s["fc2_done"], 2)
            dve.sem_inc(s["fc3_done"], 1)
            dve.sem_inc(s["img_stored"], 16)
            dve.sem_inc(s["zrow_ready"], 2)
            for buf in (w0, fc3, fb):
                fill = dve.memset(buf[:], 0.0)
            fill.then_inc(s["zeroed"], 1)
            dve.wait_ge(s["x_in"], 16)
            dve.tensor_copy(xpl.rearrange("p (i c w) -> p i c w", i=16, c=CI),
                            xraw.rearrange("p (i w c) -> p i c w", i=16, c=CI)).then_inc(s["x_split"], 1)
            for buf in (before, wc):
                fill = dve.memset(buf[:], 0.0)
            fill.then_inc(s["filled"], 1)
            dve.wait_ge(s["filled"], 1)
            dve.memset(xc[32:33], 1.0)
            dve.memset(sq[:, :, CH:], EPS).then_inc(s["filled"], 1)
            n_prep = [0]

            def step(ins):
                n_prep[0] += 1
                ins.then_inc(s["w0_ready"], 1)
                dve.wait_ge(s["w0_ready"], n_prep[0])

            dve.wait_ge(s["params_in"], 16 * 20)
            dve.sem_inc(s["wc_raw"], 1)

            def centre(x, mean, c):
                step(dve.reduce_sum(mean, x, AX.X))
                step(dve.tensor_scalar(mean, mean, 1.0 / c, None, ALU.mult))
                step(dve.tensor_tensor(x, x, mean.unsqueeze(2).broadcast_to(x.shape), ALU.subtract))

            centre(w0[:, :].rearrange("p (b c) -> p b c", b=4), w0m[:, :], CH)
            centre(cb[96:97, :, :], cbm[96:97, :], CH)
            dve.wait_ge(s["wc_t"], 1)
            step(dve.tensor_copy(cwt[:, :, :], pz[0][0:CH, 0:P].rearrange("c (l o) -> c l o", l=LAYERS)))
            centre(cwt[:, :, :], cwm, CH)
            for b in range(4):
                step(dve.tensor_copy(wc[32 * b:32 * b + 32, :, 32 * b:32 * b + 32], cwt[:, :, :]))
            dve.wait_ge(s["consts_in"], 16 * N_CONST)
            dve.sem_inc(s["prep"], 1)

            def var_sum(q, k):
                dve.wait_ge(s["squared"], q + 1)
                dve.reduce_sum(vs[:, k % 4, :], sq, AX.X).then_inc(s["var_sum"], 1)

            def scale(q, k, l, dst, banks=4):
                groups = lambda x: x[:, k % 2, :].rearrange("p (a c) -> p a c", c=CH)
                dve.wait_ge(s["rstd_ready"], q + 1)
                dve.wait_ge(s["gelu_done"], q + 1)
                dve.tensor_tensor(groups(t), pz[k % banks][:, :].rearrange("p (a c) -> p a c", c=CH),
                                  rstd[:, k % 4, :].unsqueeze(2).broadcast_to([P, 16, CH]), ALU.mult).then_inc(s["t_scaled"], 1)
                dve.wait_ge(s["t_scaled"], q + 5)
                dve.tensor_tensor(groups(t), groups(t), lng[:, l, :].unsqueeze(1).broadcast_to([P, 16, CH]), ALU.mult).then_inc(s["t_gained"], 1)
                dve.wait_ge(s["t_gained"], q + 1)
                if dst is ht:
                    dve.wait_ge(s["tr_done"], q - 1)
                add = dve.tensor_tensor(groups(dst), groups(t), lnb[:, l, :].unsqueeze(1).broadcast_to([P, 16, CH]), ALU.add)
                add.then_inc(s["t_ready"], 1) if dst is t else add.then_inc(s["gelu_done"], 1)

            def back(n, i):
                dve.wait_ge(s["bk_done"], n * BACK + i + 1)
                if i < AT_GROUPS:
                    cp = dve.tensor_copy(at[:, CW * i:CW * i + CW], (pg if i == 1 else pb)[:, :])
                else:
                    if i == AT_GROUPS:
                        dve.wait_ge(s["y_stored"], 64 * n + 1)
                    src = pb[:, 0:384].rearrange("p (y x) -> p x y", x=64)[:, 0:48, :]
                    dst = y_st[:, :].rearrange("p (x y) -> p x y", y=MY)[:, :, 6 * (i - AT_GROUPS):6 * (i - AT_GROUPS) + 6]
                    cp = dve.tensor_copy(dst, src)
                cp.then_inc(s["bk_evac"], 1)

            def centre_w(l, k):
                per = MODES // CHUNKS
                at_m = slice(per * k, per * k + per)
                dve.wait_ge(s["w_in"], 64 * (l + 1))
                dve.reduce_sum(w_mean[:, at_m], w_raw[:, :].rearrange("p (o m) -> p m o", m=MODES)[:, at_m, :], AX.X).then_inc(s["w_meaned"], 1)
                dve.wait_ge(s["w_meaned"], l * CHUNKS + k + 1)
                dve.tensor_scalar(w_mean[:, at_m], w_mean[:, at_m], 1.0 / CH, None, ALU.mult).then_inc(s["w_scaled"], 1)
                dve.wait_ge(s["w_scaled"], l * CHUNKS + k + 1)
                om = w_raw[:, :].rearrange("p (o m) -> p o m", m=MODES)[:, :, at_m]
                dve.tensor_tensor(om, om, w_mean[:, at_m].unsqueeze(1).broadcast_to([P, CH, per]), ALU.subtract).then_inc(s["w_centred"], 1)

            def slots(n, l, z, behind, ks=range(CHUNKS), centre=False):
                q0 = n * CHUNKS
                for k in ks:
                    if centre:
                        centre_w(l, k)
                    if (behind or k >= 2) and (z or k < 2):
                        scale(q0 + k - 2, (k - 2) % CHUNKS, l, t)
                    if behind and k == AT_SLOT:
                        for i in range(AT_GROUPS):
                            back(n - 1, i)
                    if behind and k in F2_SLOTS:
                        back(n - 1, AT_GROUPS + F2_SLOTS.index(k))
                    if z:
                        var_sum(q0 + k, k)

            def stage(n0, l):
                slots(n0, l, True, False)
                with dve.Fori(1, BG - 1) as g:
                    slots(n0 + g, l, True, True)
                slots(n0 + BG - 1, l, True, True, centre=True)
                slots(n0 + BG, l, False, True, range(LAG))
                for i in range(BACK):
                    back(n0 + BG - 1, i)

            def mix(l):
                ov = w_raw[:, :].rearrange("p (o m) -> p m o", m=MODES)
                for buf in w2[0] + w2[1]:
                    clear = dve.memset(buf, 0.0)
                clear.then_inc(s["w2_clear"], 1)
                dve.wait_ge(s["w2_clear"], l + 1)
                bias = g2[96:97, :, :].rearrange("p a (b c) -> p (a b) c", c=CH)
                dve.tensor_copy(bias, cb[96:97, l, :].unsqueeze(1).broadcast_to([1, 64, CH])).then_inc(s["bias_set"], 1)

                def build(x, r):
                    for hf in range(2):
                        dve.wait_ge(s["mix_half"], (l * MX + x) * 2 + hf + 1)
                        for half in range(2):
                            p0 = 64 * half
                            cp = dve.tensor_scalar(w2[r][hf][p0:p0 + 64, :, 64 * half:64 * half + 32],
                                                   ov[p0:p0 + 64, bass.ds(x * MY + hf * HALF, HALF), :],
                                                   sign[p0:p0 + 64, :], None, ALU.mult)
                        cp.then_inc(s["w2_dve"], 1)

                def evac(x, pair, r):
                    dve.wait_ge(s["mix_half"], (l * MX + x) * 2 + 6)
                    dve.wait_ge(z_stored[r], 16 * (l * (MX // 2) + pair) + 16)
                    for i in range(3):
                        out = dve.tensor_copy(z_row[:, r, :].rearrange("p (n y) -> p y n", y=MY)[:, 4 * i:4 * i + 4, :],
                                              pm[r][i][0:B, :].rearrange("p (y n) -> p y n", y=4))
                    out.then_inc(s["zrow_ready"], 1)

                build(0, 0)
                with dve.Fori(0, MX // 2 - 1) as it:
                    build(it * 2 + 1, 1)
                    evac(it * 2, it, 0)
                    build(it * 2 + 2, 0)
                    evac(it * 2 + 1, it, 1)
                build(MX - 1, 1)
                evac(MX - 2, MX // 2 - 1, 0)
                evac(MX - 1, MX // 2 - 1, 1)
                dve.memset(sq[:, :, CH:], EPS).then_inc(s["guard_set"], 1)
                dve.wait_ge(s["guard_set"], l + 1)

            stage(0, 0)
            with dve.Fori(0, LAYERS - 1) as l:
                mix(l)
                stage(BG + l * BG, l + 1)
            mix(LAYERS - 1)
            dve.sem_inc(s["o1_ready"], 1)
            dve.sem_inc(s["o2_ready"], 1)

            def o1_evac(c, k):
                dve.wait_ge(s["fc3_done"], c + 2)
                src = pb[:, :].rearrange("p (a j x) -> p a j x", a=2, j=4)[:, :, :, 0:2].rearrange("p a j b -> p a b j")
                dst = o1.rearrange("p (a b j) -> p a b j", a=2, b=2)[:, :, :, 4 * k:4 * k + 4]
                dve.tensor_scalar(dst, src, fb[:, 2:3], None, ALU.add).then_inc(s["o1_ready"], 1)

            def turned_out(g):
                dve.wait_ge(s["o_tr"], g + 1)
                dve.wait_ge(s["img_stored"], 16 * g + 16)
                dve.tensor_copy(o2, pg[:, 0:P]).then_inc(s["o2_ready"], 1)

            def last_slots(g, z, behind, ks=range(CHUNKS)):
                q0 = (LAYERS * BG + g) * CHUNKS
                for k in ks:
                    if (behind or k >= 1) and (z or k < 1):
                        scale(q0 + k - 1, (k - 1) % CHUNKS, LAYERS, ht, 2)
                    if z:
                        var_sum(q0 + k, k)
                    if behind and k == AT_SLOT:
                        turned_out(g - 1)
                    if behind or k >= 3:
                        o1_evac(g * CHUNKS + k - 3, (k - 3) % CHUNKS)

            last_slots(0, True, False)
            with dve.Fori(1, BG) as g:
                last_slots(g, True, True)
            last_slots(BG, False, True, range(3))
            turned_out(BG - 1)


def tail_constants():
    u = np.arange(T)
    f = np.float32
    return dict(k_tri=(u[:, None] <= u[None, :]).astype(f),
                k_below=np.broadcast_to((np.arange(NE)[None, :] < np.arange(NE)[:, None]).reshape(1, 64), (T, 64)).astype(f).copy())


def build_tail(nc, sems, d, img, out):
    with ExitStack() as ctx:
        sb = lambda n, s, t=F32: ctx.enter_context(nc.sbuf_tensor(n, s, t))
        x = sb("x_tok", [T, NB, D])
        centred = sb("x_centred", [T, NB, D])
        squares = sb("x_squares", [T, NB, D])
        mean, var, rs, nhalf = sb("mean_t", [T, NB]), sb("var_t", [T, NB]), sb("rstd_t", [T, NB]), sb("nhalf_t", [T, NB])
        norm = sb("norm_t", [T, 2, GB, D])
        xg = sb("xg", [P, 2, GT])
        xt = sb("xt", [P, NG, GT])
        ident = sb("ident_t", [P, P])
        tri, ones = sb("tri", [T, T]), sb("ones_t", [T, T])
        below = sb("below", [T, NE, NE])
        table = sb("table", [1, 1])
        big = sb("big", [P, 2 * T * P])
        STATES_AT = T * P
        KEYS_AT = 2 * HEADS * GT
        MAPS_AT = KEYS_AT + 2 * HEADS * D
        MIXED_AT = STATES_AT + (T + 1) * NB
        WEIGHED_AT = MIXED_AT + 2 * NE * D
        FILLS_AT = WEIGHED_AT + 2 * NE * D
        qst = big[:, 0:2 * HEADS * GT].rearrange("p (r h n) -> p r h n", r=2, h=HEADS)
        es = big[0:T, KEYS_AT:MAPS_AT].rearrange("p (r n) -> p r n", r=2)
        om = big[0:T, MAPS_AT:MAPS_AT + 2 * HEADS * T].rearrange("p (r h n) -> p r h n", r=2, h=HEADS)
        wq, we, wet = sb("wq", [P, HEADS, D]), sb("we", [P, 4, D]), sb("wet", [P, HEADS * D])
        hid = big[:, 0:2 * 16 * GT].rearrange("p (r c n) -> p r c n", r=2, c=16)
        w1 = [sb(f"w1_{i}", [P, NE, FF]) for i in range(2)]
        w2 = [sb(f"w2_{i}", [P, 2 * NE, D]) for i in range(2)]
        b2 = [sb(f"b2_{i}", [T, NE, D]) for i in range(2)]
        wg = [sb(f"wg_{i}", [P, NE]) for i in range(2)]
        logit = sb("logit", [T, NB, NE])
        gate = sb("gate", [T, NB, NE])
        picked = sb("picked", [T, NB, NE])
        place = sb("place", [T, 2, NB, NE])
        top, total = sb("top", [T, NB]), sb("total", [T, NB])
        above = squares[:, :, :].rearrange("p b (e f) -> p b e f", e=NE)
        equal = centred[:, :, :].rearrange("p b (e f) -> p b e f", e=NE)
        mixed = big[0:T, MIXED_AT:WEIGHED_AT].rearrange("p (r n) -> p r n", r=2)
        weighed = big[0:T, WEIGHED_AT:FILLS_AT].rearrange("p (r n) -> p r n", r=2)
        y = sb("y_t", [T, 2, GB * D])
        y_all = squares
        odd = sb("odd", [T, 2, GB * D], U32)
        fills = big[0:T, FILLS_AT:FILLS_AT + 3 * GB * D].rearrange("p (m n) -> p m n", m=3)
        xw = big[:, :].rearrange("p (r t n) -> p r t n", r=2, t=T)
        lw = [sb(f"lw_{i}", [P, GATES * HID]) for i in range(2)]
        lu = [sb(f"lu_{i}", [HID, GATES * HID]) for i in range(3)]
        lwd = sb("lwd", [HID, 2, GATES * HID])
        lbd = sb("lbd", [1, GATES * HID])
        hs = sb("hs", [HID, 2, 2, NB])
        cs = sb("cs", [HID, 3, NB])
        sig = sb("sig", [HID, 3, 3 * NB])
        tg, cell_t = sb("tanh_gate", [HID, 3, NB]), sb("tanh_cell", [HID, 3, NB])
        kept, ig = sb("kept_part", [HID, 3, NB]), sb("input_part", [HID, 3, NB])
        zc = sb("zc", [HID, GATES * NB])
        hd = big[:, STATES_AT:STATES_AT + (T + 1) * NB].rearrange("p (t n) -> p t n", t=T + 1)
        wo, bo = sb("wo", [HID, D]), sb("bo", [T, D])
        ps = [ctx.enter_context(nc.psum_tensor(f"pt{i}", [P, 512], F32)) for i in range(8)]
        up_banks = [ps[2], ps[3], ps[6], ps[7]]
        names = """x_in attn_in loaded zeroed xt_zeroed filled setup_done sums meaned centred squared sq_sums varied powed rstd
            normed turned turned_out we_turned wet_done q_done q_out es_done es_out om_done om_out r_done
            r_added logit_done logit_out up_done hid_done down_done added weighted summed y_added gate_step
            exp_in exp_done tri_in tri_done xw_done xw_act xw_dve zc_done zc_out dec_done dec_out out_sent
            xt_kept""".split()
        names += [f"{n}{r}" for n in ("gates_done", "sigmoids", "cell_gate", "input_part", "cell_new", "cell_tanh", "state_new") for r in range(3)]
        s = {n: sems.enter_context(nc.semaphore("t_" + n)) for n in names}
        N_LOADS = 1 + 12 + 4 + 3 + 4
        GATE_AT = (0, 1, 3, 2)
        block = ctx.enter_context(nc.Block())

        def row(ap):
            return ap.rearrange("(a n) -> a n", a=1)

        @block.sync
        def _(sp):
            def ld(dst, src, into="loaded"):
                sp.dma_start(dst, src).then_inc(s[into], 16)
            ld(x[0:TI, :, :], img.rearrange("b t w -> t b w"), "x_in")
            ld(x[TI:T, :, :], d["txt"].rearrange("b t w -> t b w"), "x_in")
            ld(ident[:, :], d["k_id"], "attn_in")
            ld(we[:, :, :], d["L0_attn_E"].rearrange("(a h) i j -> (h i) a j", h=2), "attn_in")
            ld(tri[:, :], d["k_tri"], "attn_in")
            sp.wait_ge(s["setup_done"], 1)
            ld(wq[0:D, :, :], d["L0_attn_Q"].rearrange("h i j -> i h j"), "attn_in")
            ld(below[:, :, :].rearrange("p a b -> p (a b)"), d["k_below"])
            sp.wait_ge(s["zeroed"], 2)
            for i, (g, bg, a, b, c, e) in enumerate((("L0_ffn_Wg", "L0_ffn_bg", "L0_ffn_W1", "L0_ffn_b1", "L0_ffn_W2", "L0_ffn_b2"),
                                                     ("L1_ffn_gate_w", "L1_ffn_gate_b", "L1_ffn_w1", "L1_ffn_b1", "L1_ffn_w2", "L1_ffn_b2"))):
                ld(wg[i][0:D, :], d[g])
                ld(wg[i][D:D + 1, :], row(d[bg]))
                ld(w1[i][0:D, :, :], d[a].rearrange("e d f -> d e f"))
                ld(w1[i][D:D + 1, :, :], d[b].rearrange("(a e) f -> a e f", a=1))
                ld(w2[i][:, :, :], d[c].rearrange("e (k f) d -> f (e k) d", f=P))
                ld(b2[i][:, :, :].rearrange("p e d -> p (e d)"), d[e].rearrange("(a e) d -> a (e d)", a=1).broadcast_to([T, NE * D]))
            for i, (w, b) in enumerate((("Wf", "bf"), ("Wb", "bb"))):
                ld(lw[i][0:D, :], d["L1_attn_" + w])
                ld(lw[i][D:D + 1, :], row(d["L1_attn_" + b]))
            for i, u in enumerate(("Uf", "Ub", "Ud")):
                ld(lu[i][:, :], d["L1_attn_" + u])
            ld(lwd[:, :, :], d["L1_attn_Wd"].rearrange("(k p) n -> p k n", p=HID))
            ld(lbd[:, :], row(d["L1_attn_bd"]))
            ld(wo[:, :], d["L1_attn_Wo"])
            ld(bo[:, :], row(d["L1_attn_bo"]).broadcast_to([T, D]))
            ov = out.rearrange("(g b) t w -> g t b w", b=GB)
            with sp.Fori(0, NG) as g:
                sp.wait_ge(s["y_added"], NG + g + 1)
                sp.dma_start(ov[g], x[:, bass.ts(g, GB), :]).then_inc(s["out_sent"], 16)
            sp.wait_ge(s["out_sent"], 16 * NG)

        @block.gpsimd
        def _(pool):
            pool.memset(nhalf[:, :], -0.5).then_inc(s["powed"], 1)
            pool.wait_ge(s["powed"], 1)
            for r in range(2):
                zeros = pool.memset(qst[D:P, r], 0.0)
            zeros.then_inc(s["zeroed"], 1)
            pool.wait_ge(s["zeroed"], 1)
            for n, (b0, nb) in enumerate(NORM_PARTS):
                if n == 2:
                    pool.wait_ge(s["rstd"], 2)
                    pool.memset(xt[D:P], 0.0).then_inc(s["xt_zeroed"], 1)
                    pool.wait_ge(s["xt_zeroed"], 1)
                    pool.memset(xt[D:D + 1], 1.0).then_inc(s["xt_zeroed"], 1)
                    pool.wait_ge(s["xt_zeroed"], 2)
                    for padded in (w1[0], w1[1], wg[0], wg[1], lw[0], lw[1]):
                        zeros = pool.memset(padded[D:P], 0.0)
                    zeros.then_inc(s["zeroed"], 1)
                    pool.wait_ge(s["zeroed"], 2)
                pool.wait_ge(s["varied"], n + 1)
                pool.tensor_tensor(rs[:, b0:b0 + nb], var[:, b0:b0 + nb], nhalf[:, b0:b0 + nb], ALU.pow).then_inc(s["rstd"], 1)

        @block.tensor
        def _(pe):
            pe.wait_ge(s["attn_in"], 16 * 4)
            pe.wait_ge(s["setup_done"], 1)
            pe.wait_ge(s["zeroed"], 1)
            for a in range(4):
                mm = pe.transpose(ps[0][0:D, P * a:P * a + P], we[:, a, :], ident[:, :])
            mm.then_inc(s["we_turned"], 1)
            pe.wait_ge(s["wet_done"], 1)

            def turn(n, par, g):
                k = n * NG + g
                pe.wait_ge(s["normed"], k + 1)
                pe.wait_ge(s["turned_out"], k + 2)
                for pair in range(GB // 2):
                    mm = pe.transpose(ps[0][:, T * pair:T * pair + T], norm[:, par, 2 * pair:2 * pair + 2, :], ident[0:T, 0:T])
                mm.then_inc(s["turned"], 1)

            def turned(n, g):
                pe.wait_ge(s["turned_out"], n * NG + g + 3)

            def queries(par, g):
                turned(0, g)
                for a in range(4):
                    pe.wait_ge(s["q_out"], 4 * g + a + 1)
                    pe.matmul(ps[1 + a % 2][:, 0:GT], wq[:, 2 * a:2 * a + 2, :], xg[:, par, :], start=True, stop=True).then_inc(s["q_done"], 1)

            def attend(par, b, k4):
                pe.wait_ge(s["es_out"], k4 + 1)
                sT = xg[:, par, T * b:T * b + T]
                pe.matmul(ps[3][0:T, :], sT, wet[:, :], start=True, stop=True).then_inc(s["es_done"], 1)
                pe.wait_ge(s["om_out"], k4 + 1)
                for hh in range(2):
                    mm = pe.matmul(ps[4 + hh][0:T, 0:GT], sT, qst[:, par, 4 * hh:4 * hh + 4, T * b:T * b + T], start=True, stop=True)
                mm.then_inc(s["om_done"], 1)

            def gather(b, k4):
                pe.wait_ge(s["om_out"], k4 + 2)
                pe.wait_ge(s["es_out"], k4 + 2)
                for h in range(HEADS):
                    mm = pe.matmul(ps[6 + b // 2][0:T, D * (b % 2):D * (b % 2) + D], om[:, b % 2, h, :], es[:, b % 2, D * h:D * h + D],
                                   start=(h == 0), stop=(h == HEADS - 1))
                mm.then_inc(s["r_done"], 1)

            def attention(par, g, more=True):
                pe.wait_ge(s["q_out"], 4 * g + 6)
                for b in range(GB):
                    attend(par, b, g * GB + b)
                    if b == 1 and more:
                        turn(0, 1 - par, g + 1)
                    if b == 2 and more:
                        queries(1 - par, g + 1)
                    if b % 2 == 1:
                        pe.wait_ge(s["r_added"], 2 * g + b // 2 + 1)
                    if b:
                        gather(b - 1, g * GB + b - 1)
                gather(GB - 1, g * GB + GB - 1)

            turn(0, 0, 0)
            queries(0, 0)
            with pe.Fori(0, NG // 2 - 1) as it:
                for par in range(2):
                    attention(par, it * 2 + par)
            attention(0, NG - 2)
            attention(1, NG - 1, False)

            def experts(i, n):
                def logits(par, g, more=True):
                    if more:
                        turn(n, 1 - par, g + 1)
                    turned(n, g)
                    pe.wait_ge(s["logit_out"], i * NG + g + 1)
                    for b in range(GB):
                        mm = pe.matmul(ps[1][0:T, NE * b:NE * b + NE], xg[:, par, T * b:T * b + T], wg[i][:, :], start=True, stop=True)
                    mm.then_inc(s["logit_done"], 1)

                turn(n, 0, 0)
                with pe.Fori(0, NG // 2 - 1) as it:
                    for par in range(2):
                        logits(par, it * 2 + par)
                logits(0, NG - 2)
                logits(1, NG - 1, False)
                if i:
                    pe.wait_ge(s["tri_in"], 1)
                    picks = picked[:, :, :].rearrange("p b e -> p (b e)")
                    pe.wait_ge(s["logit_out"], 2 * NG + 1)
                    pe.matmul(ps[1][0:T, 0:NB * NE], tri[:, :], picks, start=True, stop=True)
                    pe.matmul(ps[1][0:T, NB * NE:2 * NB * NE], ones[:, :], picks, start=True, stop=True).then_inc(s["tri_done"], 1)
                pe.wait_ge(s["xt_kept"], (i + 1) * NG)

                def up(par, g, cs):
                    k = (i * NG + g) * 2 * NE
                    for c in cs:
                        pe.wait_ge(s["hid_done"], k + c + 1)
                        pe.matmul(up_banks[c % 4][:, 0:GT], w1[i][:, c // 2, (c % 2) * P:(c % 2) * P + P], xt[:, g, :],
                                  start=True, stop=True).then_inc(s["up_done"], 1)

                def down(par, g, b):
                    pe.wait_ge(s["hid_done"], (i * NG + g) * 2 * NE + 2 * NE + 4)
                    pe.wait_ge(s["added"], (i * NG + g) * GB + b + 1)
                    for e in range(NE):
                        for f in range(2):
                            mm = pe.matmul(ps[4 + b % 2][0:T, D * e:D * e + D], hid[:, par, 2 * e + f, T * b:T * b + T],
                                           w2[i][:, 2 * e + f, :], start=(f == 0), stop=(f == 1))
                    mm.then_inc(s["down_done"], 1)

                def both(par, g, more=True):
                    for b in range(GB):
                        if more:
                            up(1 - par, g + 1, range(4 * b, 4 * b + 4))
                        down(par, g, b)

                up(0, 0, range(2 * NE))
                with pe.Fori(0, NG // 2 - 1) as it:
                    for par in range(2):
                        both(par, it * 2 + par)
                both(0, NG - 2)
                both(1, NG - 1, False)

            pe.wait_ge(s["loaded"], 16 * N_LOADS)
            pe.wait_ge(s["xt_zeroed"], 2)
            experts(0, 1)

            def shares(par, g, more=True):
                turned(2, g)
                for r in range(2):
                    for q in range(GATES):
                        pe.wait_ge(s[("xw_act", "xw_dve")[q % 2]], g * 4 + r * 2 + q // 2 + 1)
                        pe.matmul(up_banks[q][:, 0:GT], lw[r][:, HID * q:HID * q + HID], xg[:, par, :], start=True, stop=True).then_inc(s["xw_done"], 1)
                    if r == 0 and more:
                        turn(2, 1 - par, g + 1)

            turn(2, 0, 0)
            with pe.Fori(0, NG // 2 - 1) as it:
                for par in range(2):
                    shares(par, it * 2 + par)
            shares(0, NG - 2)
            shares(1, NG - 1, False)
            pe.wait_ge(s["xw_act"], NG * 4 + 2)
            pe.wait_ge(s["xw_dve"], NG * 4 + 2)

            def keep_fast(width):
                pe.matmul(ps[7][:, 0:width], ident[:, :], lu[2][:, 0:width], start=True, stop=True)

            def decoder_gates(par, st):
                for bank, cols in ((ps[par], slice(0, 3 * NB)), (ps[2 + par], slice(3 * NB, 4 * NB))):
                    pe.matmul(bank[:, 0:cols.stop - cols.start], ident[:, :], zc[:, cols], start=True, stop=False, skip_group_check=True)
                pe.wait_ge(s["state_new2"], st + 1)
                for q in range(GATES):
                    at = ps[par][:, NB * q:NB * q + NB] if q < 3 else ps[2 + par][:, 0:NB]
                    mm = pe.matmul(at, lu[2][:, HID * q:HID * q + HID], hd[:, st, :], start=False, stop=(q >= 2), skip_group_check=True)
                    if q >= 2:
                        mm.then_inc(s["gates_done2"], 1)

            def gates(r, bank, share, state):
                pe.matmul(bank[:, 0:P], ident[:, :], share, start=True, stop=False, skip_group_check=True)
                pe.wait_ge(s[f"state_new{r}"], state[1])
                for q in range(GATES):
                    mm = pe.matmul(bank[:, NB * GATE_AT[q]:NB * GATE_AT[q] + NB], lu[r][:, HID * q:HID * q + HID], state[0],
                                   start=False, stop=(q == GATES - 1), skip_group_check=True)
                mm.then_inc(s[f"gates_done{r}"], 1)

            for k in range(START_FILLS):
                keep_fast(512)
            with pe.Fori(0, T // 2) as it:
                for par in range(2):
                    st = it * 2 + par
                    for r in range(2):
                        at = st if r == 0 else (T - 1) - st
                        gates(r, ps[2 * r + par], xw[:, r, at, :], (hs[:, r, par, :], st + 1))
                        keep_fast(ENCODER_FILL)
            for r in range(2):
                pe.wait_ge(s[f"state_new{r}"], T + 1)
            for q in range(GATES):
                o = NB * q
                for k in range(2):
                    pe.matmul(ps[4][:, o:o + NB], lwd[:, k, HID * q:HID * q + HID], hs[:, k, 0, :], start=(k == 0), stop=False)
                mm = pe.matmul(ps[4][:, o:o + NB], lbd[:, HID * q:HID * q + HID], ones[0:1, 0:NB], start=False, stop=True)
            mm.then_inc(s["zc_done"], 1)
            for k in range(START_FILLS):
                keep_fast(512)
            pe.wait_ge(s["zc_out"], 1)
            with pe.Fori(0, T // 2) as it:
                for par in range(2):
                    st = it * 2 + par
                    decoder_gates(par, st)
                    keep_fast(DECODER_FILL)
            pe.wait_ge(s["state_new2"], T + 1)
            for b in range(NB):
                if b % 8 == 0:
                    pe.wait_ge(s["dec_out"], b // 8 + 1)
                mm = pe.matmul(ps[2 + (b // 8) % 2][0:T, D * (b % 8):D * (b % 8) + D], hd[:, 1:T + 1, b], wo[:, :], start=True, stop=True)
                if b % 8 == 7:
                    mm.then_inc(s["dec_done"], 1)
            experts(1, 3)

        @block.scalar
        def _(act):
            act.sem_inc(s["turned_out"], 2)
            act.sem_inc(s["q_out"], 2)
            act.sem_inc(s["es_out"], 1)
            act.sem_inc(s["xw_act"], 2)
            act.sem_inc(s["hid_done"], 4)

            def load_table(func):
                act.activation(table[:, :], nhalf[0:1, 0:1], func)

            def square(part, b0, nb):
                act.wait_ge(s["centred"], part + 1)
                act.activation(squares[:, bass.ds(b0, nb), :], centred[:, bass.ds(b0, nb), :], ACT.Square).then_inc(s["squared"], 1)

            def turned(n, par, g, keep=False):
                act.wait_ge(s["turned"], n * NG + g + 1)
                for h in range(2):
                    cp = act.copy(xg[0:D, par, :].rearrange("p (b h t) -> p h b t", h=2, t=T)[:, h],
                                  ps[0][D * h:D * h + D, 0:2 * T].rearrange("p (b t) -> p b t", t=T))
                cp.then_inc(s["turned_out"], 1)
                if keep:
                    act.wait_ge(s["turned_out"], n * NG + g + 3)
                    act.copy(xt[0:D, g, :], xg[0:D, par, :]).then_inc(s["xt_kept"], 1)

            def queries(par, g):
                for a in range(4):
                    act.wait_ge(s["q_done"], 4 * g + a + 1)
                    for hh in range(2):
                        cp = act.copy(qst[0:D, par, 2 * a + hh, :], ps[1 + a % 2][D * hh:D * hh + D, 0:GT])
                    cp.then_inc(s["q_out"], 1)

            def attention(par, g, more=True, behind=True):
                for b in range(GB):
                    act.wait_ge(s["es_done"], g * GB + b + 1)
                    act.copy(es[:, b % 2, :], ps[3][0:T, :]).then_inc(s["es_out"], 1)
                    if b == 1 and more:
                        turned(0, 1 - par, g + 1)
                    if b == 2 and more:
                        queries(1 - par, g + 1)
                    if b == 2 and behind:
                        square(NORM_AT[1] + g - 1, GB * (g - 1), GB)

            for part in range(2):
                square(part, *NORM_PARTS[part])
            turned(0, 0, 0)
            queries(0, 0)
            attention(0, 0, behind=False)
            attention(1, 1)
            with act.Fori(1, NG // 2 - 1) as it:
                for par in range(2):
                    attention(par, it * 2 + par)
            attention(0, NG - 2)
            attention(1, NG - 1, False)
            square(NORM_AT[1] + NG - 1, GB * (NG - 1), GB)

            def experts(i, n):
                with act.Fori(0, NG // 2) as it:
                    for par in range(2):
                        g = it * 2 + par
                        turned(n, par, g, True)
                act.wait_ge(s["exp_in"], i + 1)
                act.activation(gate[:, :, :], gate[:, :, :], ACT.Exp).then_inc(s["exp_done"], 1)
                if i == 0:
                    load_table(ACT.Gelu)

                def hidden(par, g, behind):
                    k = (i * NG + g) * 2 * NE
                    for c in range(2 * NE):
                        act.wait_ge(s["up_done"], k + c + 1)
                        act.activation(hid[:, par, c, :], up_banks[c % 4][:, 0:GT], ACT.Relu if i else ACT.Gelu).then_inc(s["hid_done"], 1)
                        if behind and c == NE:
                            square(NORM_AT[2] + g - 2, GB * (g - 2), GB)

                hidden(0, 0, False)
                hidden(1, 1, False)
                with act.Fori(1, NG // 2) as it:
                    for par in range(2):
                        hidden(par, it * 2 + par, i == 0)
                if i == 0:
                    for g in range(NG - 2, NG):
                        square(NORM_AT[2] + g, GB * g, GB)

            experts(0, 1)
            def shares(par, g, more=True):
                for r in range(2):
                    for q in (0, 2):
                        act.wait_ge(s["xw_done"], g * 8 + r * 4 + q + 1)
                        o = NB * GATE_AT[q]
                        act.copy(xw[:, r, :, o:o + NB].rearrange("p t (g b) -> p g b t", b=GB)[:, g],
                                 up_banks[q][:, 0:GT].rearrange("p (b t) -> p b t", b=GB)).then_inc(s["xw_act"], 1)
                    if r == 0 and more:
                        turned(2, 1 - par, g + 1)

            turned(2, 0, 0)
            with act.Fori(0, NG // 2 - 1) as it:
                for par in range(2):
                    shares(par, it * 2 + par)
            shares(0, NG - 2)
            shares(1, NG - 1, False)

            def cell(r, bank, st):
                act.wait_ge(s[f"gates_done{r}"], st + 1)
                act.activation(sig[:, r, :], bank[:, 0:3 * NB], ACT.Sigmoid).then_inc(s[f"sigmoids{r}"], 1)
                act.activation(tg[:, r, :], bank[:, 3 * NB:4 * NB], ACT.Tanh).then_inc(s[f"cell_gate{r}"], 1)
                act.wait_ge(s[f"cell_new{r}"], st + 1)
                act.activation(cell_t[:, r, :], cs[:, r, :], ACT.Tanh).then_inc(s[f"cell_tanh{r}"], 1)

            load_table(ACT.Sigmoid)
            with act.Fori(0, T // 2) as it:
                for par in range(2):
                    for r in range(2):
                        cell(r, ps[2 * r + par], it * 2 + par)
            with act.Fori(0, T // 2) as it:
                for par in range(2):
                    st = it * 2 + par
                    act.wait_ge(s["gates_done2"], 2 * st + 1)
                    act.activation(sig[:, 2, 0:2 * NB], ps[par][:, 0:2 * NB], ACT.Sigmoid).then_inc(s["sigmoids2"], 1)
                    act.activation(tg[:, 2, :], ps[par][:, 2 * NB:3 * NB], ACT.Tanh).then_inc(s["cell_gate2"], 1)
                    act.wait_ge(s["gates_done2"], 2 * st + 2)
                    act.activation(sig[:, 2, 2 * NB:3 * NB], ps[2 + par][:, 0:NB], ACT.Sigmoid)
                    act.wait_ge(s["cell_new2"], st + 1)
                    act.activation(cell_t[:, 2, :], cs[:, 2, :], ACT.Tanh).then_inc(s["cell_tanh2"], 1)
            for v in range(QUARTERS):
                square(NORM_AT[3] + v, 8 * v, 8)
            experts(1, 3)

        @block.vector
        def _(dve):
            dve.sem_inc(s["om_out"], 1)
            dve.sem_inc(s["r_added"], 2)
            dve.sem_inc(s["logit_out"], 1)
            dve.sem_inc(s["added"], 2)
            dve.sem_inc(s["xw_dve"], 2)
            dve.sem_inc(s["dec_out"], 2)
            for padded in (wq, wet, xg):
                zeros = dve.memset(padded[D:P], 0.0)
            zeros.then_inc(s["filled"], 1)
            dve.wait_ge(s["filled"], 1)
            dve.memset(xg[D:D + 1], 1.0)
            dve.memset(ones[:, :], 1.0)
            dve.memset(hs[:], 0.0)
            dve.memset(cs[:], 0.0).then_inc(s["setup_done"], 1)
            for r in range(3):
                dve.sem_inc(s[f"state_new{r}"], 1)
            dve.wait_ge(s["we_turned"], 1)
            dve.tensor_copy(wet[0:D, :], ps[0][0:D, :]).then_inc(s["wet_done"], 1)

            def centre(part, b0, nb):
                v = bass.ds(b0, nb)
                dve.reduce_sum(mean[:, v], x[:, v, :], AX.X).then_inc(s["sums"], 1)
                dve.wait_ge(s["sums"], part + 1)
                dve.tensor_scalar(mean[:, v], mean[:, v], 1.0 / D, None, ALU.mult).then_inc(s["meaned"], 1)
                dve.wait_ge(s["meaned"], part + 1)
                dve.tensor_tensor(centred[:, v, :], x[:, v, :], mean[:, v].unsqueeze(2).broadcast_to([T, nb, D]), ALU.subtract).then_inc(s["centred"], 1)

            def spread(part, b0, nb):
                v = bass.ds(b0, nb)
                dve.wait_ge(s["squared"], part + 1)
                dve.reduce_sum(var[:, v], squares[:, v, :], AX.X).then_inc(s["sq_sums"], 1)
                dve.wait_ge(s["sq_sums"], part + 1)
                dve.tensor_scalar(var[:, v], var[:, v], 1.0 / D, EPS, ALU.mult, ALU.add).then_inc(s["varied"], 1)

            def scale(n, par, g, part):
                k = n * NG + g
                dve.wait_ge(s["turned_out"], k + 1)
                dve.wait_ge(s["rstd"], NORM_AT[n] + part + 1)
                xb = centred[:, bass.ts(g, GB), :]
                dve.tensor_tensor(norm[:, par, :, :], xb, rs[:, bass.ts(g, GB)].unsqueeze(2).broadcast_to([T, GB, D]), ALU.mult).then_inc(s["normed"], 1)

            def attention(par, g, more=True, behind=True):
                for b in range(GB):
                    k4 = g * GB + b
                    dve.wait_ge(s["om_done"], k4 + 1)
                    for hh in range(2):
                        mk = dve.tensor_tensor(om[:, b % 2, 4 * hh:4 * hh + 4, :], ps[4 + hh][0:T, 0:GT].rearrange("p (h t) -> p h t", h=4),
                                               tri[:, :].unsqueeze(1).broadcast_to([T, 4, T]), ALU.mult)
                    mk.then_inc(s["om_out"], 1)
                    if b == 0 and more:
                        scale(0, 1 - par, g + 1, 1)
                    if b == 1 and behind:
                        dve.wait_ge(s["r_added"], 2 * g + 2)
                        centre(NORM_AT[1] + g - 1, GB * (g - 1), GB)
                    if b == 2:
                        add_pair(g, 0)
                    if b == 3 and behind:
                        spread(NORM_AT[1] + g - 1, GB * (g - 1), GB)
                add_pair(g, 1)

            def add_pair(g, pair):
                dve.wait_ge(s["r_done"], g * GB + 2 * pair + 2)
                xb = x[:, bass.ds(g * GB + 2 * pair, 2), :]
                dve.tensor_tensor(xb, ps[6 + pair][0:T, 0:2 * D].rearrange("p (b d) -> p b d", b=2), xb, ALU.add).then_inc(s["r_added"], 1)

            dve.wait_ge(s["x_in"], 32)
            for part in range(2):
                centre(part, *NORM_PARTS[part])
            spread(0, *NORM_PARTS[0])
            scale(0, 0, 0, 0)
            spread(1, *NORM_PARTS[1])
            dve.wait_ge(s["attn_in"], 16 * 4)
            attention(0, 0, behind=False)
            attention(1, 1)
            with dve.Fori(1, NG // 2 - 1) as it:
                for par in range(2):
                    attention(par, it * 2 + par)
            attention(0, NG - 2)
            attention(1, NG - 1, False)
            dve.wait_ge(s["r_added"], 2 * NG + 2)
            centre(NORM_AT[1] + NG - 1, GB * (NG - 1), GB)
            spread(NORM_AT[1] + NG - 1, GB * (NG - 1), GB)
            dve.wait_ge(s["loaded"], 16 * N_LOADS)
            steps = [0]

            def step(ins):
                steps[0] += 1
                ins.then_inc(s["gate_step"], 1)
                dve.wait_ge(s["gate_step"], steps[0])

            def by_token(v):
                return v.unsqueeze(2).broadcast_to([T, NB, NE])

            def rank_two():
                other = logit[:, :, :].unsqueeze(2).broadcast_to([T, NB, NE, NE])
                own = logit[:, :, :].unsqueeze(3).broadcast_to([T, NB, NE, NE])
                step(dve.tensor_tensor(above, other, own, ALU.is_gt))
                step(dve.tensor_tensor(equal, other, own, ALU.is_equal))
                step(dve.tensor_tensor(centred[:, :, :], centred[:, :, :], below[:, :, :].rearrange("p a b -> p (a b)").unsqueeze(1).broadcast_to([T, NB, 64]), ALU.mult))
                step(dve.tensor_tensor(squares[:, :, :], squares[:, :, :], centred[:, :, :], ALU.add))
                step(dve.reduce_sum(picked[:, :, :], above, AX.X))
                step(dve.tensor_scalar(picked[:, :, :], picked[:, :, :], 1.5, None, ALU.is_lt))

            def first_best():
                best, before = place[:, 0, :, :], place[:, 1, :, :]
                step(dve.reduce_max(top[:, :], gate[:, :, :], AX.X))
                step(dve.tensor_tensor(best, gate[:, :, :], by_token(top[:, :]), ALU.is_equal))
                src, dst = best, before
                for w in (1, 2, 4):
                    step(dve.tensor_copy(dst[:, :, 0:w], src[:, :, 0:w]))
                    step(dve.tensor_tensor(dst[:, :, w:], src[:, :, w:], src[:, :, 0:NE - w], ALU.add))
                    src, dst = dst, (logit[:, :, :] if dst is before else before)
                step(dve.tensor_scalar(picked[:, :, :], src, 1.5, None, ALU.is_lt))
                step(dve.tensor_tensor(picked[:, :, :], picked[:, :, :], best, ALU.mult))

            def experts(i, n):
                def logits(par, g, half, more=True):
                    if more:
                        scale(n, 1 - par, g + 1, half + par if i else g + 1)
                    dve.wait_ge(s["logit_done"], i * NG + g + 1)
                    dve.tensor_copy(logit[:, bass.ts(g, GB), :], ps[1][0:T, 0:GB * NE].rearrange("p (b e) -> p b e", b=GB)).then_inc(s["logit_out"], 1)

                scale(n, 0, 0, 0)
                with dve.Fori(0, NG // 2 - 1) as it:
                    for par in range(2):
                        logits(par, it * 2 + par, it)
                logits(0, NG - 2, NG // 2 - 1)
                logits(1, NG - 1, NG // 2 - 1, False)
                dve.wait_ge(s["logit_out"], (i + 1) * NG + 1)
                step(dve.reduce_max(top[:, :], logit[:, :, :], AX.X))
                dve.tensor_tensor(gate[:, :, :], logit[:, :, :], by_token(top[:, :]), ALU.subtract).then_inc(s["exp_in"], 1)
                dve.wait_ge(s["exp_done"], i + 1)
                if i:
                    step(dve.reduce_sum(total[:, :], gate[:, :, :], AX.X))
                    step(dve.reciprocal(total[:, :], total[:, :]))
                    step(dve.tensor_tensor(gate[:, :, :], gate[:, :, :], by_token(total[:, :]), ALU.mult))
                if i == 0:
                    rank_two()
                else:
                    first_best()
                step(dve.tensor_tensor(gate[:, :, :], gate[:, :, :], picked[:, :, :], ALU.mult))
                if i == 0:
                    step(dve.reduce_sum(total[:, :], gate[:, :, :], AX.X))
                    step(dve.reciprocal(total[:, :], total[:, :]))
                    step(dve.tensor_tensor(gate[:, :, :], gate[:, :, :], by_token(total[:, :]), ALU.mult))
                else:
                    dve.sem_inc(s["tri_in"], 1)
                    dve.wait_ge(s["tri_done"], 1)
                    flat = lambda v: v.rearrange("p b e -> p (b e)")
                    n_all = NB * NE
                    step(dve.memset(place[:, 0, 0:1, :], 0.0))
                    step(dve.tensor_copy(flat(place[:, 0, :, :])[:, NE:], ps[1][0:T, n_all:2 * n_all - NE]))
                    step_b, cur = 1, 0
                    while step_b < NB:
                        a, b = flat(place[:, cur, :, :]), flat(place[:, 1 - cur, :, :])
                        w = step_b * NE
                        step(dve.tensor_copy(b[:, 0:w], a[:, 0:w]))
                        step(dve.tensor_tensor(b[:, w:], a[:, w:], a[:, 0:n_all - w], ALU.add))
                        step_b, cur = 2 * step_b, 1 - cur
                    step(dve.tensor_tensor(flat(place[:, 1 - cur, :, :]), ps[1][0:T, 0:n_all], flat(place[:, cur, :, :]), ALU.add))
                    step(dve.tensor_scalar(place[:, cur, :, :], place[:, 1 - cur, :, :], CAP + 0.5, None, ALU.is_lt))
                    step(dve.tensor_tensor(gate[:, :, :], gate[:, :, :], place[:, cur, :, :], ALU.mult))

                def guard(g):
                    yg, xb = (a[:, GB * g:GB * g + GB, :].rearrange("p b d -> p (b d)") for a in (y_all, x))
                    for m, (border, op) in enumerate(((None, ALU.not_equal), (FLT_MAX, ALU.is_gt), (-FLT_MAX, ALU.is_lt))):
                        if border is None:
                            step(dve.tensor_tensor(odd[:, m % 2, :], yg, yg, op))
                        else:
                            step(dve.tensor_scalar(odd[:, m % 2, :], yg, border, None, op))
                        step(dve.copy_predicated(yg, odd[:, m % 2, :], fills[:, m, :]))
                    dve.tensor_tensor(xb, xb, yg, ALU.add).then_inc(s["y_added"], 1)

                def group(par, g, behind, guards=()):
                    for b in range(GB):
                        k4 = (i * NG + g) * GB + b
                        r = b % 2
                        eye = lambda v: v.rearrange("p (e d) -> p e d", e=NE)
                        dve.wait_ge(s["down_done"], k4 + 1)
                        dve.tensor_tensor(mixed[:, r, :], ps[4 + r][0:T, :], b2[i][:, :, :].rearrange("p e d -> p (e d)"), ALU.add).then_inc(s["added"], 1)
                        dve.wait_ge(s["added"], k4 + 3)
                        w = gate[:, bass.ds(g * GB + b, 1), :].rearrange("p a e -> p (a e)").unsqueeze(2).broadcast_to([T, NE, D])
                        dve.tensor_tensor(eye(weighed[:, r, :]), eye(mixed[:, r, :]), w, ALU.mult).then_inc(s["weighted"], 1)
                        dve.wait_ge(s["weighted"], k4 + 1)
                        to = y_all[:, bass.ds(g * GB + b, 1), :].rearrange("p a d -> p (a d)") if i else y[:, par, D * b:D * b + D]
                        dve.reduce_sum(to, weighed[:, r, :].rearrange("p (e d) -> p d e", e=NE), AX.X).then_inc(s["summed"], 1)
                        if behind and b == 1:
                            dve.wait_ge(s["y_added"], g)
                            centre(NORM_AT[2] + g - 1, GB * (g - 1), GB)
                        if behind and b == 3:
                            spread(NORM_AT[2] + g - 1, GB * (g - 1), GB)
                        if b < len(guards):
                            guard(guards[b])
                    dve.wait_ge(s["summed"], (i * NG + g) * GB + GB)
                    if i == 0:
                        xb = x[:, bass.ts(g, GB), :]
                        dve.tensor_tensor(xb, xb, y[:, par, :].rearrange("p (b d) -> p b d", b=GB), ALU.add).then_inc(s["y_added"], 1)

                group(0, 0, False)
                group(1, 1, i == 0)
                with dve.Fori(1, NG // 2 - 1) as it:
                    for par in range(2):
                        group(par, it * 2 + par, i == 0)
                group(0, NG - 2, i == 0, range(4) if i else ())
                group(1, NG - 1, i == 0, range(4, NG - 1) if i else ())
                if i:
                    guard(NG - 1)
                if i == 0:
                    dve.wait_ge(s["y_added"], NG)
                    centre(NORM_AT[2] + NG - 1, GB * (NG - 1), GB)
                    spread(NORM_AT[2] + NG - 1, GB * (NG - 1), GB)

            experts(0, 1)
            def shares(par, g, more=True):
                if more:
                    scale(2, 1 - par, g + 1, g + 1)
                for r in range(2):
                    for q in (1, 3):
                        dve.wait_ge(s["xw_done"], g * 8 + r * 4 + q + 1)
                        o = NB * GATE_AT[q]
                        dve.tensor_copy(xw[:, r, :, o:o + NB].rearrange("p t (g b) -> p g b t", b=GB)[:, g],
                                        up_banks[q][:, 0:GT].rearrange("p (b t) -> p b t", b=GB)).then_inc(s["xw_dve"], 1)

            scale(2, 0, 0, 0)
            with dve.Fori(0, NG // 2 - 1) as it:
                for par in range(2):
                    shares(par, it * 2 + par)
            shares(0, NG - 2)
            shares(1, NG - 1, False)

            def cell(r, st, dst):
                dve.wait_ge(s[f"sigmoids{r}"], st + 1)
                dve.tensor_tensor(kept[:, r, :], sig[:, r, NB:2 * NB], cs[:, r, :], ALU.mult)
                dve.wait_ge(s[f"cell_gate{r}"], st + 1)
                dve.tensor_tensor(ig[:, r, :], sig[:, r, 0:NB], tg[:, r, :], ALU.mult).then_inc(s[f"input_part{r}"], 1)
                dve.wait_ge(s[f"input_part{r}"], st + 1)
                dve.tensor_tensor(cs[:, r, :], kept[:, r, :], ig[:, r, :], ALU.add).then_inc(s[f"cell_new{r}"], 1)
                dve.wait_ge(s[f"cell_tanh{r}"], st + 1)
                dve.tensor_tensor(dst, sig[:, r, 2 * NB:3 * NB], cell_t[:, r, :], ALU.mult).then_inc(s[f"state_new{r}"], 1)

            with dve.Fori(0, T // 2) as it:
                for par in range(2):
                    for r in range(2):
                        cell(r, it * 2 + par, hs[:, r, 1 - par, :])
            dve.wait_ge(s["zc_done"], 1)
            dve.memset(hd[:, 0, :], 0.0)
            dve.memset(cs[:, 2, :], 0.0)
            dve.tensor_copy(zc[:, :], ps[4][:, 0:P]).then_inc(s["zc_out"], 1)
            step(dve.tensor_tensor(x[:, :, :], x[:, :, :], bo[:, :].unsqueeze(1).broadcast_to([T, NB, D]), ALU.add))
            with dve.Fori(0, T // 2) as it:
                for par in range(2):
                    st = it * 2 + par
                    cell(2, st, hd[:, bass.ds(st + 1, 1), :].rearrange("p a b -> p (a b)"))
            for b8 in range(QUARTERS):
                xb = x[:, 8 * b8:8 * b8 + 8, :]
                dve.wait_ge(s["dec_done"], b8 + 1)
                dve.tensor_tensor(xb, ps[2 + b8 % 2][0:T, :].rearrange("p (b d) -> p b d", b=8), xb, ALU.add).then_inc(s["dec_out"], 1)
                if b8:
                    spread(NORM_AT[3] + b8 - 1, 8 * (b8 - 1), 8)
                dve.wait_ge(s["dec_out"], b8 + 3)
                centre(NORM_AT[3] + b8, 8 * b8, 8)
            spread(NORM_AT[3] + QUARTERS - 1, 8 * (QUARTERS - 1), 8)
            for m, v in enumerate((0.0, 1e4, -1e4)):
                fill = dve.memset(fills[:, m, :], v)
            step(fill)
            experts(1, 3)


def build(nc, d, out):
    img = nc.dram_tensor("img_tokens", [NB, HH, WW], F32).ap()
    with ExitStack() as sems:
        build_fno(nc, sems, d, img)
        build_tail(nc, sems, d, img, out)


def kernel(**inputs):
    import concourse.bacc as bacc
    from concourse.bass_utils import run_bass_kernel_spmd

    nc = bacc.Bacc("TRN2", target_bir_lowering=False, num_devices=1)
    arrays = {name: np.ascontiguousarray(a) for name, a in inputs.items()}
    arrays.update(fno_constants())
    arrays.update(tail_constants())
    d = {name: nc.dram_tensor(name, a.shape, mybir.dt.from_np(a.dtype), kind="ExternalInput").ap() for name, a in arrays.items()}
    out = nc.dram_tensor("out", [NB, T, D], F32, kind="ExternalOutput").ap()
    build(nc, d, out)
    return run_bass_kernel_spmd(nc, [arrays], core_ids=[0]).results[0]["out"]
```
